# Optimizing a Trainium2 kernel written in Bass

```python
import numpy as np
import jax
import jax.numpy as jnp

def _softmax(x, axis=-1):
    return jax.nn.softmax(x, axis=axis)

def _gelu(x):
    return jax.nn.gelu(x, approximate=True)

def _silu(x):
    return jax.nn.silu(x)

def _sigmoid(x):
    return jax.nn.sigmoid(x)

def _layernorm(x, axis=-1, eps=1e-05):
    m = jnp.mean(x, axis=axis, keepdims=True)
    v = jnp.var(x, axis=axis, keepdims=True)
    return (x - m) / jnp.sqrt(v + eps)

def _scatter_add(tgt, idx, src, axis=0):
    return tgt.at[idx].add(src)

def _segment_sum(src, seg, n):
    return jax.ops.segment_sum(src, seg, n)
kernel_name = 'mk_decoder_preln_d1_seqx_r4_77c778'

def setup_inputs(seed: int=0):
    np.random.seed(seed)
    _w = jnp.asarray

    def _rec_inputs():
        import jax
        import jax.numpy as jnp
        _rk = jax.random.key(seed)
        x = 7.22e-05 + 1 * jax.random.normal(jax.random.fold_in(_rk, 1), (2, 1024, 256), jnp.float32)
        _lenS = 1024 - jax.random.randint(jax.random.fold_in(_rk, 7), (2,), 0, max(1, 1024 // 4) + 1, jnp.int32)
        _lenS2 = 154 - jax.random.randint(jax.random.fold_in(_rk, 8), (2,), 0, max(1, 154 // 4) + 1, jnp.int32)
        _ctx_1024P = jax.random.normal(jax.random.fold_in(_rk, 11), (2, 16, 256), jnp.float32)
        _ctx_1024c = jax.random.dirichlet(jax.random.fold_in(_rk, 511), 0.3 * jnp.ones((16,), jnp.float32), (2, 154))
        _ctx_1024t = jnp.einsum('bsk,bkd->bsd', _ctx_1024c, _ctx_1024P)
        _ctx_1024t = _ctx_1024t * jax.lax.rsqrt(jnp.mean(jnp.square(_ctx_1024t)) + 1e-12) * 0.953939
        ctx_1024 = 4.13588e-05 + 0.999923 * (_ctx_1024t + 0.3 * jax.random.normal(jax.random.fold_in(_rk, 611), (2, 154, 256), jnp.float32))
        return (x, ctx_1024)
    x, ctx_1024 = _rec_inputs()

    def _L0_attn_setup():
        import jax, jax.numpy as jnp
        import numpy as np
        D_MODEL = 256
        key = jax.random.key(seed)
        ks = jax.random.split(key, 7)
        scale = 1.0 / np.sqrt(D_MODEL)
        x = jax.random.normal(ks[0], (4, 1024, D_MODEL), dtype=jnp.float32)
        Wq = jax.random.uniform(ks[1], (D_MODEL, D_MODEL), jnp.float32, -scale, scale)
        bq = jax.random.uniform(ks[2], (D_MODEL,), jnp.float32, -scale, scale)
        Wk = jax.random.uniform(ks[3], (D_MODEL, D_MODEL), jnp.float32, -scale, scale)
        bk = jax.random.uniform(ks[4], (D_MODEL,), jnp.float32, -scale, scale)
        Wv = jax.random.uniform(ks[5], (D_MODEL, D_MODEL), jnp.float32, -scale, scale)
        bv = jax.random.uniform(ks[6], (D_MODEL,), jnp.float32, -scale, scale)
        return {'x': x, 'Wq': Wq, 'bq': bq, 'Wk': Wk, 'bk': bk, 'Wv': Wv, 'bv': bv}
    _L0_attn_all = _L0_attn_setup()
    _L0_attn_in = {k: v for k, v in _L0_attn_all.items() if k in ('Wq', 'bq', 'Wk', 'bk', 'Wv', 'bv')}
    del _L0_attn_all

    def _L0_xattn_setup():
        import jax, jax.numpy as jnp
        import numpy as np
        DIM = 256
        CTX_DIM = 256
        HEADS = 8
        DIM_HEAD = 64
        INNER = HEADS * DIM_HEAD
        EPS = 1e-05

        def _layer_norm(x, gamma, beta):
            mu = jnp.mean(x, axis=-1, keepdims=True)
            var = jnp.mean(jnp.square(x - mu), axis=-1, keepdims=True)
            return (x - mu) * jax.lax.rsqrt(var + EPS) * gamma + beta
        key = jax.random.key(seed)
        ks = jax.random.split(key, 8)
        b, n, m = (4, 512, 512)
        x = jax.random.normal(ks[0], (b, n, DIM), dtype=jnp.float32)
        context = jax.random.normal(ks[1], (b, m, CTX_DIM), dtype=jnp.float32)
        Wq = jax.random.normal(ks[2], (DIM, INNER), dtype=jnp.float32) / np.sqrt(DIM)
        Wkv = jax.random.normal(ks[3], (CTX_DIM, 2 * INNER), dtype=jnp.float32) / np.sqrt(CTX_DIM)
        Wout = jax.random.normal(ks[4], (INNER, DIM), dtype=jnp.float32) / np.sqrt(INNER)
        bout = jnp.zeros((DIM,), dtype=jnp.float32)
        g1 = jnp.ones((DIM,), dtype=jnp.float32)
        b1 = jnp.zeros((DIM,), dtype=jnp.float32)
        g2 = jnp.ones((CTX_DIM,), dtype=jnp.float32)
        b2 = jnp.zeros((CTX_DIM,), dtype=jnp.float32)
        return {'x': x, 'context': context, 'g1': g1, 'b1': b1, 'g2': g2, 'b2': b2, 'Wq': Wq, 'Wkv': Wkv, 'Wout': Wout, 'bout': bout}
    _L0_xattn_all = _L0_xattn_setup()
    _L0_xattn_in = {k: v for k, v in _L0_xattn_all.items() if k in ('g1', 'b1', 'g2', 'b2', 'Wq', 'Wkv', 'Wout', 'bout')}
    del _L0_xattn_all

    def _L0_ffn_setup():
        import jax, jax.numpy as jnp
        import numpy as np
        key = jax.random.key(seed)
        ks = jax.random.split(key, 5)
        B, T, D, E = (4, 512, 256, 8)
        inputs = jax.random.normal(ks[0], (B, T, D), dtype=jnp.float32)
        Wr = jax.random.normal(ks[1], (D, E), dtype=jnp.float32) * 0.02
        br = jnp.zeros((E,), dtype=jnp.float32)
        W1 = jax.random.normal(ks[2], (E, D, D), dtype=jnp.float32) * 0.02
        b1 = jnp.zeros((E, D), dtype=jnp.float32)
        W2 = jax.random.normal(ks[3], (E, D, D), dtype=jnp.float32) * 0.02
        b2 = jnp.zeros((E, D), dtype=jnp.float32)
        return {'inputs': inputs, 'Wr': Wr, 'br': br, 'W1': W1, 'b1': b1, 'W2': W2, 'b2': b2}
    _L0_ffn_all = _L0_ffn_setup()
    _L0_ffn_in = {k: v for k, v in _L0_ffn_all.items() if k in ('Wr', 'br', 'W1', 'b1', 'W2', 'b2')}
    del _L0_ffn_all
    return {'x': x, 'ctx_1024': ctx_1024, 'L0_attn_Wq': _L0_attn_in['Wq'], 'L0_attn_bq': _L0_attn_in['bq'], 'L0_attn_Wk': _L0_attn_in['Wk'], 'L0_attn_bk': _L0_attn_in['bk'], 'L0_attn_Wv': _L0_attn_in['Wv'], 'L0_attn_bv': _L0_attn_in['bv'], 'L0_xattn_g1': _L0_xattn_in['g1'], 'L0_xattn_b1': _L0_xattn_in['b1'], 'L0_xattn_g2': _L0_xattn_in['g2'], 'L0_xattn_b2': _L0_xattn_in['b2'], 'L0_xattn_Wq': _L0_xattn_in['Wq'], 'L0_xattn_Wkv': _L0_xattn_in['Wkv'], 'L0_xattn_Wout': _L0_xattn_in['Wout'], 'L0_xattn_bout': _L0_xattn_in['bout'], 'L0_ffn_Wr': _L0_ffn_in['Wr'], 'L0_ffn_br': _L0_ffn_in['br'], 'L0_ffn_W1': _L0_ffn_in['W1'], 'L0_ffn_b1': _L0_ffn_in['b1'], 'L0_ffn_W2': _L0_ffn_in['W2'], 'L0_ffn_b2': _L0_ffn_in['b2']}

def reference(x, ctx_1024, L0_attn_Wq, L0_attn_bq, L0_attn_Wk, L0_attn_bk, L0_attn_Wv, L0_attn_bv, L0_xattn_g1, L0_xattn_b1, L0_xattn_g2, L0_xattn_b2, L0_xattn_Wq, L0_xattn_Wkv, L0_xattn_Wout, L0_xattn_bout, L0_ffn_Wr, L0_ffn_br, L0_ffn_W1, L0_ffn_b1, L0_ffn_W2, L0_ffn_b2):
    import jax
    import jax.numpy as jnp

    def _L0_attn_ref(x, Wq, bq, Wk, bk, Wv, bv):
        import jax, jax.numpy as jnp
        import numpy as np
        D_MODEL = 256
        Q = jnp.einsum('bsd,de->bse', x, Wq) + bq
        K = jnp.einsum('bsd,de->bse', x, Wk) + bk
        V = jnp.einsum('bsd,de->bse', x, Wv) + bv
        scale = 1.0 / jnp.sqrt(jnp.asarray(x.shape[-1], x.dtype))
        scores = jnp.einsum('bqd,bkd->bqk', Q, K) * scale
        weights = jax.nn.softmax(scores, axis=-1)
        return jnp.einsum('bqk,bkd->bqd', weights, V)

    def _L0_xattn_ref(x, context, g1, b1, g2, b2, Wq, Wkv, Wout, bout):
        import jax, jax.numpy as jnp
        import numpy as np
        DIM = 256
        CTX_DIM = 256
        HEADS = 8
        DIM_HEAD = 64
        INNER = HEADS * DIM_HEAD
        EPS = 1e-05

        def _layer_norm(x, gamma, beta):
            mu = jnp.mean(x, axis=-1, keepdims=True)
            var = jnp.mean(jnp.square(x - mu), axis=-1, keepdims=True)
            return (x - mu) * jax.lax.rsqrt(var + EPS) * gamma + beta
        b, n, _ = x.shape
        m = context.shape[1]
        scale = DIM_HEAD ** (-0.5)
        xn = _layer_norm(x, g1, b1)
        cn = _layer_norm(context, g2, b2)
        q = xn @ Wq
        kv = cn @ Wkv
        k, v = jnp.split(kv, 2, axis=-1)
        q = q.reshape(b, n, HEADS, DIM_HEAD).transpose(0, 2, 1, 3)
        k = k.reshape(b, m, HEADS, DIM_HEAD).transpose(0, 2, 1, 3)
        v = v.reshape(b, m, HEADS, DIM_HEAD).transpose(0, 2, 1, 3)
        sim = jnp.einsum('bhid,bhjd->bhij', q, k) * scale
        attn = jax.nn.softmax(sim, axis=-1)
        out = jnp.einsum('bhij,bhjd->bhid', attn, v)
        out = out.transpose(0, 2, 1, 3).reshape(b, n, INNER)
        return out @ Wout + bout

    def _L0_ffn_ref(inputs, Wr, br, W1, b1, W2, b2):
        import jax, jax.numpy as jnp
        import numpy as np
        B, T, D = inputs.shape
        E = Wr.shape[1]
        x = inputs.reshape(B * T, D)
        N = x.shape[0]
        C = N // E
        logits = x @ Wr + br
        probs = jax.nn.softmax(logits, axis=-1)
        gate = jnp.max(probs, axis=-1, keepdims=True)
        idx = jnp.argmax(probs, axis=-1)
        mask = jax.nn.one_hot(idx, E, dtype=jnp.float32)
        pos = (jnp.cumsum(mask, axis=0) * mask).astype(jnp.int32)
        mask = mask * (pos < C).astype(jnp.float32)
        mask_flat = jnp.sum(mask, axis=-1, keepdims=True)
        gate = gate * mask_flat
        combine = (gate * mask_flat * jax.nn.one_hot(idx, E, dtype=jnp.float32))[..., None] * jax.nn.one_hot(pos, C, dtype=jnp.float32)
        dispatch = combine
        expert_in = jnp.einsum('nd,nec->ecd', x, dispatch)
        h = jax.nn.relu(jnp.einsum('ecd,edf->ecf', expert_in, W1) + b1[:, None, :])
        eo = jnp.einsum('ecf,efd->ecd', h, W2) + b2[:, None, :]
        out = jnp.einsum('ecd,nec->nd', eo, combine)
        return out.reshape(B, T, D)
    x = x + _L0_attn_ref(_layernorm(x, axis=-1), L0_attn_Wq, L0_attn_bq, L0_attn_Wk, L0_attn_bk, L0_attn_Wv, L0_attn_bv)
    x = x + _L0_xattn_ref(_layernorm(x, axis=-1), ctx_1024, L0_xattn_g1, L0_xattn_b1, L0_xattn_g2, L0_xattn_b2, L0_xattn_Wq, L0_xattn_Wkv, L0_xattn_Wout, L0_xattn_bout)
    x = x + _L0_ffn_ref(_layernorm(x, axis=-1), L0_ffn_Wr, L0_ffn_br, L0_ffn_W1, L0_ffn_b1, L0_ffn_W2, L0_ffn_b2)
    return x

_drawn_inputs = setup_inputs


def setup_inputs(seed=0):
    import zlib

    import numpy as np

    out = dict(_drawn_inputs(seed))
    spreads = {'L0_xattn_g1': (1.0, 0.2),
     'L0_xattn_b1': (0.0, 0.61),
     'L0_xattn_g2': (1.0, 0.2),
     'L0_xattn_b2': (0.0, 0.1),
     'L0_xattn_bout': (0.0, 0.1),
     'L0_ffn_br': (0.0, 0.562),
     'L0_ffn_b1': (0.0, 0.8),
     'L0_ffn_b2': (0.0, 0.531)}
    factors = {'L0_attn_Wq': 4.794,
     'L0_attn_bq': 8.0,
     'L0_attn_Wk': 4.695,
     'L0_attn_bk': 8.0,
     'L0_attn_Wv': 2.847,
     'L0_ffn_Wr': 4.062,
     'L0_ffn_W1': 8.0,
     'L0_ffn_W2': 8.0}
    for name, (base, spread) in spreads.items():
        noise = np.random.default_rng([zlib.crc32(name.encode()), seed]).standard_normal(out[name].shape)
        drawn = base * np.exp(spread * noise) if base else spread * noise
        out[name] = jnp.asarray(drawn.astype(out[name].dtype))
    for name, factor in factors.items():
        out[name] = (out[name] * factor).astype(out[name].dtype)
    return out
```

```python
from contextlib import ExitStack

import concourse.bass as bass
from concourse import mybir

ALU = mybir.AluOpType
ACT = mybir.ActivationFunctionType
AX = mybir.AxisListType.X
F32 = mybir.dt.float32
F32R = mybir.dt.float32r
BF16 = mybir.dt.bfloat16
I32 = mybir.dt.int32

P = 128
B, S, D = 2, 1024, 256
M = 154
CT = 77
H, DH = 8, 64
E = 8
KB = D // P
TB = S // P
T = B * TB
N = B * S
CAP = N // E
REM = M - P
HG = 4
RK = HG * REM
NBLK = H + H // HG
HM = H * M
REC = D + 4
EPS = 1e-5
FAR = 4096.0
SIMG = [(0, 3), (3, 6), (6, 8)]
OUT_SPLIT = 7


def at(off, n):
    return slice(off, off + n) if isinstance(off, int) else bass.ds(off, n)


def batch_of(t):
    return t // TB if isinstance(t, int) else (t >> 3).with_bounds(min_val=0, max_val=B - 1)


def known_zero(t):
    return isinstance(t, int) and t == 0


def build(nc, x, ctx_in, Wq, bq, Wk, bk, Wv, bv, g1, b1, g2, b2, WqX, Wkv, Wout, bout, Wr, br, W1, fb1, W2, fb2, out):
    X = x.rearrange("b (t p) d -> p (b t) d", p=P)
    OUT = out.rearrange("b s d -> (b s) d")
    slots = nc.dram_tensor("slots", [N, REC], F32)

    def row(v):
        return v.rearrange("(a n) -> a n", a=1)

    with ExitStack() as whole:
        def sb(ctx, name, shape, dt=F32):
            return ctx.enter_context(nc.sbuf_tensor(name, shape, dt))

        def sem(ctx, name):
            return ctx.enter_context(nc.semaphore(name))

        ps = whole.enter_context(nc.psum_tensor("ps", [P, 8, 512], F32))
        ident = sb(whole, "ident", [P, P])
        tri = sb(whole, "tri", [P, P], BF16)
        ones = sb(whole, "ones", [P, P], BF16)
        mhalf = sb(whole, "mhalf", [P, 4])
        small = sb(whole, "small", [P, 256])

        attn = ExitStack()
        KWh = sb(attn, "KWh", [P, KB * B * HM], F32R)
        KWl = sb(attn, "KWl", [P, KB * B * HM], F32R)
        VWh = sb(attn, "VWh", [P, B * NBLK * D], F32R)
        VWl = sb(attn, "VWl", [P, B * NBLK * D], F32R)
        xr = sb(attn, "xr", [P, T * D])
        xr3 = xr[:].rearrange("p (t c) -> p t c", c=D)
        tokens = sb(attn, "tokens", [P, T], I32)
        x_in = [sem(attn, f"x_in{c}") for c in range(4)]
        slots_set = sem(attn, "slots_set")

        with ExitStack() as ph:
            ctx_n = sb(ph, "ctx_n", [CT, 4, D])
            g2b = sb(ph, "g2b", [CT, D])
            b2b = sb(ph, "b2b", [CT, D])
            wqx = sb(ph, "wqx", [P, KB, H * DH])
            wkv = sb(ph, "wkv", [P, KB, 2 * H * DH])
            wkvh = sb(ph, "wkvh", [P, KB, 2 * H * DH], F32R)
            wkvl = sb(ph, "wkvl", [P, KB, 2 * H * DH], F32R)
            wo = sb(ph, "wo", [P, 4, D])
            woh = sb(ph, "woh", [P, 4, D], F32R)
            wol = sb(ph, "wol", [P, 4, D], F32R)
            cnTh = sb(ph, "cnTh", [P, KB, B * M], F32R)
            cnTl = sb(ph, "cnTl", [P, KB, B * M], F32R)
            wqTh = sb(ph, "wqxTh", [P, 4, D], F32R)
            wqTl = sb(ph, "wqxTl", [P, 4, D], F32R)
            kvz = [[sb(ph, f"{n}z{s}", [P, H, B * M], F32R) for s in "hl"] for n in "kv"]
            vrem = [sb(ph, f"vrem{s}", [P, B, 4, RK], F32R) for s in "hl"]
            cst = sb(ph, "cst", [CT, 4, 6])
            cmv = sb(ph, "cmv", [CT, 4, 2])
            crs = sb(ph, "crs", [CT, 4])
            init = sb(ph, "init", [P, REC])

            ctx_ld = sem(ph, "ctx_ld")
            wqx_ld = sem(ph, "wqx_ld")
            wkv_ld = sem(ph, "wkv_ld")
            wo_ld = sem(ph, "wo_ld")
            gb_ld = sem(ph, "gb_ld")
            const_done = sem(ph, "const_done")
            ident_set = sem(ph, "ident_set")
            ident_done = sem(ph, "ident_done")
            init_done = sem(ph, "init_done")
            cstat = sem(ph, "cstat")
            cvar = sem(ph, "cvar")
            crstd = sem(ph, "crstd")
            cz = sem(ph, "cz")
            czg = sem(ph, "czg")
            cn_done = sem(ph, "cn_done")
            zeros_done = sem(ph, "zeros_done")
            split_hi = sem(ph, "split_hi")
            split_done = sem(ph, "split_done")
            unit_mm = sem(ph, "unit_mm")
            unit_hi = sem(ph, "unit_hi")
            unit_lo = sem(ph, "unit_lo")
            rem_done = sem(ph, "rem_done")

            units = [("cn", k) for k in range(KB)] + [("wq", j) for j in range(2)]
            units += [("kv", j) for j in range(8)]
            units += [("kw", b, k, g) for b in range(B) for k in range(KB) for g in range(3)]
            units += [("vw", b, j) for b in range(B) for j in range(4)] + [("vr", b) for b in range(B)]
            number = {u: i for i, u in enumerate(units)}

            def pieces(u):
                bank = ps[:, number[u] % 8, :]
                kind = u[0]
                if kind == "cn":
                    return [(bank[:, 0:B * M], cnTh[:, u[1], :], cnTl[:, u[1], :])]
                if kind == "wq":
                    j = 2 * u[1]
                    v = bank.rearrange("p (j d) -> p j d", j=2)
                    return [(v, wqTh[:, j:j + 2, :], wqTl[:, j:j + 2, :])]
                if kind == "kv":
                    hi, lo = kvz[u[1] // 4]
                    j = u[1] % 4
                    return [(bank[r:r + 64, 0:B * M], hi[r:r + 64, 2 * j + r // 64, :], lo[r:r + 64, 2 * j + r // 64, :])
                            for r in (0, 64)]
                if kind == "kw":
                    _, b, k, g = u
                    n = (SIMG[g][1] - SIMG[g][0]) * M
                    o = (k * B + b) * HM + SIMG[g][0] * M
                    return [(bank[:, 0:n], KWh[:, o:o + n], KWl[:, o:o + n])]
                if kind == "vw":
                    o = (u[1] * NBLK + 2 * u[2]) * D
                    return [(bank, VWh[:, o:o + 2 * D], VWl[:, o:o + 2 * D])]
                o = (u[1] * NBLK + H) * D
                return [(bank[0:RK, :], VWh[0:RK, o:o + 2 * D], VWl[0:RK, o:o + 2 * D])]

            block = ph.enter_context(nc.Block())

            @block.sync
            def _(sp):
                sp.dma_start(ctx_n[:], ctx_in.rearrange("b (a p) d -> p (b a) d", p=CT)).then_inc(ctx_ld, 16)
                sp.dma_start(g2b[:], row(g2).broadcast_to([CT, D])).then_inc(gb_ld, 16)
                sp.dma_start(b2b[:], row(b2).broadcast_to([CT, D])).then_inc(gb_ld, 16)
                sp.dma_start(wkv[:], Wkv.rearrange("(k p) e -> p k e", p=P)).then_inc(wkv_ld, 16)
                for c in range(4):
                    sp.dma_start(xr3[:, 4 * c:4 * c + 4, :], X[:, 4 * c:4 * c + 4, :]).then_inc(x_in[c], 16)
                sp.wait_ge(init_done, 2)
                for k in range(N // P):
                    sp.dma_start(slots[k * P:(k + 1) * P, :], init[:]).then_inc(slots_set, 16)

            @block.gpsimd
            def _(pool):
                g = nc.gpsimd
                g.memset(mhalf[:], -0.5).then_inc(const_done, 1)
                g.memset(ident[:], 0.0).then_inc(ident_set, 1)
                g.memset(ones[:], 1.0).then_inc(ident_set, 1)
                pool.wait_ge(ident_set, 2)
                g.affine_select(out=ident[:], in_=ident[:], compare_op=ALU.not_equal, fill=1.0, base=0,
                                pattern=[[-1, P]], channel_multiplier=1).then_inc(ident_done, 1)
                g.affine_select(out=tri[:], in_=ones[:], compare_op=ALU.is_ge, fill=0.0, base=0,
                                pattern=[[1, P]], channel_multiplier=-1).then_inc(ident_done, 1)
                for z in (kvz[0][0], kvz[0][1], kvz[1][0], kvz[1][1], vrem[0], vrem[1]):
                    g.memset(z[:].bitcast(F32), 0.0).then_inc(zeros_done, 1)
                pool.wait_ge(cvar, 1)
                g.tensor_tensor(crs[:], cmv[:, :, 1], mhalf[0:CT, 0:4], ALU.pow).then_inc(crstd, 1)
                pool.wait_ge(cz, 4)
                pool.wait_ge(gb_ld, 32)
                g.tensor_tensor(ctx_n[:], ctx_n[:], g2b[:].rearrange("p (a d) -> p a d", a=1).broadcast_to([CT, 4, D]),
                                ALU.mult).then_inc(czg, 1)
                pool.wait_ge(czg, 1)
                g.tensor_tensor(ctx_n[:], ctx_n[:], b2b[:].rearrange("p (a d) -> p a d", a=1).broadcast_to([CT, 4, D]),
                                ALU.add).then_inc(cn_done, 1)
                g.memset(init[:], 0.0).then_inc(init_done, 1)
                pool.wait_ge(init_done, 1)
                g.iota(init[:, REC - 1:REC].bitcast(I32), pattern=[[0, 1]], base=int(FAR), channel_multiplier=0).then_inc(init_done, 1)
                g.iota(tokens[:], pattern=[[P, T]], base=0, channel_multiplier=1).then_inc(init_done, 1)
                pool.wait_ge(unit_lo, number[("kv", 7)] + 1)
                pool.wait_ge(init_done, 3)
                for n, h in enumerate((0, 2, 4, 6, 1, 3, 5, 7)):
                    if n == H // 2:
                        pool.wait_ge(rem_done, H)
                    r, c = 64 * (h % 2), REM * (h % HG)
                    for s in range(2):
                        src = kvz[1][s][r:r + 64, h, :].rearrange("p (b m) -> p b m", b=B)[:, :, P:M]
                        g.tensor_copy(vrem[s][r:r + 64, :, h // 2, c:c + REM], src.bitcast(F32)).then_inc(rem_done, 1)

            @block.scalar
            def _(act):
                act.dma_start(wqx[:], WqX.rearrange("(k p) e -> p k e", p=P)).then_inc(wqx_ld, 16)
                act.dma_start(wo[:], Wout.rearrange("(j p) d -> p j d", p=P)).then_inc(wo_ld, 16)
                act.wait_ge(wkv_ld, 16)
                nc.scalar.activation(wkvh[:], wkv[:], ACT.Copy).then_inc(split_hi, 1)
                act.wait_ge(wo_ld, 16)
                nc.scalar.activation(woh[:], wo[:], ACT.Copy).then_inc(split_hi, 1)
                for i, u in enumerate(units):
                    act.wait_ge(unit_mm, i + 1)
                    if u == ("kv", 0):
                        act.wait_ge(zeros_done, 6)
                    for src, hi, lo in pieces(u):
                        last = nc.scalar.activation(hi, src, ACT.Copy)
                    last.then_inc(unit_hi, 1)

            @block.vector
            def _(dve):
                v = nc.vector
                dve.wait_ge(ctx_ld, 16)
                for a in range(4):
                    v.bn_stats(cst[:, a, :], ctx_n[:, a, :]).then_inc(cstat, 1)
                for a in range(4):
                    dve.wait_ge(cstat, 4 + a)
                    v.bn_aggr(cmv[:, a, :], cst[:, a, :]).then_inc(cstat, 1)
                dve.wait_ge(cstat, 8)
                v.tensor_scalar(cmv[:, :, 1], cmv[:, :, 1], EPS, None, ALU.add).then_inc(cvar, 1)
                dve.wait_ge(crstd, 1)
                for a in range(4):
                    v.tensor_scalar(ctx_n[:, a, :], ctx_n[:, a, :], cmv[:, a, 0:1], crs[:, a:a + 1],
                                    ALU.subtract, ALU.mult).then_inc(cz, 1)
                dve.wait_ge(split_hi, 1)
                v.tensor_tensor(wkvl[:], wkv[:], wkvh[:].bitcast(F32), ALU.subtract).then_inc(split_done, 1)
                for i, u in enumerate(units):
                    if i == 4:
                        dve.wait_ge(split_hi, 2)
                        v.tensor_tensor(wol[:], wo[:], woh[:].bitcast(F32), ALU.subtract).then_inc(split_done, 1)
                    dve.wait_ge(unit_hi, i + 1)
                    for src, hi, lo in pieces(u):
                        last = v.tensor_tensor(lo, src, hi.bitcast(F32), ALU.subtract)
                    last.then_inc(unit_lo, 1)

            @block.tensor
            def _(pe):
                def bank_of(u):
                    i = number[u]
                    if i >= 8:
                        pe.wait_ge(unit_lo, i - 7)
                    return ps[:, i % 8, :]

                def product(o, a, b, first=True, last=True, skip=False):
                    nc.tensor.matmul(o, a[0], b[0], start=first, stop=False, skip_group_check=skip)
                    nc.tensor.matmul(o, a[0], b[1], start=False, stop=False, skip_group_check=skip)
                    return nc.tensor.matmul(o, a[1], b[0], start=False, stop=last, skip_group_check=skip)

                pe.wait_ge(ident_done, 2)
                pe.wait_ge(wqx_ld, 16)
                pe.wait_ge(cn_done, 1)
                for k in range(KB):
                    bank = bank_of(("cn", k))
                    for a in range(4):
                        last = nc.tensor.transpose(bank[:, a * CT:(a + 1) * CT], ctx_n[:, a, k * P:(k + 1) * P], ident[0:CT, 0:CT])
                    last.then_inc(unit_mm, 1)
                for j in range(4):
                    bank = bank_of(("wq", j // 2))
                    for k in range(KB):
                        o = (j % 2) * D + k * P
                        last = nc.tensor.transpose(bank[:, o:o + P], wqx[:, k, j * P:(j + 1) * P], ident[:])
                    if j % 2:
                        last.then_inc(unit_mm, 1)
                pe.wait_ge(unit_lo, number[("cn", KB - 1)] + 1)
                pe.wait_ge(split_done, 1)
                for j in range(8):
                    bank = bank_of(("kv", j))
                    for k in range(KB):
                        w = slice(j * P, (j + 1) * P)
                        last = product(bank[:, 0:B * M], (wkvh[:, k, w], wkvl[:, k, w]), (cnTh[:, k, :], cnTl[:, k, :]), k == 0, k == KB - 1)
                    last.then_inc(unit_mm, 1)
                pe.wait_ge(unit_lo, number[("kv", 3)] + 1)
                for b in range(B):
                    for k in range(KB):
                        for g in range(3):
                            bank = bank_of(("kw", b, k, g))
                            for h in range(*SIMG[g]):
                                c = slice((h - SIMG[g][0]) * M, (h - SIMG[g][0] + 1) * M)
                                d = slice(k * P, (k + 1) * P)
                                m = slice(b * M, (b + 1) * M)
                                last = product(bank[:, c], (wqTh[:, h // 2, d], wqTl[:, h // 2, d]),
                                               (kvz[0][0][:, h, m], kvz[0][1][:, h, m]))
                            last.then_inc(unit_mm, 1)
                pe.wait_ge(split_done, 2)
                pe.wait_ge(rem_done, 2 * H)
                for b in range(B):
                    for j in range(4):
                        bank = bank_of(("vw", b, j))
                        for h in (2 * j, 2 * j + 1):
                            m = slice(b * M, b * M + P)
                            last = product(bank[:, (h % 2) * D:(h % 2 + 1) * D], (kvz[1][0][:, h, m], kvz[1][1][:, h, m]),
                                           (woh[:, j, :], wol[:, j, :]))
                        last.then_inc(unit_mm, 1)
                for b in range(B):
                    bank = bank_of(("vr", b))
                    for g in range(H // HG):
                        for j in (2 * g, 2 * g + 1):
                            last = product(bank[0:RK, g * D:(g + 1) * D], (vrem[0][:, b, j, :], vrem[1][:, b, j, :]),
                                           (woh[:, j, :], wol[:, j, :]), j % 2 == 0, j % 2 == 1)
                    last.then_inc(unit_mm, 1)

        xhTh = sb(attn, "xhTh", [P, KB * N], F32R)
        xhTl = sb(attn, "xhTl", [P, KB * N], F32R)
        Vh = sb(attn, "Vh", [P, T * D], F32R)
        Vl = sb(attn, "Vl", [P, T * D], F32R)
        Ah = sb(attn, "Ah", [P, KB, D], F32R)
        Al = sb(attn, "Al", [P, KB, D], F32R)
        cb = sb(attn, "cb", [P, KB])
        u = sb(attn, "u", [P, T])

        with ExitStack() as ph:
            wqk = [sb(ph, f"w{n}", [P, KB, D]) for n in "qk"]
            wv = sb(ph, "wv", [P, KB, D])
            wTh = [sb(ph, f"w{n}Th", [P, KB, D + 2], F32R) for n in "qk"]
            wTl = [sb(ph, f"w{n}Tl", [P, KB, D + 2], F32R) for n in "qk"]
            bcol = [sb(ph, f"b{n}c", [P, KB]) for n in "qk"]
            wvh = sb(ph, "wvh", [P, KB, D + 2], F32R)
            wvl = sb(ph, "wvl", [P, KB, D + 2], F32R)
            bvb = sb(ph, "bvb", [P, D + 1])
            xst = sb(ph, "xst", [P, T, 6])
            xmv = sb(ph, "xmv", [P, T, 2])
            xrs = sb(ph, "xrs", [P, T])
            xh = sb(ph, "xh", [P, 2, D])
            sth = sb(ph, "sth", [P, 2, D], F32R)
            stl = sb(ph, "stl", [P, 2, D], F32R)
            vf = sb(ph, "vf", [P, 2, D + 1])

            w_ld = [sem(ph, f"w{n}_ld") for n in "qkv"]
            bias_ld = sem(ph, "bias_ld")
            bv_ld = sem(ph, "bv_ld")
            wt_mm = sem(ph, "wt_mm")
            wt_hi = sem(ph, "wt_hi")
            wt_lo = sem(ph, "wt_lo")
            wvs_hi = sem(ph, "wvs_hi")
            wvs_lo = sem(ph, "wvs_lo")
            a_mm = sem(ph, "a_mm")
            a_hi = sem(ph, "a_hi")
            a_lo = sem(ph, "a_lo")
            stat = sem(ph, "stat")
            var_ok = sem(ph, "var_ok")
            rstd = sem(ph, "rstd")
            xh_done = sem(ph, "xh_done")
            xt_mm = sem(ph, "xt_mm")
            st_hi = sem(ph, "st_hi")
            st_lo = sem(ph, "st_lo")
            kept = sem(ph, "kept")
            v_mm = sem(ph, "v_mm")
            vf_done = sem(ph, "vf_done")
            v_hi = sem(ph, "v_hi")
            v_lo = sem(ph, "v_lo")
            block = ph.enter_context(nc.Block())

            @block.sync
            def _(sp):
                for n, w in enumerate((Wq, Wk)):
                    sp.dma_start(wqk[n][:], w.rearrange("(k p) e -> p k e", p=P)).then_inc(w_ld[n], 16)
                for n, bias in enumerate((bq, bk)):
                    sp.dma_start(bcol[n][:], bias.rearrange("(k p) -> p k", p=P), allow_slow_non_contiguous=True).then_inc(bias_ld, 16)
                sp.dma_start(wv[:], Wv.rearrange("(k p) e -> p k e", p=P)).then_inc(w_ld[2], 16)
                sp.dma_start(bvb[:, 0:D], row(bv).broadcast_to([P, D])).then_inc(bv_ld, 16)

            @block.tensor
            def _(pe):
                def product(o, a, b, first=True, last=True):
                    nc.tensor.matmul(o, a[0], b[0], start=first, stop=False)
                    nc.tensor.matmul(o, a[0], b[1], start=False, stop=False)
                    return nc.tensor.matmul(o, a[1], b[0], start=False, stop=last)

                for n in range(2):
                    pe.wait_ge(w_ld[n], 16)
                    for e in range(KB):
                        for k in range(KB):
                            last = nc.tensor.transpose(ps[:, 4 + n, e * D + k * P:e * D + (k + 1) * P],
                                                       wqk[n][:, k, e * P:(e + 1) * P], ident[:])
                    last.then_inc(wt_mm, 1)
                pe.wait_ge(wt_lo, 4)
                for k in range(KB):
                    d = slice(k * P, (k + 1) * P)
                    for e in range(KB):
                        last = product(ps[:, 6 + k, 0:D + 2], (wTh[0][:, e, d], wTl[0][:, e, d]), (wTh[1][:, e, :], wTl[1][:, e, :]),
                                       e == 0, e == KB - 1)
                    last.then_inc(a_mm, 1)
                for k in range(KB):
                    d = slice(k * P, (k + 1) * P)
                    for e in range(KB):
                        bqh, bql = wTh[0][:, e, D:D + 2], wTl[0][:, e, D:D + 2]
                        product(ps[:, 4, 2 * k:2 * k + 2], (wTh[1][:, e, d], wTl[1][:, e, d]), (bqh, bql), e == 0, e == KB - 1)
                for e in range(KB):
                    bqs = [w[0][:, e, D:D + 1].broadcast_to([P, P]) for w in (wTh, wTl)]
                    last = product(ps[:, 4, 4:6], bqs, (wTh[1][:, e, D:D + 2], wTl[1][:, e, D:D + 2]), e == 0, e == KB - 1)
                last.then_inc(a_mm, 1)
                pe.wait_ge(a_lo, 3)
                with pe.Fori(0, T // 2) as i:
                    for j in range(2):
                        pe.wait_ge(xh_done, 2 * i + j + 1)
                        for k in range(KB):
                            last = nc.tensor.transpose(ps[:, j, k * P:(k + 1) * P], xh[:, j, k * P:(k + 1) * P], ident[:])
                        last.then_inc(xt_mm, 1)
                    for j in range(2):
                        pe.wait_ge(st_lo, 2 * i + j + 1)
                        for k in range(KB):
                            d = slice(k * P, (k + 1) * P)
                            last = product(ps[:, 2 + j, 0:D + 2], (sth[:, j, d], stl[:, j, d]), (wvh[:, k, :], wvl[:, k, :]),
                                           k == 0, k == KB - 1)
                        last.then_inc(v_mm, 1)

            @block.scalar
            def _(act):
                a = nc.scalar.activation
                act.wait_ge(bias_ld, 32)
                for n in range(2):
                    for r in range(2):
                        last = a(wTh[n][:, :, D + r], bcol[n][:], ACT.Copy)
                    last.then_inc(wt_hi, 1)
                for n in range(2):
                    act.wait_ge(wt_mm, n + 1)
                    a(wTh[n][:, :, 0:D], ps[:, 4 + n, :].rearrange("p (e d) -> p e d", e=KB), ACT.Copy).then_inc(wt_hi, 1)
                act.wait_ge(w_ld[2], 16)
                a(wvh[:, :, 0:D], wv[:], ACT.Copy).then_inc(wvs_hi, 1)
                for k in range(KB):
                    act.wait_ge(a_mm, k + 1)
                    a(Ah[:, k, :], ps[:, 6 + k, 0:D], ACT.Copy)
                    a(wvh[:, k, D:D + 2], ps[:, 6 + k, D:D + 2], ACT.Copy).then_inc(a_hi, 1)
                with act.Fori(0, T // 2) as i:
                    for j in range(2):
                        act.wait_ge(xt_mm, 2 * i + j + 1)
                        act.wait_ge(kept, 2 * (2 * i + j) + 2)
                        a(sth[:, j, :], ps[:, j, 0:D], ACT.Copy).then_inc(st_hi, 1)
                    for j in range(2):
                        act.wait_ge(vf_done, 2 * i + j + 1)
                        a(Vh[:, at((2 * i + j) * D, D)], vf[:, j, 0:D], ACT.Copy).then_inc(v_hi, 1)

            @block.vector
            def _(dve):
                v = nc.vector
                for n in range(2):
                    dve.wait_ge(wt_hi, 2)
                    for r in range(2):
                        last = v.tensor_tensor(wTl[n][:, :, D + r], bcol[n][:], wTh[n][:, :, D + r].bitcast(F32), ALU.subtract)
                    last.then_inc(wt_lo, 1)
                for c in range(4):
                    dve.wait_ge(x_in[c], 16)
                    for t in range(4 * c, 4 * c + 4):
                        v.bn_stats(xst[:, t, :], xr3[:, t, :]).then_inc(stat, 1)
                    for t in range(4 * c, 4 * c + 4):
                        dve.wait_ge(stat, 4 * c + t + 1)
                        v.bn_aggr(xmv[:, t, :], xst[:, t, :]).then_inc(stat, 1)
                    dve.wait_ge(stat, 8 * c + 8)
                    v.tensor_scalar(xmv[:, 4 * c:4 * c + 4, 1], xmv[:, 4 * c:4 * c + 4, 1], EPS, None, ALU.add).then_inc(var_ok, 1)
                for n in range(2):
                    dve.wait_ge(wt_hi, 3 + n)
                    v.tensor_tensor(wTl[n][:, :, 0:D], ps[:, 4 + n, :].rearrange("p (e d) -> p e d", e=KB),
                                    wTh[n][:, :, 0:D].bitcast(F32), ALU.subtract).then_inc(wt_lo, 1)
                dve.wait_ge(wvs_hi, 1)
                v.tensor_tensor(wvl[:, :, 0:D], wv[:], wvh[:, :, 0:D].bitcast(F32), ALU.subtract).then_inc(wvs_lo, 1)
                for k in range(KB):
                    dve.wait_ge(a_hi, k + 1)
                    v.tensor_tensor(Al[:, k, :], ps[:, 6 + k, 0:D], Ah[:, k, :].bitcast(F32), ALU.subtract)
                    v.tensor_tensor(wvl[:, k, D:D + 2], ps[:, 6 + k, D:D + 2], wvh[:, k, D:D + 2].bitcast(F32), ALU.subtract).then_inc(a_lo, 1)
                dve.wait_ge(a_mm, 3)
                dve.wait_ge(bv_ld, 16)
                v.tensor_copy(cb[:], ps[:, 4, 0:4].rearrange("p (k r) -> p k r", r=2)[:, :, 0])
                v.tensor_copy(bvb[:, D:D + 1], ps[:, 4, 4:5]).then_inc(a_lo, 1)
                dve.wait_ge(rstd, 4)
                dve.wait_ge(a_lo, 3)
                with dve.Fori(0, T // 2) as i:
                    for j in range(2):
                        t = 2 * i + j
                        v.tensor_scalar(xh[:, j, :], xr[:, at(t * D, D)], xmv[:].rearrange("p t c -> p (t c)")[:, at(2 * t, 1)],
                                        xrs[:, at(t, 1)], ALU.subtract, ALU.mult).then_inc(xh_done, 1)
                    for j in range(2):
                        t = 2 * i + j
                        dve.wait_ge(st_hi, t + 1)
                        v.tensor_tensor(stl[:, j, :], ps[:, j, 0:D], sth[:, j, :].bitcast(F32), ALU.subtract).then_inc(st_lo, 1)
                    for j in range(2):
                        t = 2 * i + j
                        dve.wait_ge(v_mm, t + 1)
                        v.tensor_tensor(vf[:, j, :], ps[:, 2 + j, 0:D + 1], bvb[:], ALU.add).then_inc(vf_done, 1)
                    for j in range(2):
                        t = 2 * i + j
                        dve.wait_ge(v_hi, t + 1)
                        v.tensor_tensor(Vl[:, at(t * D, D)], vf[:, j, 0:D], Vh[:, at(t * D, D)].bitcast(F32), ALU.subtract)
                        v.tensor_copy(u[:, at(t, 1)], vf[:, j, D:D + 1]).then_inc(v_lo, 1)

            @block.gpsimd
            def _(pool):
                g = nc.gpsimd
                for c in range(4):
                    pool.wait_ge(var_ok, c + 1)
                    g.tensor_tensor(xrs[:, 4 * c:4 * c + 4], xmv[:, 4 * c:4 * c + 4, 1], mhalf[:], ALU.pow).then_inc(rstd, 1)
                for c in range(4):
                    g.memset(small[:, c:c + 1], 0.0).then_inc(kept, 1)
                with pool.Fori(0, T // 2) as i:
                    for j in range(2):
                        t = 2 * i + j
                        pool.wait_ge(st_lo, t + 1)
                        for st, big in ((sth, xhTh), (stl, xhTl)):
                            g.tensor_copy(big[:].rearrange("p (k n) -> p k n", k=KB)[:, :, at(t * P, P)],
                                          st[:, j, :].rearrange("p (k n) -> p k n", k=KB).bitcast(F32)).then_inc(kept, 1)

        PSC = D ** -0.5
        P2SC = DH ** -0.5
        with ExitStack() as ph:
            GTh = sb(ph, "GTh", [P, KB, P], F32R)
            GTl = sb(ph, "GTl", [P, KB, P], F32R)
            Pr = sb(ph, "Pr", [P, S])
            PTh = sb(ph, "PTh", [P, S], F32R)
            PTl = sb(ph, "PTl", [P, S], F32R)
            P2 = sb(ph, "P2", [P, HM])
            P2r = sb(ph, "P2r", [P, H, REM])
            P2Th = sb(ph, "P2Th", [P, NBLK * P], F32R)
            P2Tl = sb(ph, "P2Tl", [P, NBLK * P], F32R)
            x1s = sb(ph, "x1s", [P, D])
            rec = sb(ph, "rec", [P, REC])
            zn = sb(ph, "zn", [P, D])
            xnTh = sb(ph, "xnTh", [P, D], F32R)
            xnTl = sb(ph, "xnTl", [P, D], F32R)
            z3 = sb(ph, "z3", [P, D])
            z3T = sb(ph, "z3T", [P, D])
            g1b = sb(ph, "g1b", [P, D])
            b1b = sb(ph, "b1b", [P, D])
            boutb = sb(ph, "boutb", [P, D])
            wr = sb(ph, "wr", [P, KB, E])
            brb = sb(ph, "brb", [P, E])
            desc = sb(ph, "desc", [P, E])
            base = sb(ph, "base", [P, E])
            sm = sb(ph, "sm", [P, 160])
            racc = sb(ph, "racc", [P, E], BF16)
            oh = sb(ph, "oh", [P, E], BF16)
            idx = sb(ph, "idx", [P, 1], I32)
            st1, mv1, r1, v1 = sm[:, 0:6], sm[:, 6:8], sm[:, 8:9], sm[:, 9:10]
            mx, sh, nb, ssum, rs = (sm[:, c:c + 1] for c in range(10, 15))
            mx2, nb2, ss2, rs2 = sm[:, 16:24], sm[:, 24:32], sm[:, 32:40], sm[:, 40:48]
            st3, r3, v3 = sm[:, 48:54], sm[:, 54:55], sm[:, 55:56]
            lg, e8, w8 = sm[:, 56:64], sm[:, 64:72], sm[:, 72:80]
            mx3, nmx3, se, wm, slot_at = (sm[:, c:c + 1] for c in range(80, 85))
            far, pb, q8 = sm[:, 88:96], sm[:, 96:104], sm[:, 104:112]

            names = ("par_ld const_c g_mm g_hi g_lo s_mm s_max s_sh s_nb p_done rs_done tp_mm tp_hi tp_lo pv_mm "
                     "x1_done st1_done mv1_done v1_done r1_done z_done zg_done zn_done xb_done zt_mm xn_hi xn_lo "
                     "sim_mm max2 nb2_done exp2 rs2_done p2_done t2_mm t2_hi t2_lo out_mm x2_done st3_done mv3_done "
                     "v3_done r3_done z3_done zt3_mm zt3_sb lg_mm lg_done mx3_done nmx3_done e8_done w8_done wm_done "
                     "oh_done gate_done rg_done cnt_mm far_done pb_done q1_done q2_done slot_done idx_done racc_done "
                     "x2_out scattered idx_read token_set").split()
            Q = {n: sem(ph, n) for n in names}

            block = ph.enter_context(nc.Block())
            BIG = ps[:].rearrange("p b n -> p (b n)")

            def bank(i):
                return ps[:, i, :]

            LOOP = (5, T - 1)
            LAST = T + 4

            def slots_of(eng, slot):
                for s in range(LOOP[0]):
                    slot(s)
                with eng.Fori(*LOOP) as s:
                    slot(s)
                for s in range(LOOP[1], LAST):
                    slot(s)

            def live(t):
                return not isinstance(t, int) or 0 <= t < T

            @block.sync
            def _(sp):
                sp.dma_start(g1b[:], row(g1).broadcast_to([P, D])).then_inc(Q["par_ld"], 16)
                sp.dma_start(b1b[:], row(b1).broadcast_to([P, D])).then_inc(Q["par_ld"], 16)
                sp.dma_start(boutb[:], row(bout).broadcast_to([P, D])).then_inc(Q["par_ld"], 16)
                sp.dma_start(wr[:], Wr.rearrange("(k p) e -> p k e", p=P)).then_inc(Q["par_ld"], 16)
                sp.dma_start(brb[:], row(br).broadcast_to([P, E])).then_inc(Q["par_ld"], 16)
                with sp.Fori(0, T) as t:
                    sp.wait_ge(Q["x2_done"], t + 1)
                    sp.dma_start(OUT[at(t * P, P), :], rec[:, 0:D]).then_inc(Q["x2_out"], 16)
                sp.wait_ge(Q["x2_out"], 16 * T)

            @block.tensor
            def _(pe):
                def mm(o, a, b, first=False, last=False):
                    return nc.tensor.matmul(o, a, b, start=first, stop=last)

                def product(o, a, b, first=True, last=True):
                    mm(o, a[0], b[0], first)
                    mm(o, a[0], b[1])
                    return mm(o, a[1], b[0], False, last)

                def project(t):
                    if not isinstance(t, int) or t >= 2:
                        pe.wait_ge(Q["tp_lo"], 2 * (t - 1))
                    for k in range(KB):
                        for d in range(KB):
                            c = slice(k * P, (k + 1) * P)
                            o = at(d * N + t * P, P)
                            last = product(bank(4)[:, c], (Ah[:, d, c], Al[:, d, c]), (xhTh[:, o], xhTl[:, o]), d == 0, d == KB - 1)
                    last.then_inc(Q["g_mm"], 1)

                def p_turn(t):
                    pe.wait_ge(Q["p_done"], t + 1)
                    if isinstance(t, int) and t + 1 >= T:
                        pe.wait_ge(Q["g_lo"], T)
                    else:
                        pe.wait_ge(Q["g_lo"], t + 2)
                    if not isinstance(t, int) or t >= 3:
                        pe.wait_ge(Q["x2_done"], t - 2)
                    for n in range(TB):
                        last = nc.tensor.transpose(BIG[:, (3 * 4 + n) * P:(3 * 4 + n + 1) * P], Pr[:, n * P:(n + 1) * P], ident[:])
                        if n % 4 == 3:
                            last.then_inc(Q["tp_mm"], 1)

                def p2_turn(t):
                    pe.wait_ge(Q["p2_done"], t + 1)
                    pe.wait_ge(Q["x1_done"], T if isinstance(t, int) and t + 2 > T else t + 2)
                    pe.wait_ge(Q["p_done"], T if isinstance(t, int) and t + 3 > T else t + 3)
                    for n in range(NBLK):
                        if n < H:
                            src, rows = P2[:, n * M:n * M + P], P
                        else:
                            h = (n - H) * HG
                            src = P2r[:, h:h + HG, :].rearrange("p h m -> p (h m)")
                            rows = RK
                        last = nc.tensor.transpose(BIG[0:rows, n * P:(n + 1) * P], src, ident[:])
                        if n % 4 == 3 or n == NBLK - 1:
                            last.then_inc(Q["t2_mm"], 1)

                def sim(t):
                    pe.wait_ge(Q["xn_lo"], t + 1)
                    if not isinstance(t, int) or t >= 3:
                        pe.wait_ge(Q["q2_done"], t - 2)
                    b = batch_of(t)
                    for g in range(3):
                        n = (SIMG[g][1] - SIMG[g][0]) * M
                        if not known_zero(t):
                            pe.wait_ge(Q["exp2"], 3 * (t - 1) + g + 1)
                        for k in range(KB):
                            d = slice(k * P, (k + 1) * P)
                            o = at((k * B + b) * HM + SIMG[g][0] * M, n)
                            last = product(bank(5 + g)[:, 0:n], (xnTh[:, d], xnTl[:, d]), (KWh[:, o], KWl[:, o]), k == 0, k == KB - 1)
                        last.then_inc(Q["sim_mm"], 1)

                def z3_turn(t):
                    pe.wait_ge(Q["z3_done"], t + 1)
                    pe.wait_ge(Q["tp_lo"], 2 * T if isinstance(t, int) and t + 4 > T else 2 * (t + 4))
                    for k in range(KB):
                        d = slice(k * P, (k + 1) * P)
                        last = nc.tensor.transpose(bank(4)[:, d], z3[:, d], ident[:])
                    last.then_inc(Q["zt3_mm"], 1)

                def pv(t):
                    b = batch_of(t)
                    for n in range(TB):
                        if n % 4 == 0:
                            pe.wait_ge(Q["tp_lo"], 2 * t + n // 4 + 1)
                        if n == 0 and (not isinstance(t, int) or t >= 2):
                            pe.wait_ge(Q["t2_lo"], 3 * (t - 1) - 2)
                        c = slice(n * P, (n + 1) * P)
                        o = at((b * TB + n) * D, D)
                        last = product(bank(0)[:, 0:D], (PTh[:, c], PTl[:, c]), (Vh[:, o], Vl[:, o]), n == 0, n == TB - 1)
                    last.then_inc(Q["pv_mm"], 1)

                def logits(t):
                    pe.wait_ge(Q["zt3_sb"], t + 1)
                    for k in range(KB):
                        last = mm(bank(4)[:, 0:E], z3T[:, k * P:(k + 1) * P], wr[:, k, :], k == 0, k == KB - 1)
                    last.then_inc(Q["lg_mm"], 1)

                def scores(t):
                    pe.wait_ge(Q["g_lo"], t + 1)
                    if not isinstance(t, int) or t >= 3:
                        pe.wait_ge(Q["t2_lo"], 3 * (t - 2) if not isinstance(t, int) or t - 2 <= T else 3 * T)
                    b = batch_of(t)
                    for h in range(2):
                        for k in range(KB):
                            o = at(k * N + b * S + h * 512, 512)
                            last = product(bank(1 + h), (GTh[:, k, :], GTl[:, k, :]), (xhTh[:, o], xhTl[:, o]), k == 0, k == KB - 1)
                    last.then_inc(Q["s_mm"], 1)

                def count(t, sim_tile):
                    pe.wait_ge(Q["oh_done"], t + 1)
                    pe.wait_ge(Q["exp2"], 3 * T if isinstance(sim_tile, int) and sim_tile >= T else 3 * sim_tile + 3)
                    mm(bank(7)[:, 0:E], tri[:], oh[:], True, False)
                    mm(bank(7)[:, 0:E], ones[:], racc[:], False, True).then_inc(Q["cnt_mm"], 1)

                def outp(t, blocks):
                    b = batch_of(t)
                    for n in blocks:
                        if n == 0:
                            pe.wait_ge(Q["tp_lo"], 2 * T if isinstance(t, int) and t + 3 > T else 2 * (t + 3))
                        if n % 4 == 0:
                            pe.wait_ge(Q["t2_lo"], 3 * t + n // 4 + 1)
                        rows = P if n < H else RK
                        c = slice(n * P, (n + 1) * P)
                        o = at((b * NBLK + n) * D, D)
                        last = product(bank(3)[:, 0:D], (P2Th[0:rows, c], P2Tl[0:rows, c]), (VWh[0:rows, o], VWl[0:rows, o]),
                                       n == 0, n == NBLK - 1)
                    if NBLK - 1 in blocks:
                        last.then_inc(Q["out_mm"], 1)

                def z_turn(t):
                    pe.wait_ge(Q["zn_done"], t + 1)
                    if not known_zero(t):
                        pe.wait_ge(Q["exp2"], 3 * (t - 1) + 1)
                    for k in range(KB):
                        d = slice(k * P, (k + 1) * P)
                        last = nc.tensor.transpose(bank(5)[:, d], zn[:, d], ident[:])
                    last.then_inc(Q["zt_mm"], 1)

                def slot(s):
                    if live(s - 1):
                        p_turn(s - 1)
                    if live(s - 3):
                        p2_turn(s - 3)
                    if live(s - 2):
                        sim(s - 2)
                    if live(s - 4):
                        z3_turn(s - 4)
                    if live(s - 1):
                        pv(s - 1)
                    if live(s - 4):
                        logits(s - 4)
                    if live(s):
                        scores(s)
                    if live(s - 4):
                        count(s - 4, s - 2)
                    if live(s - 3):
                        outp(s - 3, range(OUT_SPLIT))
                    if live(s - 1):
                        z_turn(s - 1)
                    if live(s - 3):
                        outp(s - 3, range(OUT_SPLIT, NBLK))
                    if live(s + 1):
                        if live(s - 4):
                            pe.wait_ge(Q["lg_done"], s - 3)
                        project(s + 1)

                pe.wait_ge(Q["par_ld"], 80)
                pe.wait_ge(Q["const_c"], 4)
                project(0)
                slots_of(pe, slot)

            @block.scalar
            def _(act):
                a = nc.scalar.activation

                def p_hi(t):
                    for h in range(2):
                        act.wait_ge(Q["tp_mm"], 2 * t + h + 1)
                        a(PTh[:, h * 512:(h + 1) * 512], bank(3 + h), ACT.Copy).then_inc(Q["tp_hi"], 1)

                def p2_hi(t):
                    for g in range(3):
                        act.wait_ge(Q["t2_mm"], 3 * t + g + 1)
                        rows, n = (P, 512) if g < 2 else (RK, 256)
                        a(P2Th[0:rows, g * 512:g * 512 + n], bank(g)[0:rows, 0:n], ACT.Copy).then_inc(Q["t2_hi"], 1)

                def exp2(t):
                    for g in range(3):
                        act.wait_ge(Q["nb2_done"], 3 * t + g + 1)
                        for h in range(*SIMG[g]):
                            o = (h - SIMG[g][0]) * M
                            last = a(P2[:, h * M:(h + 1) * M], bank(5 + g)[:, o:o + M], ACT.Exp, bias=nb2[:, h:h + 1], scale=P2SC,
                                     accum_out=ss2[:, h:h + 1])
                        last.then_inc(Q["exp2"], 1)

                def gate(t):
                    act.wait_ge(Q["nmx3_done"], t + 1)
                    if not known_zero(t):
                        act.wait_ge(Q["gate_done"], t)
                    a(e8, lg, ACT.Exp, bias=nmx3, scale=1.0, accum_out=se).then_inc(Q["e8_done"], 1)

                def exps(t):
                    act.wait_ge(Q["s_nb"], t + 1)
                    if not known_zero(t):
                        act.wait_ge(Q["tp_mm"], 2 * t)
                        act.wait_ge(Q["rs_done"], t)
                    a(Pr[:], BIG[:, 512:1536], ACT.Exp, bias=nb, scale=PSC, accum_out=ssum).then_inc(Q["p_done"], 1)

                def xn_hi(t):
                    act.wait_ge(Q["zt_mm"], t + 1)
                    a(xnTh[:], bank(5)[:, 0:D], ACT.Copy).then_inc(Q["xn_hi"], 1)

                def g_hi(t):
                    act.wait_ge(Q["g_mm"], t + 1)
                    for k in range(KB):
                        last = a(GTh[:, k, :], bank(4)[:, k * P:(k + 1) * P], ACT.Identity, bias=cb[:, k:k + 1], scale=1.0)
                    last.then_inc(Q["g_hi"], 1)

                def slot(s):
                    if live(s - 1):
                        p_hi(s - 1)
                    if live(s - 3):
                        p2_hi(s - 3)
                    if live(s - 2):
                        exp2(s - 2)
                    if live(s - 4):
                        gate(s - 4)
                    if live(s):
                        exps(s)
                    if live(s - 1):
                        xn_hi(s - 1)
                    if live(s + 1):
                        g_hi(s + 1)

                g_hi(0)
                slots_of(act, slot)

            @block.gpsimd
            def _(pool):
                g = nc.gpsimd
                g.memset(racc[:], 0.0).then_inc(Q["const_c"], 1)
                g.iota(q8, pattern=[[1, E]], base=0, channel_multiplier=0, allow_small_or_imprecise_dtypes=True).then_inc(Q["const_c"], 1)
                pool.wait_ge(Q["const_c"], 2)
                g.tensor_scalar(desc[:], q8, -1.0, float(E), ALU.mult, ALU.add).then_inc(Q["const_c"], 1)
                g.tensor_scalar(base[:], q8, float(CAP), 0.0, ALU.mult, ALU.add).then_inc(Q["const_c"], 1)
                last_row = pool.to_reg(N - 1)
                pool.wait_ge(slots_set, 16 * (N // P))
                pool.wait_ge(Q["par_ld"], 80)

                def affine(t):
                    pool.wait_ge(Q["v1_done"], t + 1)
                    g.tensor_tensor(r1, v1, mhalf[:, 0:1], ALU.pow).then_inc(Q["r1_done"], 1)
                    pool.wait_ge(Q["z_done"], t + 1)
                    g.tensor_tensor(zn[:], zn[:], g1b[:], ALU.mult).then_inc(Q["zg_done"], 1)
                    pool.wait_ge(Q["zg_done"], t + 1)
                    g.tensor_tensor(zn[:], zn[:], b1b[:], ALU.add).then_inc(Q["zn_done"], 1)
                    g.tensor_tensor(xr[:, at(t * D, D)], x1s[:], boutb[:], ALU.add).then_inc(Q["xb_done"], 1)

                def norm(t):
                    pool.wait_ge(Q["rs2_done"], t + 1)
                    p3 = P2[:].rearrange("p (h m) -> p h m", h=H)
                    r3d = rs2.rearrange("p (h a) -> p h a", a=1)
                    g.tensor_tensor(p3[:, :, 0:P], p3[:, :, 0:P], r3d.broadcast_to([P, H, P]), ALU.mult)
                    g.tensor_tensor(P2r[:], p3[:, :, P:M], r3d.broadcast_to([P, H, REM]), ALU.mult).then_inc(Q["p2_done"], 1)

                def scatter(t):
                    pool.wait_ge(Q["idx_done"], t + 1)
                    pool.wait_ge(Q["token_set"], t + 1)
                    pool.nop(nofuse=True)
                    g.indirect_dma_start(out=slots[:, :], out_offset=bass.IndirectOffsetOnAxis(ap=idx[:], axis=0),
                                         in_=rec[:], in_offset=None, bounds_check=last_row,
                                         oob_is_err=False, engine_sem=Q["idx_read"]).then_inc(Q["scattered"], 16)

                def rstd3(t):
                    pool.wait_ge(Q["v3_done"], t + 1)
                    g.tensor_tensor(r3, v3, mhalf[:, 0:1], ALU.pow).then_inc(Q["r3_done"], 1)

                def slot(s):
                    if live(s - 1):
                        affine(s - 1)
                    if live(s - 2):
                        norm(s - 2)
                    if live(s - 4):
                        scatter(s - 4)
                    if live(s - 3):
                        rstd3(s - 3)

                slots_of(pool, slot)
                pool.wait_ge(Q["scattered"], 16 * T)

            @block.vector
            def _(dve):
                v = nc.vector

                def p_lo(t):
                    for h in range(2):
                        dve.wait_ge(Q["tp_hi"], 2 * t + h + 1)
                        c = slice(h * 512, (h + 1) * 512)
                        v.tensor_tensor(PTl[:, c], bank(3 + h), PTh[:, c].bitcast(F32), ALU.subtract).then_inc(Q["tp_lo"], 1)
                    v.reciprocal(rs, ssum).then_inc(Q["rs_done"], 1)

                def p2_lo(t):
                    for g in range(3):
                        dve.wait_ge(Q["t2_hi"], 3 * t + g + 1)
                        rows, n = (P, 512) if g < 2 else (RK, 256)
                        c = slice(g * 512, g * 512 + n)
                        v.tensor_tensor(P2Tl[0:rows, c], bank(g)[0:rows, 0:n], P2Th[0:rows, c].bitcast(F32), ALU.subtract).then_inc(Q["t2_lo"], 1)

                def max2(t):
                    for g in range(3):
                        dve.wait_ge(Q["sim_mm"], 3 * t + g + 1)
                        h0, h1 = SIMG[g]
                        v.tensor_reduce(mx2[:, h0:h1], bank(5 + g)[:, 0:(h1 - h0) * M].rearrange("p (h m) -> p h m", m=M), AX,
                                        ALU.max).then_inc(Q["max2"], 1)
                        dve.wait_ge(Q["max2"], 3 * t + g + 1)
                        v.tensor_scalar(nb2[:, h0:h1], mx2[:, h0:h1], -P2SC, None, ALU.mult).then_inc(Q["nb2_done"], 1)

                def z3t_copy(t):
                    dve.wait_ge(Q["zt3_mm"], t + 1)
                    v.tensor_copy(z3T[:], bank(4)[:, 0:D]).then_inc(Q["zt3_sb"], 1)

                def x1(t):
                    dve.wait_ge(Q["pv_mm"], t + 1)
                    dve.wait_ge(Q["rs_done"], t + 1)
                    if not known_zero(t):
                        dve.wait_ge(Q["xb_done"], t)
                    v.scalar_tensor_tensor(out=x1s[:], in0=bank(0)[:, 0:D], scalar=rs, in1=xr[:, at(t * D, D)], op0=ALU.mult,
                                           op1=ALU.add).then_inc(Q["x1_done"], 1)
                    dve.wait_ge(Q["x1_done"], t + 1)
                    dve.nop(nofuse=True)
                    v.bn_stats(st1, x1s[:]).then_inc(Q["st1_done"], 1)
                    dve.wait_ge(Q["st1_done"], t + 1)
                    dve.nop(nofuse=True)
                    v.bn_aggr(mv1, st1).then_inc(Q["mv1_done"], 1)
                    dve.wait_ge(Q["mv1_done"], t + 1)
                    v.tensor_scalar(v1, mv1[:, 1:2], 1.0 + EPS, EPS * EPS, ALU.mult, ALU.add).then_inc(Q["v1_done"], 1)

                def route1(t):
                    dve.wait_ge(Q["lg_mm"], t + 1)
                    v.tensor_tensor(lg, bank(4)[:, 0:E], brb[:], ALU.add).then_inc(Q["lg_done"], 1)
                    dve.wait_ge(Q["lg_done"], t + 1)
                    v.tensor_reduce(mx3, lg, AX, ALU.max).then_inc(Q["mx3_done"], 1)
                    dve.wait_ge(Q["mx3_done"], t + 1)
                    v.tensor_scalar(nmx3, mx3, -1.0, None, ALU.mult).then_inc(Q["nmx3_done"], 1)

                def zee(t):
                    dve.wait_ge(Q["r1_done"], t + 1)
                    if not known_zero(t):
                        dve.wait_ge(Q["zt_mm"], t)
                    v.tensor_scalar(zn[:], x1s[:], mv1[:, 0:1], r1, ALU.subtract, ALU.mult).then_inc(Q["z_done"], 1)

                def recip2(t):
                    dve.wait_ge(Q["exp2"], 3 * t + 3)
                    v.reciprocal(rs2, ss2).then_inc(Q["rs2_done"], 1)

                def route2(t):
                    dve.wait_ge(Q["e8_done"], t + 1)
                    v.scalar_tensor_tensor(out=w8, in0=e8, scalar=1.0, in1=desc[:], op0=ALU.is_ge, op1=ALU.mult).then_inc(Q["w8_done"], 1)
                    gt = rec[:, D + 2:D + 3]
                    v.reciprocal(gt, se).then_inc(Q["gate_done"], 1)
                    dve.wait_ge(Q["w8_done"], t + 1)
                    v.tensor_reduce(wm, w8, AX, ALU.max).then_inc(Q["wm_done"], 1)
                    dve.wait_ge(Q["wm_done"], t + 1)
                    v.tensor_scalar(oh[:], w8, wm, None, ALU.is_equal).then_inc(Q["oh_done"], 1)
                    dve.wait_ge(Q["gate_done"], t + 1)
                    v.tensor_tensor(rec[:, D + 1:D + 2], r3, gt, ALU.mult).then_inc(Q["rg_done"], 1)

                def smax(t):
                    dve.wait_ge(Q["s_mm"], t + 1)
                    v.tensor_reduce(mx, BIG[:, 512:1536], AX, ALU.max).then_inc(Q["s_max"], 1)
                    dve.wait_ge(Q["s_max"], t + 1)
                    ut = u[:, at(t, 1)]
                    v.tensor_tensor(sh, mx, ut, ALU.add).then_inc(Q["s_sh"], 1)
                    dve.wait_ge(Q["s_sh"], t + 1)
                    v.tensor_scalar(nb, sh, ut, -PSC, ALU.subtract, ALU.mult).then_inc(Q["s_nb"], 1)

                def place(t):
                    dve.wait_ge(Q["cnt_mm"], t + 1)
                    cnt = bank(7)[:, 0:E]
                    v.tensor_scalar(far, cnt, float(CAP), FAR, ALU.is_ge, ALU.mult).then_inc(Q["far_done"], 1)
                    v.tensor_tensor(pb, cnt, base[:], ALU.add).then_inc(Q["pb_done"], 1)
                    v.tensor_tensor(racc[:], racc[:], oh[:], ALU.add).then_inc(Q["racc_done"], 1)
                    dve.wait_ge(Q["far_done"], t + 1)
                    dve.wait_ge(Q["pb_done"], t + 1)
                    v.tensor_tensor(far, far, pb, ALU.add).then_inc(Q["q1_done"], 1)
                    dve.wait_ge(Q["q1_done"], t + 1)
                    v.tensor_tensor(far, far, oh[:], ALU.mult).then_inc(Q["q2_done"], 1)
                    dve.wait_ge(Q["q2_done"], t + 1)
                    v.tensor_reduce(slot_at, far, AX, ALU.add).then_inc(Q["slot_done"], 1)
                    dve.wait_ge(Q["slot_done"], t + 1)
                    dve.wait_ge(Q["rg_done"], t + 1)
                    dve.wait_ge(Q["racc_done"], t + 1)
                    if not known_zero(t):
                        dve.wait_ge(Q["idx_read"], t)
                    v.tensor_copy(idx[:], slot_at).then_inc(Q["idx_done"], 1)

                def xn_lo(t):
                    dve.wait_ge(Q["xn_hi"], t + 1)
                    v.tensor_tensor(xnTl[:], bank(5)[:, 0:D], xnTh[:].bitcast(F32), ALU.subtract).then_inc(Q["xn_lo"], 1)

                def x2(t):
                    dve.wait_ge(Q["out_mm"], t + 1)
                    dve.wait_ge(Q["xb_done"], t + 1)
                    if not known_zero(t):
                        dve.wait_ge(Q["scattered"], 16 * t)
                        dve.wait_ge(Q["x2_out"], 16 * t)
                    v.tensor_tensor(rec[:, 0:D], bank(3)[:, 0:D], xr[:, at(t * D, D)], ALU.add).then_inc(Q["x2_done"], 1)
                    v.tensor_copy(rec[:, REC - 1:REC].bitcast(I32), tokens[:, at(t, 1)]).then_inc(Q["token_set"], 1)
                    dve.wait_ge(Q["x2_done"], t + 1)
                    dve.nop(nofuse=True)
                    v.bn_stats(st3, rec[:, 0:D]).then_inc(Q["st3_done"], 1)
                    dve.wait_ge(Q["st3_done"], t + 1)
                    dve.nop(nofuse=True)
                    v.bn_aggr(rec[:, D:D + 2], st3).then_inc(Q["mv3_done"], 1)
                    dve.wait_ge(Q["mv3_done"], t + 1)
                    v.tensor_scalar(v3, rec[:, D + 1:D + 2], EPS, None, ALU.add).then_inc(Q["v3_done"], 1)

                def g_lo(t):
                    dve.wait_ge(Q["g_hi"], t + 1)
                    for k in range(KB):
                        last = v.scalar_tensor_tensor(out=GTl[:, k, :], in0=bank(4)[:, k * P:(k + 1) * P], scalar=cb[:, k:k + 1],
                                                      in1=GTh[:, k, :].bitcast(F32), op0=ALU.add, op1=ALU.subtract)
                    last.then_inc(Q["g_lo"], 1)

                def zee3(t):
                    dve.wait_ge(Q["r3_done"], t + 1)
                    v.tensor_scalar(z3[:], rec[:, 0:D], rec[:, D:D + 1], r3, ALU.subtract, ALU.mult).then_inc(Q["z3_done"], 1)

                def slot(s):
                    if live(s - 1):
                        p_lo(s - 1)
                    if live(s - 3):
                        p2_lo(s - 3)
                    if live(s - 2):
                        max2(s - 2)
                    if live(s - 4):
                        z3t_copy(s - 4)
                    if live(s - 1):
                        x1(s - 1)
                    if live(s - 4):
                        route1(s - 4)
                    if live(s - 1):
                        zee(s - 1)
                    if live(s - 2):
                        recip2(s - 2)
                    if live(s - 4):
                        route2(s - 4)
                    if live(s):
                        smax(s)
                    if live(s - 4):
                        place(s - 4)
                    if live(s - 1):
                        xn_lo(s - 1)
                    if live(s - 3):
                        x2(s - 3)
                    if live(s + 1):
                        g_lo(s + 1)
                    if live(s - 3):
                        zee3(s - 3)

                dve.wait_ge(Q["par_ld"], 80)
                g_lo(0)
                slots_of(dve, slot)

        attn.close()

        with ExitStack() as ph:
            w_raw = [sb(ph, f"wraw{n}", [P, E * KB * D]) for n in (1, 2)]
            w_h = [[sb(ph, f"w{n}h{j}", [P, KB * D], F32R) for j in range(2)] for n in (1, 2)]
            w_l = [[sb(ph, f"w{n}l{j}", [P, KB * D], F32R) for j in range(2)] for n in (1, 2)]
            b1c = sb(ph, "b1c", [P, E * KB])
            b2r = sb(ph, "b2r", [P, E * D])
            rec = sb(ph, "recs", [P, E * 2 * REC])
            xg = [sb(ph, f"xg{j}", [P, 2, D]) for j in range(2)]
            dTh = [sb(ph, f"dTh{j}", [P, KB, CAP], F32R) for j in range(2)]
            dTl = [sb(ph, f"dTl{j}", [P, KB, CAP], F32R) for j in range(2)]
            hf = [sb(ph, f"hf{j}", [P, KB, CAP]) for j in range(2)]
            hTh = [sb(ph, f"hTh{j}", [P, KB, CAP], F32R) for j in range(2)]
            hTl = [sb(ph, f"hTl{j}", [P, KB, CAP], F32R) for j in range(2)]
            tok = [sb(ph, f"tok{j}", [P, 2], I32) for j in range(2)]
            res = [sb(ph, f"res{j}", [P, 2, D]) for j in range(2)]
            raw_ld = [sem(ph, f"raw_ld{n}") for n in range(4)]
            b_ld = sem(ph, "b_ld")
            token_out = [sem(ph, f"token_out{j}") for j in range(2)]
            rec_ld = [sem(ph, f"rec_ld{e}") for e in range(E)]
            names = "xg_done xt_mm2 dt_hi dt_lo w_hi w_lo h_mm hf_done ht_hi ht_lo o_mm t_done res_done tok_read tok_done".split()
            R = {n: sem(ph, "e_" + n) for n in names}
            block = ph.enter_context(nc.Block())

            def run(eng, slot):
                for s in range(4):
                    slot(s, s % 2)
                with eng.Fori(2, E // 2) as i:
                    for j in range(2):
                        slot(2 * i + j, j)
                for s in range(E, E + 2):
                    slot(s, s % 2)

            def here(e):
                return not isinstance(e, int) or 0 <= e < E

            def later(e, n):
                return not isinstance(e, int) or e >= n

            @block.sync
            def _(sp):
                for q in range(2):
                    for n, w in enumerate((W1, W2)):
                        o, k = (0, 1) if q == 0 else (1, E - 1)
                        sp.dma_start(w_raw[n][:, o * KB * D:(o + k) * KB * D],
                                     w[o:o + k].rearrange("e (k p) f -> p e k f", p=P)).then_inc(raw_ld[2 * q + n], 16)
                        if q == 0:
                            sp.dma_start(rec[:, n * REC:(n + 1) * REC], slots[n * P:(n + 1) * P, :]).then_inc(rec_ld[0], 16)

            @block.tensor
            def _(pe):
                def product(o, a, b, first, last):
                    nc.tensor.matmul(o, a[0], b[0], start=first, stop=False)
                    nc.tensor.matmul(o, a[0], b[1], start=False, stop=False)
                    return nc.tensor.matmul(o, a[1], b[0], start=False, stop=last)

                def second(e, j):
                    pe.wait_ge(R["ht_lo"], e + 1)
                    pe.wait_ge(R["w_lo"], 2 * e + 2)
                    if later(e, 2):
                        pe.wait_ge(R["t_done"], 2 * e - 2)
                    for i in range(2):
                        for f in range(KB):
                            c = slice(i * P, (i + 1) * P)
                            w = slice(f * D, (f + 1) * D)
                            last = product(ps[:, 4 + j, i * D:(i + 1) * D], (hTh[j][:, f, c], hTl[j][:, f, c]),
                                           (w_h[1][j][:, w], w_l[1][j][:, w]), f == 0, f == KB - 1)
                    last.then_inc(R["o_mm"], 1)

                def first(e, j):
                    pe.wait_ge(R["dt_lo"], e + 1)
                    pe.wait_ge(R["w_lo"], 2 * e + 1)
                    if later(e, 2):
                        pe.wait_ge(R["hf_done"], e - 1)
                    for f in range(KB):
                        for k in range(KB):
                            c = slice(k * D + f * P, k * D + (f + 1) * P)
                            last = product(ps[:, 2 + j, f * CAP:(f + 1) * CAP], (w_h[0][j][:, c], w_l[0][j][:, c]),
                                           (dTh[j][:, k, :], dTl[j][:, k, :]), k == 0, k == KB - 1)
                    last.then_inc(R["h_mm"], 1)

                def turn(e, j):
                    pe.wait_ge(R["xg_done"], 2 * e + 2)
                    if later(e, 2):
                        pe.wait_ge(R["dt_lo"], e - 1)
                    for k in range(KB):
                        for i in range(2):
                            o = k * CAP + i * P
                            last = nc.tensor.transpose(ps[:, j, o:o + P], xg[j][:, i, k * P:(k + 1) * P], ident[:])
                    last.then_inc(R["xt_mm2"], 1)

                def slot(s, j):
                    if here(s - 2):
                        second(s - 2, j)
                    if here(s - 1):
                        first(s - 1, 1 - j)
                    if here(s):
                        turn(s, j)

                run(pe, slot)

            @block.scalar
            def _(act):
                a = nc.scalar.activation
                act.dma_start(b1c[:].rearrange("p (e k) -> p e k", e=E), fb1.rearrange("e (k p) -> p e k", p=P), allow_slow_non_contiguous=True).then_inc(b_ld, 16)
                act.dma_start(b2r[:], fb2.rearrange("(a e) d -> a (e d)", a=1).broadcast_to([P, E * D])).then_inc(b_ld, 16)
                for e in range(1, E):
                    for n in range(2):
                        act.dma_start(rec[:, (2 * e + n) * REC:(2 * e + n + 1) * REC],
                                      slots[(2 * e + n) * P:(2 * e + n + 1) * P, :]).then_inc(rec_ld[e], 16)
                act.wait_ge(b_ld, 32)

                def slot(s, j):
                    if here(s):
                        for n in range(2):
                            if isinstance(s, int) and s == 0:
                                act.wait_ge(raw_ld[n], 16)
                            if isinstance(s, int) and s == 1:
                                act.wait_ge(raw_ld[2 + n], 16)
                            if later(s, 2):
                                act.wait_ge(R["h_mm"] if n == 0 else R["o_mm"], s - 1)
                            a(w_h[n][j][:], w_raw[n][:, at(s * KB * D, KB * D)], ACT.Copy).then_inc(R["w_hi"], 1)
                            if n == 0:
                                act.wait_ge(R["xt_mm2"], s + 1)
                                a(dTh[j][:], ps[:, j, :].rearrange("p (k c) -> p k c", k=KB), ACT.Copy).then_inc(R["dt_hi"], 1)
                    if here(s - 1):
                        e, q = s - 1, 1 - j
                        act.wait_ge(R["h_mm"], e + 1)
                        for f in range(KB):
                            last = a(hf[q][:, f, :], ps[:, 2 + q, f * CAP:(f + 1) * CAP], ACT.Relu, bias=b1c[:, at(e * KB + f, 1)], scale=1.0)
                        last.then_inc(R["hf_done"], 1)
                        act.wait_ge(R["hf_done"], e + 1)
                        a(hTh[q][:], hf[q][:], ACT.Copy).then_inc(R["ht_hi"], 1)

                run(act, slot)

            @block.vector
            def _(dve):
                v = nc.vector
                dve.wait_ge(b_ld, 32)
                for e in range(E):
                    dve.wait_ge(rec_ld[e], 32)

                def slot(s, j):
                    if here(s):
                        if later(s, 2):
                            dve.wait_ge(R["xt_mm2"], s - 1)
                        for i in range(2):
                            o = (2 * s + i) * REC
                            v.tensor_scalar(xg[j][:, i, :], rec[:, at(o, D)], rec[:, at(o + D, 1)], rec[:, at(o + D + 1, 1)],
                                            ALU.subtract, ALU.mult).then_inc(R["xg_done"], 1)
                        dve.wait_ge(R["dt_hi"], s + 1)
                        v.tensor_tensor(dTl[j][:], ps[:, j, :].rearrange("p (k c) -> p k c", k=KB), dTh[j][:].bitcast(F32),
                                        ALU.subtract).then_inc(R["dt_lo"], 1)
                    if here(s - 1):
                        e, q = s - 1, 1 - j
                        dve.wait_ge(R["ht_hi"], e + 1)
                        v.tensor_tensor(hTl[q][:], hf[q][:], hTh[q][:].bitcast(F32), ALU.subtract).then_inc(R["ht_lo"], 1)
                    if here(s - 2):
                        e = s - 2
                        dve.wait_ge(R["o_mm"], e + 1)
                        if later(e, 2):
                            dve.wait_ge(R["tok_read"], 2 * e - 2)
                            dve.wait_ge(token_out[j], 32 * (e >> 1))
                        for i in range(2):
                            v.tensor_copy(tok[j][:, i:i + 1], rec[:].bitcast(I32)[:, at((2 * e + i) * REC + D + 3, 1)]).then_inc(R["tok_done"], 1)
                            r = res[j][:, i, :]
                            v.tensor_tensor(r, ps[:, 4 + j, i * D:(i + 1) * D], b2r[:, at(e * D, D)], ALU.add).then_inc(R["t_done"], 1)
                            dve.wait_ge(R["t_done"], 2 * e + i + 1)
                            o = (2 * e + i) * REC
                            v.scalar_tensor_tensor(out=r, in0=r, scalar=rec[:, at(o + D + 2, 1)], in1=rec[:, at(o, D)],
                                                   op0=ALU.mult, op1=ALU.add).then_inc(R["res_done"], 1)

                run(dve, slot)

            @block.gpsimd
            def _(pool):
                g = nc.gpsimd
                last_row = pool.to_reg(N - 1)
                for e in range(E):
                    pool.wait_ge(rec_ld[e], 32)

                def slot(s, j):
                    if here(s):
                        for n in range(2):
                            pool.wait_ge(R["w_hi"], 2 * s + n + 1)
                            g.tensor_tensor(w_l[n][j][:], w_raw[n][:, at(s * KB * D, KB * D)], w_h[n][j][:].bitcast(F32),
                                            ALU.subtract).then_inc(R["w_lo"], 1)
                    if here(s - 2):
                        e = s - 2
                        for i in range(2):
                            pool.wait_ge(R["res_done"], 2 * e + i + 1)
                            pool.wait_ge(R["tok_done"], 2 * e + i + 1)
                            pool.nop(nofuse=True)
                            g.indirect_dma_start(out=OUT, out_offset=bass.IndirectOffsetOnAxis(ap=tok[j][:, i:i + 1], axis=0),
                                                 in_=res[j][:, i, :], in_offset=None, bounds_check=last_row,
                                                 oob_is_err=False, engine_sem=R["tok_read"]).then_inc(token_out[j], 16)

                run(pool, slot)
                for j in range(2):
                    pool.wait_ge(token_out[j], 16 * E)


_INS = ["x", "ctx_1024", "L0_attn_Wq", "L0_attn_bq", "L0_attn_Wk", "L0_attn_bk", "L0_attn_Wv", "L0_attn_bv", "L0_xattn_g1",
        "L0_xattn_b1", "L0_xattn_g2", "L0_xattn_b2", "L0_xattn_Wq", "L0_xattn_Wkv", "L0_xattn_Wout", "L0_xattn_bout",
        "L0_ffn_Wr", "L0_ffn_br", "L0_ffn_W1", "L0_ffn_b1", "L0_ffn_W2", "L0_ffn_b2"]


def kernel(**inputs):
    import numpy as np
    import concourse.bacc as bacc
    from concourse.bass_utils import run_bass_kernel_spmd as run

    nc = bacc.Bacc("TRN2", target_bir_lowering=False, num_devices=1)
    arrays, args = {}, []
    for name in _INS:
        a = np.ascontiguousarray(inputs[name])
        arrays[f"in_{name}"] = a
        args.append(nc.dram_tensor(f"in_{name}", a.shape, mybir.dt.from_np(a.dtype), kind="ExternalInput").ap())
    args.append(nc.dram_tensor("out_rows", (B, S, D), F32, kind="ExternalOutput").ap())
    build(nc, *args)
    r = run(nc, [arrays], core_ids=[0])
    return r.results[0]["out_rows"]
```

```python
from contextlib import ExitStack

import concourse.bass as bass
from concourse import mybir

ALU = mybir.AluOpType
ACT = mybir.ActivationFunctionType
AX = mybir.AxisListType.X
F32 = mybir.dt.float32
F32R = mybir.dt.float32r
BF16 = mybir.dt.bfloat16
I32 = mybir.dt.int32

P = 128
B, S, D = 2, 1024, 256
M = 154
CT = 77
H, DH = 8, 64
E = 8
KB = D // P
TB = S // P
T = B * TB
N = B * S
CAP = N // E
REM = M - P
HG = 4
RK = HG * REM
NBLK = H + H // HG
HM = H * M
REC = D + 4
EPS = 1e-5
FAR = 4096.0
SIMG = [(0, 3), (3, 6), (6, 8)]
SLAB = 212000
OUT_SPLIT = 6


def at(off, n):
    return slice(off, off + n) if isinstance(off, int) else bass.ds(off, n)


def batch_of(t):
    return t // TB if isinstance(t, int) else (t >> 3).with_bounds(min_val=0, max_val=B - 1)


def known_zero(t):
    return isinstance(t, int) and t == 0


def build(nc, x, ctx_in, Wq, bq, Wk, bk, Wv, bv, g1, b1, g2, b2, WqX, Wkv, Wout, bout, Wr, br, W1, fb1, W2, fb2, out):
    X = x.rearrange("b (t p) d -> p (b t) d", p=P)
    OUT = out.rearrange("b s d -> (b s) d")
    slots = nc.dram_tensor("slots", [N, REC], F32)

    def row(v):
        return v.rearrange("(a n) -> a n", a=1)

    sizes = {F32: 4, F32R: 4, I32: 4, BF16: 2}

    with ExitStack() as whole:
        def sem(ctx, name):
            return ctx.enter_context(nc.semaphore(name))

        slab = whole.enter_context(nc.sbuf_tensor("slab", [P, SLAB], mybir.dt.uint8))
        origin = nc.sbuf_base - SLAB

        def lay(start, things):
            made = []
            for name, shape, dt in things:
                n = sizes[dt]
                for k in shape[1:]:
                    n *= k
                start = (start + 31) // 32 * 32
                made.append(nc.alloc_sbuf_tensor_at(name, shape, dt, offset=origin + start))
                start += n
            assert start <= SLAB, (start, SLAB)
            return made, start

        ps = whole.enter_context(nc.psum_tensor("ps", [P, 8, 512], F32))
        (ident, tri, ones, mhalf, tokens, cb, u, Ah, Al), end = lay(0, [
            ("ident", [P, P], F32), ("tri", [P, P], BF16), ("ones", [P, P], BF16), ("mhalf", [P, 4], F32),
            ("tokens", [P, T], I32),
            ("cb", [P, KB], F32),
            ("u", [P, T], F32),
            ("Ah", [P, KB, D], F32R), ("Al", [P, KB, D], F32R)])

        KW_AT = end = (end + 31) // 32 * 32
        (KWh, KWl), end = lay(end, [(f"KW{s}", [P, B * KB * HM], F32R) for s in "hl"])
        VW_AT = end
        (VWh, VWl), end = lay(end, [(f"VW{s}", [P, B * NBLK * D], F32R) for s in "hl"])
        XR_AT = end
        (xr,), end = lay(end, [("xr", [P, T * D], F32)])
        XT_AT = end
        (xhTh, xhTl), end = lay(end, [(f"xhT{s}", [P, B * KB * S], F32R) for s in "hl"])
        V_AT = end
        (Vh, Vl), TEMP = lay(end, [(f"V{s}", [P, T * D], F32R) for s in "hl"])
        xr3 = xr[:].rearrange("p (t c) -> p t c", c=D)
        ROW = 4 * D

        slots_set = sem(whole, "slots_set")

        (ctx_n, cnf, cnTh, cnTl, wkv, wkvh, wkvl), end = lay(KW_AT, [
            ("ctx_n", [CT, 4, D], F32), ("cnf", [P, KB, B * M], F32), ("cnTh", [P, KB, B * M], F32R), ("cnTl", [P, KB, B * M], F32R),
            ("wkv", [P, KB, 2 * H * DH], F32), ("wkvh", [P, KB, 2 * H * DH], F32R), ("wkvl", [P, KB, 2 * H * DH], F32R)])
        assert end <= VW_AT
        (wqx, wqTh, wqTl, wo, bqb, bkb, wqbk, prod), end = lay(VW_AT, [
            ("wqx", [P, KB, H * DH], F32), ("wqTh", [P, 4, D], F32R), ("wqTl", [P, 4, D], F32R), ("wo", [P, 4, D], F32),
            ("bqb", [P, D], F32), ("bkb", [P, D], F32), ("wqbk", [P, KB], F32), ("prod", [P, 5, D], F32)])
        assert end <= XR_AT
        (wv,), end = lay(V_AT + 14 * ROW, [("wv", [P, KB, D], F32)])
        assert end <= V_AT + T * ROW
        (wqr, wkr, aqh, akh, aql, akl), end = lay(V_AT + (T + 4) * ROW, [
            ("wqr", [P, KB, D], F32), ("wkr", [P, KB, D], F32), ("aqTh", [P, KB, D], F32R), ("akTh", [P, KB, D], F32R),
            ("aqTl", [P, KB, D], F32R), ("akTl", [P, KB, D], F32R)])
        assert end <= TEMP
        (kTh, kTl, vTh, vTl, vremh, vreml, woh, wol, wvh, wvl, xh, bvb, init, g2c, cst, cmv, crs, xst, xmv, xnm, xrs, qk), _ = lay(TEMP, [
            ("kTh", [P, 4, B * M], F32R), ("kTl", [P, 4, B * M], F32R), ("vTh", [P, 4, B * M], F32R), ("vTl", [P, 4, B * M], F32R),
            ("vremh", [P, B, 4, RK], F32R), ("vreml", [P, B, 4, RK], F32R),
            ("woh", [P, 4, D], F32R), ("wol", [P, 4, D], F32R),
            ("wvh", [P, KB, D + 2], F32R), ("wvl", [P, KB, D + 2], F32R),
            ("xh", [P, 2, D], F32), ("bvb", [P, D], F32), ("init", [P, REC], F32), ("g2c", [P, 2 * KB], F32),
            ("cst", [CT, 4, 6], F32), ("cmv", [CT, 4, 2], F32), ("crs", [CT, 4], F32),
            ("xst", [P, T, 6], F32), ("xmv", [P, T, 2], F32), ("xnm", [P, T], F32), ("xrs", [P, T], F32), ("qk", [P, 1], F32)])

        with ExitStack() as ph:
            names = ("wq_ld wk_ld bias_ld wv_ld ctx_ld g2_ld wqx_ld wk2_ld wv2_ld wo_ld bv_ld "
                     "zero_done iota_done ident_set ident_done init_done rem_zero cstat cvar crstd cz split_hi split_done "
                     "dots_done wcol_hi wcol_lo unit_mm unit_hi unit_lo cn_aff xstat xvar xrstd xh_done xt_mm xt_hi xt_lo "
                     "v_mm v_hi v_lo rem_done bv_done").split()
            Q = {n: sem(ph, "a_" + n) for n in names}
            x_in = [sem(ph, f"x_in{c}") for c in range(4)]

            units = [("at", 0), ("at", 1), ("am", 0), ("am", 1), ("cn", 0), ("cn", 1), ("wq", 0), ("wq", 1)]
            first_units = units[:]
            units += [("kv", j) for j in range(8)]
            units += [("kw", k, h) for h in range(H) for k in range(KB)]
            units += [("vw", b, j) for b in range(B) for j in range(4)] + [("vr", b) for b in range(B)]
            number = {q: i for i, q in enumerate(units)}
            tiles = []
            for t in range(2, T + 1):
                tiles += [("V", t - 2)] + [("T", t)] * (t < T)
            tiles.append(("V", T - 1))
            items = first_units[:4] + [("T", 0)] + first_units[4:6] + [("T", 1)] + first_units[6:]
            rest = units[len(first_units):]
            while tiles or rest:
                items += rest[:1] + tiles[:1]
                tiles, rest = tiles[1:], rest[1:]
            VWG = [(0, 2), (1, 3), (4, 6), (5, 7)]

            def pieces(q):
                bank = ps[:, 4 + number[q] % 4, :]
                kind, j = q[0], q[1]
                if kind == "at":
                    return bank.rearrange("p (e d) -> p e d", e=KB), (aqh, akh)[j][:], (aql, akl)[j][:]
                if kind == "wq":
                    return bank.rearrange("p (j d) -> p j d", j=2), wqTh[:, 2 * j:2 * j + 2, :], wqTl[:, 2 * j:2 * j + 2, :]
                if kind == "am":
                    return bank[:, 0:D], Ah[:, j, :], Al[:, j, :]
                if kind == "cn":
                    return cnf[:, j, :], cnTh[:, j, :], cnTl[:, j, :]
                if kind == "kv":
                    hi, lo = (kTh, kTl) if j < 4 else (vTh, vTl)
                    return bank[:, 0:B * M], hi[:, j % 4, :], lo[:, j % 4, :]
                if kind == "kw":
                    _, k, h = q
                    hi, lo = (w[:].rearrange("p (b k h m) -> p b k h m", b=B, k=KB, h=H)[:, :, k, h, :] for w in (KWh, KWl))
                    return bank[:, 0:B * M].rearrange("p (b m) -> p b m", b=B), hi, lo
                if kind == "vw":
                    o = q[1] * NBLK + VWG[q[2]][0]
                    hi, lo = (w[:].rearrange("p (n d) -> p n d", d=D)[:, o:o + 3:2, :] for w in (VWh, VWl))
                    return bank.rearrange("p (n d) -> p n d", n=2), hi, lo
                o = (j * NBLK + H) * D
                return bank[0:RK, :], VWh[0:RK, o:o + 2 * D], VWl[0:RK, o:o + 2 * D]

            keys, values = slice(0, H * DH), slice(H * DH, 2 * H * DH)
            splits = [("wv_ld", wvh[:, :, 0:D], wv[:], wvl[:, :, 0:D]), ("wk2_ld", wkvh[:, :, keys], wkv[:, :, keys], wkvl[:, :, keys]),
                      ("wv2_ld", wkvh[:, :, values], wkv[:, :, values], wkvl[:, :, values]), ("wo_ld", woh[:], wo[:], wol[:])]

            block = ph.enter_context(nc.Block())

            @block.sync
            def _(sp):
                wkv_in = Wkv.rearrange("(k p) e -> p k e", p=P)
                sp.dma_start(ctx_n[:], ctx_in.rearrange("b (a p) d -> p (b a) d", p=CT)).then_inc(Q["ctx_ld"], 16)
                sp.dma_start(xr3[:, 0:4, :], X[:, 0:4, :]).then_inc(x_in[0], 16)
                sp.dma_start(wqr[:], Wq.rearrange("(k p) e -> p k e", p=P)).then_inc(Q["wq_ld"], 16)
                sp.dma_start(wkr[:], Wk.rearrange("(k p) e -> p k e", p=P)).then_inc(Q["wk_ld"], 16)
                sp.dma_start(bqb[:], row(bq).broadcast_to([P, D])).then_inc(Q["bias_ld"], 16)
                sp.dma_start(bkb[:], row(bk).broadcast_to([P, D])).then_inc(Q["bias_ld"], 16)
                sp.dma_start(wv[:], Wv.rearrange("(k p) e -> p k e", p=P)).then_inc(Q["wv_ld"], 16)
                sp.dma_start(g2c[:, 0:KB], g2.rearrange("(k p) -> p k", p=P), allow_slow_non_contiguous=True).then_inc(Q["g2_ld"], 16)
                sp.dma_start(g2c[:, KB:2 * KB], b2.rearrange("(k p) -> p k", p=P), allow_slow_non_contiguous=True).then_inc(Q["g2_ld"], 16)
                sp.dma_start(wkv[:, :, keys], wkv_in[:, :, keys]).then_inc(Q["wk2_ld"], 16)
                sp.dma_start(wqx[:], WqX.rearrange("(k p) e -> p k e", p=P)).then_inc(Q["wqx_ld"], 16)
                sp.dma_start(wkv[:, :, values], wkv_in[:, :, values]).then_inc(Q["wv2_ld"], 16)
                sp.dma_start(xr3[:, 4:8, :], X[:, 4:8, :]).then_inc(x_in[1], 16)
                sp.dma_start(wo[:], Wout.rearrange("(j p) d -> p j d", p=P)).then_inc(Q["wo_ld"], 16)
                for c in range(2, 4):
                    sp.dma_start(xr3[:, 4 * c:4 * c + 4, :], X[:, 4 * c:4 * c + 4, :]).then_inc(x_in[c], 16)
                sp.dma_start(bvb[:], row(bv).broadcast_to([P, D])).then_inc(Q["bv_ld"], 16)
                sp.wait_ge(Q["init_done"], 2)
                for k in range(N // P):
                    sp.dma_start(slots[k * P:(k + 1) * P, :], init[:]).then_inc(slots_set, 16)
                sp.wait_ge(slots_set, 16 * (N // P))

            @block.gpsimd
            def _(pool):
                g = nc.gpsimd
                g.memset(mhalf[:], -0.5).then_inc(Q["ident_set"], 1)
                g.memset(ident[:], 0.0).then_inc(Q["ident_set"], 1)
                g.memset(ones[:], 1.0).then_inc(Q["ident_set"], 1)
                pool.wait_ge(Q["ident_set"], 3)
                g.affine_select(out=ident[:], in_=ident[:], compare_op=ALU.not_equal, fill=1.0, base=0,
                                pattern=[[-1, P]], channel_multiplier=1).then_inc(Q["ident_done"], 1)
                g.affine_select(out=tri[:], in_=ones[:], compare_op=ALU.is_ge, fill=0.0, base=0,
                                pattern=[[1, P]], channel_multiplier=-1).then_inc(Q["ident_done"], 1)
                pool.wait_ge(Q["cvar"], 1)
                pool.wait_ge(Q["ident_done"], 2)
                g.tensor_tensor(crs[:], cmv[:, :, 1], mhalf[0:CT, 0:4], ALU.pow).then_inc(Q["crstd"], 1)
                pool.wait_ge(Q["crstd"], 1)

                def rstd(c):
                    pool.wait_ge(Q["xvar"], 2 * c + 2)
                    g.tensor_tensor(xrs[:, 4 * c:4 * c + 4], xmv[:, 4 * c:4 * c + 4, 1], mhalf[:], ALU.pow).then_inc(Q["xrstd"], 1)
                    pool.wait_ge(Q["xrstd"], c + 1)

                def split_lo(n):
                    hi, raw, lo = splits[n][1:]
                    pool.wait_ge(Q["split_hi"], n + 1)
                    g.tensor_tensor(lo, raw, hi.bitcast(F32), ALU.subtract).then_inc(Q["split_done"], 1)

                def values_of_rest():
                    pool.wait_ge(Q["rem_zero"], 2)
                    pool.wait_ge(Q["unit_lo"], number[("kv", 7)] + 1)
                    made = 0
                    for src, dst in ((vTh, vremh), (vTl, vreml)):
                        for h in range(H):
                            r, c = 64 * (h % 2), REM * (h % HG)
                            g.tensor_copy(dst[r:r + 64, :, h // 2, c:c + REM],
                                          src[r:r + 64, h // 2, :].rearrange("p (b m) -> p b m", b=B)[:, :, P:M].bitcast(F32)).then_inc(Q["rem_done"], 1)
                            made += 1
                            pool.wait_ge(Q["rem_done"], made)

                for t in range(T):
                    if t % 4 == 0:
                        rstd(t // 4)
                    if t == 2:
                        split_lo(0)
                        split_lo(1)
                    if t == 3:
                        split_lo(2)
                    if t == 4:
                        for z in (vremh, vreml):
                            g.memset(z[:].bitcast(F32), 0.0).then_inc(Q["rem_zero"], 1)
                    if t == 5:
                        split_lo(3)
                        g.memset(init[:], 0.0).then_inc(Q["init_done"], 1)
                        pool.wait_ge(Q["init_done"], 1)
                        g.iota(init[:, REC - 1:REC].bitcast(I32), pattern=[[0, 1]], base=int(FAR), channel_multiplier=0).then_inc(Q["init_done"], 1)
                        g.iota(tokens[:], pattern=[[P, T]], base=0, channel_multiplier=1).then_inc(Q["iota_done"], 1)
                    if t == 8:
                        pool.wait_ge(Q["xh_done"], t)
                        values_of_rest()
                    if t >= 2:
                        pool.wait_ge(Q["xt_mm"], t - 1)
                    g.tensor_scalar(xh[:, t % 2, :], xr3[:, t, :], xnm[:, t:t + 1], xrs[:, t:t + 1], ALU.add, ALU.mult).then_inc(Q["xh_done"], 1)
                pool.wait_ge(Q["bv_ld"], 16)
                for c in range(4):
                    pool.wait_ge(Q["xh_done"], 4 * c + 4)
                    xc = xr3[:, 4 * c:4 * c + 4, :]
                    g.tensor_tensor(xc, xc, bvb[:].rearrange("p (a d) -> p a d", a=1).broadcast_to([P, 4, D]), ALU.add).then_inc(Q["bv_done"], 1)

            @block.scalar
            def _(act):
                a = nc.scalar.activation
                def split_high(n):
                    ld, hi, raw = splits[n][:3]
                    act.wait_ge(Q[ld], 16)
                    a(hi, raw, ACT.Copy).then_inc(Q["split_hi"], 1)

                for q in items:
                    kind, t = q[0], q[1]
                    if q == ("am", 0):
                        split_high(0)
                    if q == ("cn", 0):
                        split_high(1)
                    if q == ("kv", 0):
                        split_high(2)
                        act.wait_ge(Q["dots_done"], 5)
                        for k in range(KB):
                            a(wvh[:, k, D:D + 2], wqbk[:, k:k + 1].broadcast_to([P, 2]), ACT.Copy).then_inc(Q["wcol_hi"], 1)
                    if q == ("T", 3):
                        split_high(3)
                    if kind == "T":
                        act.wait_ge(Q["xt_mm"], t + 1)
                        b, o = t // TB, (t % TB) * P
                        dst = xhTh[:].rearrange("p (b k n) -> p b k n", b=B, k=KB)[:, b, :, o:o + P]
                        a(dst, ps[:, t % 2, 0:D].rearrange("p (k n) -> p k n", k=KB), ACT.Copy).then_inc(Q["xt_hi"], 1)
                    elif kind == "V":
                        act.wait_ge(Q["v_mm"], t + 1)
                        a(Vh[:, t * D:(t + 1) * D], ps[:, 2 + t % 2, 0:D], ACT.Copy).then_inc(Q["v_hi"], 1)
                    else:
                        act.wait_ge(Q["unit_mm"], number[q] + 1)
                        if kind == "cn":
                            act.wait_ge(Q["g2_ld"], 32)
                            a(cnf[:, t, :], ps[:, 4 + number[q] % 4, 0:B * M], ACT.Identity, bias=g2c[:, KB + t:KB + t + 1],
                              scale=g2c[:, t:t + 1]).then_inc(Q["cn_aff"], 1)
                            act.wait_ge(Q["cn_aff"], t + 1)
                        src, hi, lo = pieces(q)
                        a(hi, src, ACT.Copy).then_inc(Q["unit_hi"], 1)

            @block.vector
            def _(dve):
                v = nc.vector

                def x_stats(tiles):
                    for t in tiles:
                        c = t // 4
                        if t % 4 == 0:
                            dve.wait_ge(x_in[c], 16)
                        v.bn_stats(xst[:, t, :], xr3[:, t, :]).then_inc(Q["xstat"], 1)
                        if t % 4 == 3:
                            for i in range(4 * c, t + 1):
                                dve.wait_ge(Q["xstat"], 4 * c + i + 1)
                                v.bn_aggr(xmv[:, i, :], xst[:, i, :]).then_inc(Q["xstat"], 1)
                            dve.wait_ge(Q["xstat"], 8 * c + 8)
                            v.tensor_scalar(xmv[:, 4 * c:t + 1, 1], xmv[:, 4 * c:t + 1, 1], EPS, None, ALU.add).then_inc(Q["xvar"], 1)
                            v.tensor_scalar(xnm[:, 4 * c:t + 1], xmv[:, 4 * c:t + 1, 0], -1.0, None, ALU.mult).then_inc(Q["xvar"], 1)

                def unit_low(q):
                    dve.wait_ge(Q["unit_hi"], number[q] + 1)
                    src, hi, lo = pieces(q)
                    v.tensor_tensor(lo, src, hi.bitcast(F32), ALU.subtract).then_inc(Q["unit_lo"], 1)

                dve.wait_ge(Q["ctx_ld"], 16)
                for a in range(4):
                    v.bn_stats(cst[:, a, :], ctx_n[:, a, :]).then_inc(Q["cstat"], 1)
                for a in range(4):
                    dve.wait_ge(Q["cstat"], 4 + a)
                    v.bn_aggr(cmv[:, a, :], cst[:, a, :]).then_inc(Q["cstat"], 1)
                dve.wait_ge(Q["cstat"], 8)
                v.tensor_scalar(cmv[:, :, 1], cmv[:, :, 1], EPS, None, ALU.add).then_inc(Q["cvar"], 1)
                x_stats(range(4))
                unit_low(("at", 0))
                unit_low(("at", 1))
                dve.wait_ge(Q["crstd"], 1)
                for a in range(4):
                    v.tensor_scalar(ctx_n[:, a, :], ctx_n[:, a, :], cmv[:, a, 0:1], crs[:, a:a + 1],
                                    ALU.subtract, ALU.mult).then_inc(Q["cz"], 1)
                dve.wait_ge(Q["bias_ld"], 32)
                for n, (w, bias, to) in enumerate(((wqr[:, 0, :], bkb, wqbk[:, 0:1]), (wqr[:, 1, :], bkb, wqbk[:, 1:2]),
                                                   (wkr[:, 0, :], bqb, cb[:, 0:1]), (wkr[:, 1, :], bqb, cb[:, 1:2]),
                                                   (bqb[:], bkb, qk[:]))):
                    v.tensor_tensor_reduce(prod[:, n, :], w, bias[:], 1.0, 0.0, ALU.mult, ALU.add, to).then_inc(Q["dots_done"], 1)
                dve.wait_ge(Q["dots_done"], 5)
                for q in items:
                    kind, t = q[0], q[1]
                    if kind == "at":
                        continue
                    if q == ("kv", 0):
                        dve.wait_ge(Q["wcol_hi"], 2)
                        for k in range(KB):
                            v.tensor_tensor(wvl[:, k, D:D + 2], wqbk[:, k:k + 1].broadcast_to([P, 2]), wvh[:, k, D:D + 2].bitcast(F32),
                                            ALU.subtract).then_inc(Q["wcol_lo"], 1)
                    if q == ("T", 1):
                        x_stats((4, 5))
                    if q == ("V", 0):
                        x_stats((6, 7))
                    if kind == "T" and 2 <= t < T - 6:
                        x_stats((t + 6,))
                    if kind == "T":
                        dve.wait_ge(Q["xt_hi"], t + 1)
                        b, o = t // TB, (t % TB) * P
                        hi, lo = (w[:].rearrange("p (b k n) -> p b k n", b=B, k=KB)[:, b, :, o:o + P] for w in (xhTh, xhTl))
                        v.tensor_tensor(lo, ps[:, t % 2, 0:D].rearrange("p (k n) -> p k n", k=KB), hi.bitcast(F32), ALU.subtract).then_inc(Q["xt_lo"], 1)
                    elif kind == "V":
                        dve.wait_ge(Q["v_hi"], t + 1)
                        c = slice(t * D, (t + 1) * D)
                        v.tensor_tensor(Vl[:, c], ps[:, 2 + t % 2, 0:D], Vh[:, c].bitcast(F32), ALU.subtract)
                        v.tensor_tensor(u[:, t:t + 1], ps[:, 2 + t % 2, D:D + 1], qk[:], ALU.add).then_inc(Q["v_lo"], 1)
                    else:
                        unit_low(q)

            @block.tensor
            def _(pe):
                def product(o, a, b, first=True, last=True):
                    nc.tensor.matmul(o, a[0], b[0], start=first, stop=False)
                    nc.tensor.matmul(o, a[0], b[1], start=False, stop=False)
                    return nc.tensor.matmul(o, a[1], b[0], start=False, stop=last)

                def unit(q):
                    i, kind = number[q], q[0]
                    if i >= 4:
                        pe.wait_ge(Q["unit_lo"], i - 3)
                    bank = ps[:, 4 + i % 4, :]
                    if kind == "at":
                        n = q[1]
                        pe.wait_ge(Q[("wq_ld", "wk_ld")[n]], 16)
                        for e in range(KB):
                            for k in range(KB):
                                last = nc.tensor.transpose(bank[:, e * D + k * P:e * D + (k + 1) * P],
                                                           (wqr, wkr)[n][:, k, e * P:(e + 1) * P], ident[:])
                    elif kind == "wq":
                        pe.wait_ge(Q["wqx_ld"], 16)
                        for j in range(2):
                            for k in range(KB):
                                e = 2 * q[1] + j
                                last = nc.tensor.transpose(bank[:, j * D + k * P:j * D + (k + 1) * P], wqx[:, k, e * P:(e + 1) * P], ident[:])
                    elif kind == "am":
                        k = q[1]
                        pe.wait_ge(Q["unit_lo"], 2)
                        for e in range(KB):
                            d = slice(k * P, (k + 1) * P)
                            last = product(bank[:, 0:D], (aqh[:, e, d], aql[:, e, d]), (akh[:, e, :], akl[:, e, :]), e == 0, e == KB - 1)
                    elif kind == "cn":
                        k = q[1]
                        pe.wait_ge(Q["cz"], 4)
                        for a in range(4):
                            last = nc.tensor.transpose(bank[:, a * CT:(a + 1) * CT], ctx_n[:, a, k * P:(k + 1) * P], ident[0:CT, 0:CT])
                    elif kind == "kv":
                        if q[1] == 0:
                            pe.wait_ge(Q["unit_lo"], number[("cn", KB - 1)] + 1)
                            pe.wait_ge(Q["split_done"], 2)
                        if q[1] == 4:
                            pe.wait_ge(Q["split_done"], 3)
                        w = slice(q[1] * P, (q[1] + 1) * P)
                        for k in range(KB):
                            last = product(bank[:, 0:B * M], (wkvh[:, k, w], wkvl[:, k, w]), (cnTh[:, k, :], cnTl[:, k, :]), k == 0, k == KB - 1)
                    elif kind == "kw":
                        _, k, h = q
                        pe.wait_ge(Q["unit_lo"], number[("kv", 3)] + 1)
                        r, d = slice(64 * (h % 2), 64 * (h % 2) + 64), slice(k * P, (k + 1) * P)
                        last = product(bank[:, 0:B * M], (wqTh[r, h // 2, d], wqTl[r, h // 2, d]), (kTh[r, h // 2, :], kTl[r, h // 2, :]))
                    elif kind == "vw":
                        _, b, j = q
                        pe.wait_ge(Q["unit_lo"], number[("kv", 7)] + 1)
                        pe.wait_ge(Q["split_done"], 4)
                        for n, h in enumerate(VWG[j]):
                            r = slice(64 * (h % 2), 64 * (h % 2) + 64)
                            m = slice(b * M, b * M + P)
                            last = product(bank[:, n * D:(n + 1) * D], (vTh[r, h // 2, m], vTl[r, h // 2, m]), (woh[r, h // 2, :], wol[r, h // 2, :]))
                    else:
                        b = q[1]
                        pe.wait_ge(Q["rem_done"], 2 * H)
                        for g in range(H // HG):
                            for j in (2 * g, 2 * g + 1):
                                last = product(bank[0:RK, g * D:(g + 1) * D], (vremh[:, b, j, :], vreml[:, b, j, :]), (woh[:, j, :], wol[:, j, :]),
                                               j % 2 == 0, j % 2 == 1)
                    last.then_inc(Q["unit_mm"], 1)

                pe.wait_ge(Q["ident_done"], 2)
                for q in items:
                    t = q[1]
                    if q[0] == "T":
                        pe.wait_ge(Q["xh_done"], t + 1)
                        if t >= 2:
                            pe.wait_ge(Q["xt_lo"], t - 1)
                        for k in range(KB):
                            last = nc.tensor.transpose(ps[:, t % 2, k * P:(k + 1) * P], xh[:, t % 2, k * P:(k + 1) * P], ident[:])
                        last.then_inc(Q["xt_mm"], 1)
                    elif q[0] == "V":
                        pe.wait_ge(Q["xt_lo"], t + 1)
                        if t == 0:
                            pe.wait_ge(Q["split_done"], 1)
                            pe.wait_ge(Q["wcol_lo"], 2)
                        if t >= 2:
                            pe.wait_ge(Q["v_lo"], t - 1)
                        for k in range(KB):
                            o = ((t // TB) * KB + k) * S + (t % TB) * P
                            last = product(ps[:, 2 + t % 2, 0:D + 2], (xhTh[:, o:o + P], xhTl[:, o:o + P]), (wvh[:, k, :], wvl[:, k, :]), k == 0, k == KB - 1)
                        last.then_inc(Q["v_mm"], 1)
                    else:
                        unit(q)

        PSC = D ** -0.5
        P2SC = DH ** -0.5
        with ExitStack() as ph:
            (GTh, GTl, Pr, PTh, PTl, P2, P2r, P2Th, P2Tl, x1s, x2s, rec, zn, xnTh, xnTl, z3, z3T, g1b, b1b, boutb, wr, brb, desc, base, sm, racc, oh, idx), _ = lay(TEMP, [
                ("GTh", [P, KB, P], F32R),
                ("GTl", [P, KB, P], F32R),
                ("Pr", [P, S], F32),
                ("PTh", [P, S], F32R),
                ("PTl", [P, S], F32R),
                ("P2", [P, HM], F32),
                ("P2r", [P, H, REM], F32),
                ("P2Th", [P, NBLK * P], F32R),
                ("P2Tl", [P, NBLK * P], F32R),
                ("x1s", [P, D], F32),
                ("x2s", [P, D + 2], F32),
                ("rec", [P, REC], F32),
                ("zn", [P, D], F32),
                ("xnTh", [P, D], F32R),
                ("xnTl", [P, D], F32R),
                ("z3", [P, D], F32),
                ("z3T", [P, D], F32),
                ("g1b", [P, D], F32),
                ("b1b", [P, D], F32),
                ("boutb", [P, D], F32),
                ("wr", [P, KB, E], F32),
                ("brb", [P, E], F32),
                ("desc", [P, E], F32),
                ("base", [P, E], F32),
                ("sm", [P, 160], F32),
                ("racc", [P, E], BF16),
                ("oh", [P, E], BF16),
                ("idx", [P, 1], I32)])
            st1, mv1, r1, v1 = sm[:, 0:6], sm[:, 6:8], sm[:, 8:9], sm[:, 9:10]
            mx, sh, nb, ssum, rs = (sm[:, c:c + 1] for c in range(10, 15))
            mx2, nb2, ss2, rs2 = sm[:, 16:24], sm[:, 24:32], sm[:, 32:40], sm[:, 40:48]
            st3, r3s, v3 = sm[:, 48:54], (sm[:, 54:55], sm[:, 112:113]), sm[:, 55:56]
            lg, e8, w8 = sm[:, 56:64], sm[:, 64:72], sm[:, 72:80]
            mx3, nmx3, se, wm, slot_at = (sm[:, c:c + 1] for c in range(80, 85))
            far, pb, q8 = sm[:, 88:96], sm[:, 96:104], sm[:, 104:112]

            names = ("par_ld const_c g_mm g_hi g_lo s_mm s_max s_sh s_nb p_done rs_done tp_mm tp_hi tp_lo pv_mm "
                     "x1_done st1_done mv1_done v1_done r1_done z_done zg_done zn_done xb_done zt_mm xn_hi xn_lo "
                     "sim_mm max2 nb2_done exp2 rs2_done p2_done t2_mm t2_hi t2_lo out_mm x2_done st3_done mv3_done "
                     "v3_done r3_done z3_done zt3_mm zt3_sb lg_mm lg_done mx3_done nmx3_done e8_done w8_done wm_done "
                     "oh_done gate_done rg_done cnt_mm far_done pb_done q1_done q2_done slot_done idx_done racc_done "
                     "x2_out scattered idx_read token_set rec_x").split()
            Q = {n: sem(ph, n) for n in names}

            holes = [KW_AT, KW_AT + 4 * B * KB * HM, VW_AT, VW_AT + 4 * B * NBLK * D,
                     XT_AT, XT_AT + 4 * B * KB * S, V_AT, V_AT + 4 * T * D]
            W = {}
            for half in range(2):
                for n in range(2):
                    for part in range(3):
                        hole = holes[4 * half + 2 * n + min(part, 1)]
                        name, dt = f"W{n + 1}{('hi', 'lo', 'raw')[part]}{half}", (F32R, F32R, F32)[part]
                        (W[n, part, half],), _ = lay(hole, [(name, [P, E // 2, KB * D], dt)])
            w_ld = {(n, half): sem(ph, f"w{n + 1}_ld{half}") for half in range(2) for n in range(2)}
            w_hi = sem(ph, "w_hi")
            w_pool = sem(ph, "w_pool")
            SPLIT = {T - 1: (6, 0), T: (3, 1), T + 1: (2, 1), T + 2: (2, 1)}
            order = [(e, n) for e in range(E) for n in range(2)]
            shares, done = {}, 0
            for s_, (n_pool, n_dve) in SPLIT.items():
                shares[s_] = (range(done, done + n_pool), range(done + n_pool, done + n_pool + n_dve))
                done += n_pool + n_dve
            assert done == len(order)

            (P2z, P2rz), _ = lay(XT_AT + 4 * KB * S, [("P2_last", [P, HM], F32), ("P2r_last", [P, H, REM], F32)])

            (P2Thz,), _ = lay(XT_AT + 4 * (B + 1) * KB * S, [("P2Th_last", [P, NBLK * P], F32R)])
            (P2Tlz,), _ = lay(V_AT + TB * ROW, [("P2Tl_last", [P, NBLK * P], F32R)])

            def p2_of(t):
                return (P2z, P2rz) if isinstance(t, int) and t == T - 1 else (P2, P2r)

            def p2t_of(t):
                return (P2Thz, P2Tlz) if isinstance(t, int) and t == T - 1 else (P2Th, P2Tl)

            def piece(i, part):
                e, n = order[i]
                return W[n, part, e // (E // 2)][:, e % (E // 2), :]

            block = ph.enter_context(nc.Block())
            BIG = ps[:].rearrange("p b n -> p (b n)")

            def bank(i):
                return ps[:, i, :]

            def out_bank(t):
                return bank(6 if isinstance(t, int) and t == T - 1 else 3)

            def r3_of(t):
                return r3s[isinstance(t, int) and t == T - 1]

            LOOP = (5, T - 1)

            def slots_of(eng, slot):
                for s in range(LOOP[0]):
                    slot(s)
                with eng.Fori(*LOOP) as s:
                    slot(s)
                slot(LOOP[1])

            def live(t):
                return not isinstance(t, int) or 0 <= t < T

            @block.sync
            def _(sp):
                sp.dma_start(g1b[:], row(g1).broadcast_to([P, D])).then_inc(Q["par_ld"], 16)
                sp.dma_start(b1b[:], row(b1).broadcast_to([P, D])).then_inc(Q["par_ld"], 16)
                sp.dma_start(boutb[:], row(bout).broadcast_to([P, D])).then_inc(Q["par_ld"], 16)
                sp.dma_start(wr[:], Wr.rearrange("(k p) e -> p k e", p=P)).then_inc(Q["par_ld"], 16)
                sp.dma_start(brb[:], row(br).broadcast_to([P, E])).then_inc(Q["par_ld"], 16)
                def rows_out(t):
                    sp.wait_ge(Q["rec_x"], t + 1)
                    sp.dma_start(OUT[at(t * P, P), :], rec[:, 0:D]).then_inc(Q["x2_out"], 16)

                with sp.Fori(0, TB) as t:
                    rows_out(t)
                for half in range(2):
                    for n, w in enumerate((W1, W2)):
                        sp.dma_start(W[n, 2, half][:].rearrange("p e (k f) -> p e k f", k=KB),
                                     w[half * (E // 2):(half + 1) * (E // 2)].rearrange("e (k p) f -> p e k f", p=P)).then_inc(w_ld[n, half], 16)
                with sp.Fori(TB, T) as t:
                    rows_out(t)
                sp.wait_ge(Q["x2_out"], 16 * T)

            @block.tensor
            def _(pe):
                def mm(o, a, b, first=False, last=False):
                    return nc.tensor.matmul(o, a, b, start=first, stop=last)

                def product(o, a, b, first=True, last=True):
                    mm(o, a[0], b[0], first)
                    mm(o, a[0], b[1])
                    return mm(o, a[1], b[0], False, last)

                def project(t):
                    if not isinstance(t, int) or t >= 2:
                        pe.wait_ge(Q["tp_lo"], 2 * (t - 1))
                    for k in range(KB):
                        for d in range(KB):
                            c = slice(k * P, (k + 1) * P)
                            o = at(batch_of(t) * ((KB - 1) * S) + d * S + t * P, P)
                            last = product(bank(4)[:, c], (Ah[:, d, c], Al[:, d, c]), (xhTh[:, o], xhTl[:, o]), d == 0, d == KB - 1)
                    last.then_inc(Q["g_mm"], 1)

                def p_turn(t):
                    pe.wait_ge(Q["p_done"], t + 1)
                    if isinstance(t, int) and t + 1 >= T:
                        pe.wait_ge(Q["g_lo"], T)
                    else:
                        pe.wait_ge(Q["g_lo"], t + 2)
                    if not isinstance(t, int) or t >= 3:
                        pe.wait_ge(Q["x2_done"], t - 2)
                    for n in range(TB):
                        last = nc.tensor.transpose(BIG[:, (3 * 4 + n) * P:(3 * 4 + n + 1) * P], Pr[:, n * P:(n + 1) * P], ident[:])
                        if n % 4 == 3:
                            last.then_inc(Q["tp_mm"], 1)

                def p2_turn(t):
                    pe.wait_ge(Q["p2_done"], t + 1)
                    pe.wait_ge(Q["x1_done"], T if isinstance(t, int) and t + 2 > T else t + 2)
                    pe.wait_ge(Q["p_done"], T if isinstance(t, int) and t + 3 > T else t + 3)
                    for n in range(NBLK):
                        if n < H:
                            src, rows = p2_of(t)[0][:, n * M:n * M + P], P
                        else:
                            h = (n - H) * HG
                            src = p2_of(t)[1][:, h:h + HG, :].rearrange("p h m -> p (h m)")
                            rows = RK
                        last = nc.tensor.transpose(BIG[0:rows, n * P:(n + 1) * P], src, ident[:])
                        if n % 4 == 3 or n == NBLK - 1:
                            last.then_inc(Q["t2_mm"], 1)

                def sim(t):
                    pe.wait_ge(Q["xn_lo"], t + 1)
                    b = batch_of(t)
                    for g in range(3):
                        if g == 2 and (not isinstance(t, int) or t >= 3):
                            pe.wait_ge(Q["q2_done"], t - 2)
                        n = (SIMG[g][1] - SIMG[g][0]) * M
                        if not known_zero(t):
                            pe.wait_ge(Q["exp2"], 3 * (t - 1) + g + 1)
                        for k in range(KB):
                            d = slice(k * P, (k + 1) * P)
                            o = at((b * KB + k) * HM + SIMG[g][0] * M, n)
                            last = product(bank(5 + g)[:, 0:n], (xnTh[:, d], xnTl[:, d]), (KWh[:, o], KWl[:, o]), k == 0, k == KB - 1)
                        last.then_inc(Q["sim_mm"], 1)

                def z3_turn(t):
                    if isinstance(t, int) and t == T - 1:
                        pe.wait_ge(Q["lg_done"], T - 1)
                    pe.wait_ge(Q["z3_done"], t + 1)
                    pe.wait_ge(Q["tp_lo"], 2 * T if isinstance(t, int) and t + 4 > T else 2 * (t + 4))
                    for k in range(KB):
                        d = slice(k * P, (k + 1) * P)
                        last = nc.tensor.transpose(bank(4)[:, d], z3[:, d], ident[:])
                    last.then_inc(Q["zt3_mm"], 1)

                def pv(t):
                    b = batch_of(t)
                    for n in range(TB):
                        if n % 4 == 0:
                            pe.wait_ge(Q["tp_lo"], 2 * t + n // 4 + 1)
                        if n == 0 and (not isinstance(t, int) or t >= 2):
                            pe.wait_ge(Q["t2_lo"], 3 * (t - 1) - 2)
                        c = slice(n * P, (n + 1) * P)
                        o = at((b * TB + n) * D, D)
                        last = product(bank(0)[:, 0:D], (PTh[:, c], PTl[:, c]), (Vh[:, o], Vl[:, o]), n == 0, n == TB - 1)
                    last.then_inc(Q["pv_mm"], 1)

                def logits(t):
                    if known_zero(t):
                        pe.wait_ge(Q["par_ld"], 80)
                    pe.wait_ge(Q["zt3_sb"], t + 1)
                    for k in range(KB):
                        last = mm(bank(4)[:, 0:E], z3T[:, k * P:(k + 1) * P], wr[:, k, :], k == 0, k == KB - 1)
                    last.then_inc(Q["lg_mm"], 1)

                def scores(t):
                    pe.wait_ge(Q["g_lo"], t + 1)
                    if not isinstance(t, int) or t >= 3:
                        pe.wait_ge(Q["t2_lo"], 3 * (t - 2) if not isinstance(t, int) or t - 2 <= T else 3 * T)
                    b = batch_of(t)
                    for h in range(2):
                        for k in range(KB):
                            o = at((b * KB + k) * S + h * 512, 512)
                            last = product(bank(1 + h), (GTh[:, k, :], GTl[:, k, :]), (xhTh[:, o], xhTl[:, o]), k == 0, k == KB - 1)
                    last.then_inc(Q["s_mm"], 1)

                def count(t, sim_tile):
                    pe.wait_ge(Q["oh_done"], t + 1)
                    pe.wait_ge(Q["exp2"], 3 * T if isinstance(sim_tile, int) and sim_tile >= T else 3 * sim_tile + 3)
                    mm(bank(7)[:, 0:E], tri[:], oh[:], True, False)
                    mm(bank(7)[:, 0:E], ones[:], racc[:], False, True).then_inc(Q["cnt_mm"], 1)

                def outp(t, blocks):
                    b = batch_of(t)
                    o_bank = out_bank(t)
                    p2h, p2l = p2t_of(t)
                    for n in blocks:
                        if n == 0:
                            pe.wait_ge(Q["tp_lo"], 2 * T if isinstance(t, int) and t + 3 > T else 2 * (t + 3))
                        if n % 4 == 0:
                            pe.wait_ge(Q["t2_lo"], 3 * t + n // 4 + 1)
                        rows = P if n < H else RK
                        c = slice(n * P, (n + 1) * P)
                        o = at((b * NBLK + n) * D, D)
                        last = product(o_bank[:, 0:D], (p2h[0:rows, c], p2l[0:rows, c]), (VWh[0:rows, o], VWl[0:rows, o]),
                                       n == 0, n == NBLK - 1)
                    if NBLK - 1 in blocks:
                        last.then_inc(Q["out_mm"], 1)

                def z_turn(t):
                    pe.wait_ge(Q["zn_done"], t + 1)
                    if not known_zero(t):
                        pe.wait_ge(Q["exp2"], 3 * (t - 1) + 1)
                    for k in range(KB):
                        d = slice(k * P, (k + 1) * P)
                        last = nc.tensor.transpose(bank(5)[:, d], zn[:, d], ident[:])
                    last.then_inc(Q["zt_mm"], 1)

                def slot(s):
                    if live(s - 3):
                        p2_turn(s - 3)
                    if live(s - 1):
                        p_turn(s - 1)
                    if live(s - 2):
                        sim(s - 2)
                    if live(s - 4):
                        z3_turn(s - 4)
                    if live(s - 1):
                        pv(s - 1)
                    if live(s - 4):
                        logits(s - 4)
                    scores(s)
                    if live(s - 3):
                        outp(s - 3, range(OUT_SPLIT))
                    if live(s - 4):
                        count(s - 4, s - 2)
                    if live(s - 1):
                        z_turn(s - 1)
                    if live(s + 1):
                        if live(s - 4):
                            pe.wait_ge(Q["lg_done"], s - 3)
                        project(s + 1)
                    if live(s - 3):
                        outp(s - 3, range(OUT_SPLIT, NBLK))

                pe.wait_ge(Q["const_c"], 4)
                project(0)
                slots_of(pe, slot)
                p_turn(T - 1)
                p2_turn(T - 3)
                sim(T - 2)
                z3_turn(T - 4)
                pv(T - 1)
                outp(T - 3, range(NBLK))
                logits(T - 4)
                z_turn(T - 1)
                count(T - 4, T - 2)
                sim(T - 1)
                p2_turn(T - 2)
                z3_turn(T - 3)
                logits(T - 3)
                count(T - 3, T - 1)
                p2_turn(T - 1)
                outp(T - 2, range(NBLK))
                outp(T - 1, range(NBLK))
                z3_turn(T - 2)
                logits(T - 2)
                count(T - 2, T)
                z3_turn(T - 1)
                logits(T - 1)
                count(T - 1, T)

            @block.scalar
            def _(act):
                a = nc.scalar.activation

                def p_hi(t):
                    for h in range(2):
                        act.wait_ge(Q["tp_mm"], 2 * t + h + 1)
                        a(PTh[:, h * 512:(h + 1) * 512], bank(3 + h), ACT.Copy).then_inc(Q["tp_hi"], 1)

                def p2_hi(t):
                    for g in range(3):
                        act.wait_ge(Q["t2_mm"], 3 * t + g + 1)
                        rows, n = (P, 512) if g < 2 else (RK, 256)
                        a(p2t_of(t)[0][0:rows, g * 512:g * 512 + n], bank(g)[0:rows, 0:n], ACT.Copy).then_inc(Q["t2_hi"], 1)

                def exp2(t):
                    for g in range(3):
                        act.wait_ge(Q["nb2_done"], 3 * t + g + 1)
                        for n in range(*SIMG[g]):
                            o = (n - SIMG[g][0]) * M
                            last = a(p2_of(t)[0][:, n * M:(n + 1) * M], bank(5 + g)[:, o:o + M], ACT.Exp, bias=nb2[:, n:n + 1], scale=P2SC,
                                     accum_out=ss2[:, n:n + 1])
                        last.then_inc(Q["exp2"], 1)

                def record(t):
                    if not known_zero(t):
                        act.wait_ge(Q["scattered"], 16 * t)
                        act.wait_ge(Q["x2_out"], 16 * t)
                    act.wait_ge(Q["mv3_done"], t + 1)
                    a(rec[:, 0:D + 1], x2s[:, 0:D + 1], ACT.Copy).then_inc(Q["rec_x"], 1)

                def gate(t):
                    act.wait_ge(Q["nmx3_done"], t + 1)
                    if not known_zero(t):
                        act.wait_ge(Q["gate_done"], t)
                    a(e8, lg, ACT.Exp, bias=nmx3, scale=1.0, accum_out=se).then_inc(Q["e8_done"], 1)

                def exps(t):
                    act.wait_ge(Q["s_nb"], t + 1)
                    if not known_zero(t):
                        act.wait_ge(Q["tp_mm"], 2 * t)
                        act.wait_ge(Q["rs_done"], t)
                    a(Pr[:], BIG[:, 512:1536], ACT.Exp, bias=nb, scale=PSC, accum_out=ssum).then_inc(Q["p_done"], 1)

                def xn_hi(t):
                    act.wait_ge(Q["zt_mm"], t + 1)
                    a(xnTh[:], bank(5)[:, 0:D], ACT.Copy).then_inc(Q["xn_hi"], 1)

                def g_hi(t):
                    act.wait_ge(Q["g_mm"], t + 1)
                    for k in range(KB):
                        last = a(GTh[:, k, :], bank(4)[:, k * P:(k + 1) * P], ACT.Identity, bias=cb[:, k:k + 1], scale=1.0)
                    last.then_inc(Q["g_hi"], 1)

                def weights_hi(s):
                    for share in shares[s]:
                        for i in share:
                            e, n = order[i]
                            act.wait_ge(w_ld[n, e // (E // 2)], 16)
                            a(piece(i, 0), piece(i, 2), ACT.Copy).then_inc(w_hi, 1)

                def slot(s):
                    if live(s - 3):
                        p2_hi(s - 3)
                    if live(s - 1):
                        p_hi(s - 1)
                    if live(s - 2):
                        exp2(s - 2)
                    if live(s - 4):
                        record(s - 4)
                        gate(s - 4)
                    exps(s)
                    if live(s - 1):
                        xn_hi(s - 1)
                    if live(s + 1):
                        g_hi(s + 1)

                g_hi(0)
                slots_of(act, slot)
                weights_hi(T - 1)
                p_hi(T - 1)
                p2_hi(T - 3)
                exp2(T - 2)
                record(T - 4)
                gate(T - 4)
                xn_hi(T - 1)
                weights_hi(T)
                exp2(T - 1)
                p2_hi(T - 2)
                record(T - 3)
                gate(T - 3)
                weights_hi(T + 1)
                p2_hi(T - 1)
                record(T - 2)
                weights_hi(T + 2)
                gate(T - 2)
                record(T - 1)
                gate(T - 1)

            @block.gpsimd
            def _(pool):
                g = nc.gpsimd
                g.memset(racc[:], 0.0).then_inc(Q["const_c"], 1)
                g.iota(q8, pattern=[[1, E]], base=0, channel_multiplier=0, allow_small_or_imprecise_dtypes=True).then_inc(Q["const_c"], 1)
                pool.wait_ge(Q["const_c"], 2)
                g.tensor_scalar(desc[:], q8, -1.0, float(E), ALU.mult, ALU.add).then_inc(Q["const_c"], 1)
                g.tensor_scalar(base[:], q8, float(CAP), 0.0, ALU.mult, ALU.add).then_inc(Q["const_c"], 1)
                last_row = pool.to_reg(N - 1)
                pool.wait_ge(Q["par_ld"], 80)

                def affine(t):
                    pool.wait_ge(Q["v1_done"], t + 1)
                    g.tensor_tensor(r1, v1, mhalf[:, 0:1], ALU.pow).then_inc(Q["r1_done"], 1)
                    pool.wait_ge(Q["z_done"], t + 1)
                    g.tensor_tensor(zn[:], zn[:], g1b[:], ALU.mult).then_inc(Q["zg_done"], 1)
                    pool.wait_ge(Q["zg_done"], t + 1)
                    g.tensor_tensor(zn[:], zn[:], b1b[:], ALU.add).then_inc(Q["zn_done"], 1)

                def residual(t):
                    g.tensor_tensor(xr[:, at(t * D, D)], x1s[:], boutb[:], ALU.add).then_inc(Q["xb_done"], 1)

                def norm(t):
                    pool.wait_ge(Q["rs2_done"], t + 1)
                    p2, p2r = p2_of(t)
                    p3 = p2[:].rearrange("p (h m) -> p h m", h=H)
                    r3d = rs2.rearrange("p (h a) -> p h a", a=1)
                    g.tensor_tensor(p3[:, :, 0:P], p3[:, :, 0:P], r3d.broadcast_to([P, H, P]), ALU.mult)
                    g.tensor_tensor(p2r[:], p3[:, :, P:M], r3d.broadcast_to([P, H, REM]), ALU.mult).then_inc(Q["p2_done"], 1)

                def scatter(t):
                    pool.wait_ge(Q["idx_done"], t + 1)
                    pool.wait_ge(Q["token_set"], t + 1)
                    pool.nop(nofuse=True)
                    g.indirect_dma_start(out=slots[:, :], out_offset=bass.IndirectOffsetOnAxis(ap=idx[:], axis=0),
                                         in_=rec[:], in_offset=None, bounds_check=last_row,
                                         oob_is_err=False, engine_sem=Q["idx_read"]).then_inc(Q["scattered"], 16)

                def rstd3(t):
                    pool.wait_ge(Q["v3_done"], t + 1)
                    g.tensor_tensor(r3_of(t), v3, mhalf[:, 0:1], ALU.pow).then_inc(Q["r3_done"], 1)

                def weights_lo(s):
                    for i in shares[s][0]:
                        pool.wait_ge(w_hi, i + 1)
                        g.tensor_tensor(piece(i, 1), piece(i, 2), piece(i, 0).bitcast(F32), ALU.subtract).then_inc(w_pool, 1)

                def slot(s):
                    if live(s - 1):
                        affine(s - 1)
                    if live(s - 2):
                        norm(s - 2)
                    if live(s - 1):
                        residual(s - 1)
                    if live(s - 4):
                        scatter(s - 4)
                    if live(s - 3):
                        rstd3(s - 3)

                slots_of(pool, slot)
                weights_lo(T - 1)
                affine(T - 1)
                norm(T - 2)
                residual(T - 1)
                rstd3(T - 3)
                scatter(T - 4)
                weights_lo(T)
                norm(T - 1)
                scatter(T - 3)
                weights_lo(T + 1)
                rstd3(T - 2)
                rstd3(T - 1)
                weights_lo(T + 2)
                scatter(T - 2)
                scatter(T - 1)
                pool.wait_ge(Q["scattered"], 16 * T)

            @block.vector
            def _(dve):
                v = nc.vector

                def p_lo(t):
                    for h in range(2):
                        dve.wait_ge(Q["tp_hi"], 2 * t + h + 1)
                        c = slice(h * 512, (h + 1) * 512)
                        v.tensor_tensor(PTl[:, c], bank(3 + h), PTh[:, c].bitcast(F32), ALU.subtract).then_inc(Q["tp_lo"], 1)
                    v.reciprocal(rs, ssum).then_inc(Q["rs_done"], 1)

                def p2_lo(t):
                    for g in range(3):
                        dve.wait_ge(Q["t2_hi"], 3 * t + g + 1)
                        rows, n = (P, 512) if g < 2 else (RK, 256)
                        c = slice(g * 512, g * 512 + n)
                        p2h, p2l = p2t_of(t)
                        v.tensor_tensor(p2l[0:rows, c], bank(g)[0:rows, 0:n], p2h[0:rows, c].bitcast(F32), ALU.subtract).then_inc(Q["t2_lo"], 1)

                def max2(t):
                    for g in range(3):
                        dve.wait_ge(Q["sim_mm"], 3 * t + g + 1)
                        h0, h1 = SIMG[g]
                        v.tensor_reduce(mx2[:, h0:h1], bank(5 + g)[:, 0:(h1 - h0) * M].rearrange("p (h m) -> p h m", m=M), AX,
                                        ALU.max).then_inc(Q["max2"], 1)
                        dve.wait_ge(Q["max2"], 3 * t + g + 1)
                        v.tensor_scalar(nb2[:, h0:h1], mx2[:, h0:h1], -P2SC, None, ALU.mult).then_inc(Q["nb2_done"], 1)

                def z3t_copy(t):
                    dve.wait_ge(Q["zt3_mm"], t + 1)
                    v.tensor_copy(z3T[:], bank(4)[:, 0:D]).then_inc(Q["zt3_sb"], 1)

                def x1_route1(t, r):
                    if live(t):
                        dve.wait_ge(Q["pv_mm"], t + 1)
                        dve.wait_ge(Q["rs_done"], t + 1)
                        if not known_zero(t):
                            dve.wait_ge(Q["xb_done"], t)
                        v.scalar_tensor_tensor(out=x1s[:], in0=bank(0)[:, 0:D], scalar=rs, in1=xr[:, at(t * D, D)], op0=ALU.mult,
                                               op1=ALU.add).then_inc(Q["x1_done"], 1)
                    if live(r):
                        if known_zero(r):
                            dve.wait_ge(Q["par_ld"], 80)
                        dve.wait_ge(Q["lg_mm"], r + 1)
                        v.tensor_tensor(lg, bank(4)[:, 0:E], brb[:], ALU.add).then_inc(Q["lg_done"], 1)
                    if live(t):
                        dve.wait_ge(Q["x1_done"], t + 1)
                        dve.nop(nofuse=True)
                        v.bn_stats(st1, x1s[:]).then_inc(Q["st1_done"], 1)
                    if live(r):
                        dve.wait_ge(Q["lg_done"], r + 1)
                        v.tensor_reduce(mx3, lg, AX, ALU.max).then_inc(Q["mx3_done"], 1)
                    if live(t):
                        dve.wait_ge(Q["st1_done"], t + 1)
                        dve.nop(nofuse=True)
                        v.bn_aggr(mv1, st1).then_inc(Q["mv1_done"], 1)
                    if live(r):
                        dve.wait_ge(Q["mx3_done"], r + 1)
                        v.tensor_scalar(nmx3, mx3, -1.0, None, ALU.mult).then_inc(Q["nmx3_done"], 1)
                    if live(t):
                        dve.wait_ge(Q["mv1_done"], t + 1)
                        v.tensor_scalar(v1, mv1[:, 1:2], 1.0 + EPS, EPS * EPS, ALU.mult, ALU.add).then_inc(Q["v1_done"], 1)

                def zee(t):
                    dve.wait_ge(Q["r1_done"], t + 1)
                    if not known_zero(t):
                        dve.wait_ge(Q["zt_mm"], t)
                    v.tensor_scalar(zn[:], x1s[:], mv1[:, 0:1], r1, ALU.subtract, ALU.mult).then_inc(Q["z_done"], 1)

                def recip2(t):
                    dve.wait_ge(Q["exp2"], 3 * t + 3)
                    v.reciprocal(rs2, ss2).then_inc(Q["rs2_done"], 1)

                def route2(t):
                    dve.wait_ge(Q["e8_done"], t + 1)
                    v.scalar_tensor_tensor(out=w8, in0=e8, scalar=1.0, in1=desc[:], op0=ALU.is_ge, op1=ALU.mult).then_inc(Q["w8_done"], 1)
                    dve.wait_ge(Q["rec_x"], t + 1)
                    v.tensor_copy(rec[:, REC - 1:REC].bitcast(I32), tokens[:, at(t, 1)]).then_inc(Q["token_set"], 1)
                    gt = rec[:, D + 2:D + 3]
                    v.reciprocal(gt, se).then_inc(Q["gate_done"], 1)
                    dve.wait_ge(Q["w8_done"], t + 1)
                    v.tensor_reduce(wm, w8, AX, ALU.max).then_inc(Q["wm_done"], 1)
                    dve.wait_ge(Q["wm_done"], t + 1)
                    v.tensor_scalar(oh[:], w8, wm, None, ALU.is_equal).then_inc(Q["oh_done"], 1)
                    dve.wait_ge(Q["gate_done"], t + 1)
                    v.tensor_tensor(rec[:, D + 1:D + 2], r3_of(t), gt, ALU.mult).then_inc(Q["rg_done"], 1)

                def smax(t):
                    dve.wait_ge(Q["s_mm"], t + 1)
                    v.tensor_reduce(mx, BIG[:, 512:1536], AX, ALU.max).then_inc(Q["s_max"], 1)
                    dve.wait_ge(Q["s_max"], t + 1)
                    ut = u[:, at(t, 1)]
                    v.tensor_tensor(sh, mx, ut, ALU.add).then_inc(Q["s_sh"], 1)
                    dve.wait_ge(Q["s_sh"], t + 1)
                    v.tensor_scalar(nb, sh, ut, -PSC, ALU.subtract, ALU.mult).then_inc(Q["s_nb"], 1)

                def place(t):
                    dve.wait_ge(Q["cnt_mm"], t + 1)
                    cnt = bank(7)[:, 0:E]
                    v.tensor_scalar(far, cnt, float(CAP), FAR, ALU.is_ge, ALU.mult).then_inc(Q["far_done"], 1)
                    v.tensor_tensor(pb, cnt, base[:], ALU.add).then_inc(Q["pb_done"], 1)
                    v.tensor_tensor(racc[:], racc[:], oh[:], ALU.add).then_inc(Q["racc_done"], 1)
                    dve.wait_ge(Q["far_done"], t + 1)
                    dve.wait_ge(Q["pb_done"], t + 1)
                    v.tensor_tensor(far, far, pb, ALU.add).then_inc(Q["q1_done"], 1)
                    dve.wait_ge(Q["q1_done"], t + 1)
                    v.tensor_tensor(far, far, oh[:], ALU.mult).then_inc(Q["q2_done"], 1)
                    dve.wait_ge(Q["q2_done"], t + 1)
                    v.tensor_reduce(slot_at, far, AX, ALU.add).then_inc(Q["slot_done"], 1)
                    dve.wait_ge(Q["slot_done"], t + 1)
                    dve.wait_ge(Q["rg_done"], t + 1)
                    dve.wait_ge(Q["racc_done"], t + 1)
                    if not known_zero(t):
                        dve.wait_ge(Q["idx_read"], t)
                    v.tensor_copy(idx[:], slot_at).then_inc(Q["idx_done"], 1)

                def xn_lo(t):
                    dve.wait_ge(Q["xn_hi"], t + 1)
                    v.tensor_tensor(xnTl[:], bank(5)[:, 0:D], xnTh[:].bitcast(F32), ALU.subtract).then_inc(Q["xn_lo"], 1)

                def x2(t):
                    dve.wait_ge(Q["out_mm"], t + 1)
                    dve.wait_ge(Q["xb_done"], t + 1)
                    if not known_zero(t):
                        dve.wait_ge(Q["rec_x"], t)
                        dve.wait_ge(Q["z3_done"], t)
                    v.tensor_tensor(x2s[:, 0:D], out_bank(t)[:, 0:D], xr[:, at(t * D, D)], ALU.add).then_inc(Q["x2_done"], 1)
                    dve.wait_ge(Q["x2_done"], t + 1)
                    dve.nop(nofuse=True)
                    v.bn_stats(st3, x2s[:, 0:D]).then_inc(Q["st3_done"], 1)
                    dve.wait_ge(Q["st3_done"], t + 1)
                    dve.nop(nofuse=True)
                    v.bn_aggr(x2s[:, D:D + 2], st3).then_inc(Q["mv3_done"], 1)
                    dve.wait_ge(Q["mv3_done"], t + 1)
                    v.tensor_scalar(v3, x2s[:, D + 1:D + 2], EPS, None, ALU.add).then_inc(Q["v3_done"], 1)

                def g_lo(t):
                    dve.wait_ge(Q["g_hi"], t + 1)
                    for k in range(KB):
                        last = v.scalar_tensor_tensor(out=GTl[:, k, :], in0=bank(4)[:, k * P:(k + 1) * P], scalar=cb[:, k:k + 1],
                                                      in1=GTh[:, k, :].bitcast(F32), op0=ALU.add, op1=ALU.subtract)
                    last.then_inc(Q["g_lo"], 1)

                def zee3(t):
                    dve.wait_ge(Q["r3_done"], t + 1)
                    v.tensor_scalar(z3[:], x2s[:, 0:D], x2s[:, D:D + 1], r3_of(t), ALU.subtract, ALU.mult).then_inc(Q["z3_done"], 1)

                def weights_lo(s):
                    for i in shares[s][1]:
                        dve.wait_ge(w_hi, i + 1)
                        v.tensor_tensor(piece(i, 1), piece(i, 2), piece(i, 0).bitcast(F32), ALU.subtract)

                def slot(s):
                    if live(s - 3):
                        p2_lo(s - 3)
                    if live(s - 1):
                        p_lo(s - 1)
                    if live(s - 2):
                        max2(s - 2)
                    if live(s - 4):
                        z3t_copy(s - 4)
                    x1_route1(s - 1, s - 4)
                    if live(s - 2):
                        recip2(s - 2)
                    if live(s - 1):
                        zee(s - 1)
                    if live(s - 4):
                        route2(s - 4)
                    smax(s)
                    if live(s - 4):
                        place(s - 4)
                    if live(s - 1):
                        xn_lo(s - 1)
                    if live(s + 1):
                        g_lo(s + 1)
                    if live(s - 3):
                        x2(s - 3)
                        zee3(s - 3)

                dve.wait_ge(Q["const_c"], 4)
                g_lo(0)
                slots_of(dve, slot)
                p_lo(T - 1)
                p2_lo(T - 3)
                max2(T - 2)
                z3t_copy(T - 4)
                x1_route1(T - 1, T - 4)
                recip2(T - 2)
                zee(T - 1)
                route2(T - 4)
                x2(T - 3)
                xn_lo(T - 1)
                zee3(T - 3)
                place(T - 4)
                weights_lo(T)
                max2(T - 1)
                z3t_copy(T - 3)
                x1_route1(T, T - 3)
                recip2(T - 1)
                p2_lo(T - 2)
                route2(T - 3)
                place(T - 3)
                weights_lo(T + 1)
                p2_lo(T - 1)
                x2(T - 2)
                zee3(T - 2)
                weights_lo(T + 2)
                x2(T - 1)
                z3t_copy(T - 2)
                zee3(T - 1)
                x1_route1(T, T - 2)
                route2(T - 2)
                place(T - 2)
                z3t_copy(T - 1)
                x1_route1(T, T - 1)
                route2(T - 1)
                place(T - 1)

        with ExitStack() as ph:
            things = [("b2r", [P, E * D], F32), ("b1c", [P, E * KB], F32), ("b1rows", [E * KB, P], F32)]
            for j in range(2):
                things += [(f"xg{j}", [P, 2, D], F32), (f"dTh{j}", [P, KB, CAP], F32R), (f"dTl{j}", [P, KB, CAP], F32R),
                           (f"hf{j}", [P, KB, CAP], F32), (f"hTh{j}", [P, KB, CAP], F32R), (f"hTl{j}", [P, KB, CAP], F32R),
                           (f"res{j}", [P, 2, D], F32)]
            (b2r, b1c, b1rows, *by_parity), _ = lay(TEMP, things)
            xg, dTh, dTl, hf, hTh, hTl, res = zip(by_parity[:7], by_parity[7:])
            rec = []
            for half in range(2):
                made, _ = lay(VW_AT + 4 * D * NBLK * (2 * half + 1), [(f"rec{e}", [P, 2, REC], F32) for e in range(4 * half, 4 * half + 4)])
                rec += made
            b1_ld = sem(ph, "b1_ld")
            b2_ld = sem(ph, "b2_ld")
            rec_ld = [sem(ph, f"rec_ld{e}") for e in range(E)]
            token_out = [sem(ph, f"token_out{j}") for j in range(2)]
            names = "b1_mm b1_done xg_done xt_mm dt_hi dt_lo h_mm hf_done ht_hi ht_lo o_mm t_done res_done".split()
            R = {n: sem(ph, "e_" + n) for n in names}
            block = ph.enter_context(nc.Block())

            def steps(slot):
                for s in range(E + 2):
                    slot(s)

            def here(e):
                return 0 <= e < E

            def w_of(n, e):
                return [W[n, part, e // (E // 2)][:, e % (E // 2), :] for part in range(2)]

            @block.sync
            def _(sp):
                sp.dma_start(b1rows[:], fb1.rearrange("e (k p) -> (e k) p", p=P)).then_inc(b1_ld, 16)
                for e in range(0, E, 2):
                    sp.dma_start(rec[e][:], slots[e * CAP:(e + 1) * CAP, :].rearrange("(i p) c -> p i c", p=P)).then_inc(rec_ld[e], 16)
                sp.dma_start(b2r[:], fb2.rearrange("(a e) d -> a (e d)", a=1).broadcast_to([P, E * D])).then_inc(b2_ld, 16)

            @block.tensor
            def _(pe):
                def product(o, a, b, first, last):
                    nc.tensor.matmul(o, a[0], b[0], start=first, stop=False)
                    nc.tensor.matmul(o, a[0], b[1], start=False, stop=False)
                    return nc.tensor.matmul(o, a[1], b[0], start=False, stop=last)

                pe.wait_ge(b1_ld, 16)
                nc.tensor.transpose(ps[:, 6, 0:E * KB], b1rows[:], ident[0:E * KB, 0:E * KB]).then_inc(R["b1_mm"], 1)

                def first(e):
                    j = e % 2
                    wh, wl = w_of(0, e)
                    pe.wait_ge(R["dt_lo"], e + 1)
                    if e >= 2:
                        pe.wait_ge(R["hf_done"], e - 1)
                    for f in range(KB):
                        for k in range(KB):
                            c = slice(k * D + f * P, k * D + (f + 1) * P)
                            last = product(ps[:, 2 + j, f * CAP:(f + 1) * CAP], (wh[:, c], wl[:, c]),
                                           (dTh[j][:, k, :], dTl[j][:, k, :]), k == 0, k == KB - 1)
                    last.then_inc(R["h_mm"], 1)

                def turn(e):
                    j = e % 2
                    pe.wait_ge(R["xg_done"], 2 * e + 2)
                    if e >= 2:
                        pe.wait_ge(R["dt_lo"], e - 1)
                    for k in range(KB):
                        for i in range(2):
                            o = k * CAP + i * P
                            last = nc.tensor.transpose(ps[:, j, o:o + P], xg[j][:, i, k * P:(k + 1) * P], ident[:])
                    last.then_inc(R["xt_mm"], 1)

                def second(e):
                    j = e % 2
                    wh, wl = w_of(1, e)
                    pe.wait_ge(R["ht_lo"], e + 1)
                    if e >= 2:
                        pe.wait_ge(R["t_done"], 2 * e - 2)
                    for i in range(2):
                        for f in range(KB):
                            c, w = slice(i * P, (i + 1) * P), slice(f * D, (f + 1) * D)
                            last = product(ps[:, 4 + j, i * D:(i + 1) * D], (hTh[j][:, f, c], hTl[j][:, f, c]), (wh[:, w], wl[:, w]),
                                           f == 0, f == KB - 1)
                    last.then_inc(R["o_mm"], 1)

                def slot(s):
                    if here(s - 1):
                        first(s - 1)
                    if here(s):
                        turn(s)
                    if here(s - 2):
                        second(s - 2)

                steps(slot)

            @block.scalar
            def _(act):
                a = nc.scalar.activation
                for e in range(1, E, 2):
                    act.dma_start(rec[e][:], slots[e * CAP:(e + 1) * CAP, :].rearrange("(i p) c -> p i c", p=P)).then_inc(rec_ld[e], 16)
                act.wait_ge(R["b1_mm"], 1)
                a(b1c[:], ps[:, 6, 0:E * KB], ACT.Copy).then_inc(R["b1_done"], 1)
                act.wait_ge(R["b1_done"], 1)

                def slot(s):
                    if here(s - 1):
                        e, j = s - 1, (s - 1) % 2
                        act.wait_ge(R["h_mm"], e + 1)
                        for f in range(KB):
                            last = a(hf[j][:, f, :], ps[:, 2 + j, f * CAP:(f + 1) * CAP], ACT.Relu,
                                     bias=b1c[:, e * KB + f:e * KB + f + 1], scale=1.0)
                        last.then_inc(R["hf_done"], 1)
                    if here(s):
                        j = s % 2
                        act.wait_ge(R["xt_mm"], s + 1)
                        a(dTh[j][:], ps[:, j, :].rearrange("p (k c) -> p k c", k=KB), ACT.Copy).then_inc(R["dt_hi"], 1)
                    if here(s - 1):
                        act.wait_ge(R["hf_done"], s)
                        j = (s - 1) % 2
                        a(hTh[j][:], hf[j][:], ACT.Copy).then_inc(R["ht_hi"], 1)

                steps(slot)

            @block.vector
            def _(dve):
                v = nc.vector

                def gated(e):
                    j = e % 2
                    dve.wait_ge(rec_ld[e], 16)
                    if e >= 2:
                        dve.wait_ge(R["xt_mm"], e - 1)
                    for i in range(2):
                        r = rec[e][:, i, :]
                        v.tensor_scalar(xg[j][:, i, :], r[:, 0:D], r[:, D:D + 1], r[:, D + 1:D + 2], ALU.subtract, ALU.mult).then_inc(R["xg_done"], 1)

                def slot(s):
                    if here(s):
                        j = s % 2
                        dve.wait_ge(R["dt_hi"], s + 1)
                        v.tensor_tensor(dTl[j][:], ps[:, j, :].rearrange("p (k c) -> p k c", k=KB), dTh[j][:].bitcast(F32),
                                        ALU.subtract).then_inc(R["dt_lo"], 1)
                    if here(s + 1):
                        gated(s + 1)
                    if here(s - 1):
                        j = (s - 1) % 2
                        dve.wait_ge(R["ht_hi"], s)
                        v.tensor_tensor(hTl[j][:], hf[j][:], hTh[j][:].bitcast(F32), ALU.subtract).then_inc(R["ht_lo"], 1)
                    if here(s - 2):
                        e, j = s - 2, s % 2
                        if e == 0:
                            dve.wait_ge(b2_ld, 16)
                        if e >= 2:
                            dve.wait_ge(token_out[j], 32 * (e // 2))
                        dve.wait_ge(R["o_mm"], e + 1)
                        for i in range(2):
                            v.tensor_tensor(res[j][:, i, :], ps[:, 4 + j, i * D:(i + 1) * D], b2r[:, e * D:(e + 1) * D], ALU.add).then_inc(R["t_done"], 1)
                        for i in range(2):
                            r = rec[e][:, i, :]
                            dve.wait_ge(R["t_done"], 2 * e + i + 1)
                            v.scalar_tensor_tensor(out=res[j][:, i, :], in0=res[j][:, i, :], scalar=r[:, D + 2:D + 3], in1=r[:, 0:D],
                                                   op0=ALU.mult, op1=ALU.add).then_inc(R["res_done"], 1)

                gated(0)
                steps(slot)

            @block.gpsimd
            def _(pool):
                g = nc.gpsimd
                last_row = pool.to_reg(N - 1)
                for e in range(E):
                    for i in range(2):
                        pool.wait_ge(R["res_done"], 2 * e + i + 1)
                        tok = rec[e][:].bitcast(I32)[:, i, REC - 1:REC]
                        g.indirect_dma_start(out=OUT, out_offset=bass.IndirectOffsetOnAxis(ap=tok, axis=0),
                                             in_=res[e % 2][:, i, :], in_offset=None, bounds_check=last_row,
                                             oob_is_err=False).then_inc(token_out[e % 2], 16)
                for j in range(2):
                    pool.wait_ge(token_out[j], 16 * E)


_INS = ["x", "ctx_1024", "L0_attn_Wq", "L0_attn_bq", "L0_attn_Wk", "L0_attn_bk", "L0_attn_Wv", "L0_attn_bv", "L0_xattn_g1",
        "L0_xattn_b1", "L0_xattn_g2", "L0_xattn_b2", "L0_xattn_Wq", "L0_xattn_Wkv", "L0_xattn_Wout", "L0_xattn_bout",
        "L0_ffn_Wr", "L0_ffn_br", "L0_ffn_W1", "L0_ffn_b1", "L0_ffn_W2", "L0_ffn_b2"]


def kernel(**inputs):
    import numpy as np
    import concourse.bacc as bacc
    from concourse.bass_utils import run_bass_kernel_spmd as run

    nc = bacc.Bacc("TRN2", target_bir_lowering=False, num_devices=1)
    arrays, args = {}, []
    for name in _INS:
        a = np.ascontiguousarray(inputs[name])
        arrays[f"in_{name}"] = a
        args.append(nc.dram_tensor(f"in_{name}", a.shape, mybir.dt.from_np(a.dtype), kind="ExternalInput").ap())
    args.append(nc.dram_tensor("out_rows", (B, S, D), F32, kind="ExternalOutput").ap())
    build(nc, *args)
    r = run(nc, [arrays], core_ids=[0])
    return r.results[0]["out_rows"]
```

```python
from contextlib import ExitStack

import concourse.bass as bass
from concourse import mybir

ALU = mybir.AluOpType
ACT = mybir.ActivationFunctionType
AX = mybir.AxisListType.X
F32 = mybir.dt.float32
F32R = mybir.dt.float32r
BF16 = mybir.dt.bfloat16
I32 = mybir.dt.int32

P = 128
B, S, D = 2, 1024, 256
M = 154
CT = 77
H, DH = 8, 64
E = 8
KB = D // P
TB = S // P
T = B * TB
N = B * S
CAP = N // E
REM = M - P
HG = 4
RK = HG * REM
NBLK = H + H // HG
HM = H * M
REC = D + 4
EPS = 1e-5
FAR = 4096.0
SIMG = [(0, 3), (3, 6), (6, 8)]
SLAB = 212800
OUT_SPLIT = 6


def at(off, n):
    return slice(off, off + n) if isinstance(off, int) else bass.ds(off, n)


def batch_of(t):
    return t // TB if isinstance(t, int) else (t >> 3).with_bounds(min_val=0, max_val=B - 1)


def known_zero(t):
    return isinstance(t, int) and t == 0


def build(nc, x, ctx_in, Wq, bq, Wk, bk, Wv, bv, g1, b1, g2, b2, WqX, Wkv, Wout, bout, Wr, br, W1, fb1, W2, fb2, out):
    X = x.rearrange("b (t p) d -> p (b t) d", p=P)
    OUT = out.rearrange("b s d -> (b s) d")
    slots = nc.dram_tensor("slots", [N, REC], F32)

    def row(v):
        return v.rearrange("(a n) -> a n", a=1)

    sizes = {F32: 4, F32R: 4, I32: 4, BF16: 2}

    with ExitStack() as whole:
        def sem(ctx, name):
            return ctx.enter_context(nc.semaphore(name))

        slab = whole.enter_context(nc.sbuf_tensor("slab", [P, SLAB], mybir.dt.uint8))
        origin = nc.sbuf_base - SLAB

        def lay(start, things):
            made = []
            for name, shape, dt in things:
                n = sizes[dt]
                for k in shape[1:]:
                    n *= k
                start = (start + 31) // 32 * 32
                made.append(nc.alloc_sbuf_tensor_at(name, shape, dt, offset=origin + start))
                start += n
            assert start <= SLAB, (start, SLAB)
            return made, start

        ps = whole.enter_context(nc.psum_tensor("ps", [P, 8, 512], F32))
        (ident, tri, ones, mhalf, tokens, cb, u, Ah, Al), end = lay(0, [
            ("ident", [P, P], F32), ("tri", [P, P], BF16), ("ones", [P, P], BF16), ("mhalf", [P, 4], F32),
            ("tokens", [P, T], I32),
            ("cb", [P, KB], F32),
            ("u", [P, T], F32),
            ("Ah", [P, KB, D], F32R), ("Al", [P, KB, D], F32R)])

        KW_AT = end = (end + 31) // 32 * 32
        (KWh, KWl), end = lay(end, [(f"KW{s}", [P, B * KB * HM], F32R) for s in "hl"])
        VW_AT = end
        (VWh, VWl), end = lay(end, [(f"VW{s}", [P, B * NBLK * D], F32R) for s in "hl"])
        XR_AT = end
        (xr,), end = lay(end, [("xr", [P, T * D], F32)])
        XT_AT = end
        (xhTh, xhTl), end = lay(end, [(f"xhT{s}", [P, B * KB * S], F32R) for s in "hl"])
        V_AT = end
        (Vh, Vl), end = lay(end, [(f"V{s}", [P, T * D], F32R) for s in "hl"])
        V_END = end
        (GTh, GTl), TEMP = lay(end, [("GTh", [P, KB, 2 * P], F32R), ("GTl", [P, KB, 2 * P], F32R)])
        xr3 = xr[:].rearrange("p (t c) -> p t c", c=D)
        ROW = 4 * D

        slots_set = sem(whole, "slots_set")
        b1_ld = sem(whole, "b1_ld")
        b2_ld = sem(whole, "b2_ld")

        def keep_warm(n, bank):
            for _ in range(n):
                nc.tensor.matmul(ps[:, bank, 0:P], ones[:], ones[:], start=True, stop=True)

        def project_xh(bank, tokens_at):
            for k in range(KB):
                for d in range(KB):
                    a, o = slice(k * P, (k + 1) * P), tokens_at(d)
                    for n, (w, x_) in enumerate(((Ah, xhTh), (Ah, xhTl), (Al, xhTh))):
                        last = nc.tensor.matmul(ps[:, bank, k * 2 * P:(k + 1) * 2 * P], w[:, d, a], x_[:, o], start=d == n == 0,
                                                stop=d == KB - 1 and n == 2)
            return last

        def high_g(bank, k):
            return nc.scalar.activation(GTh[:, k, :], ps[:, bank, k * 2 * P:(k + 1) * 2 * P], ACT.Identity, bias=cb[:, k:k + 1], scale=1.0)

        def low_g(bank, k):
            return nc.vector.scalar_tensor_tensor(out=GTl[:, k, :], in0=ps[:, bank, k * 2 * P:(k + 1) * 2 * P], scalar=cb[:, k:k + 1],
                                                  in1=GTh[:, k, :].bitcast(F32), op0=ALU.add, op1=ALU.subtract)

        (ctx_n, cnf, cnTh, cnTl, wkv, wkvh, wkvl), end = lay(KW_AT, [
            ("ctx_n", [CT, 4, D], F32), ("cnf", [P, KB, B * M], F32), ("cnTh", [P, KB, B * M], F32R), ("cnTl", [P, KB, B * M], F32R),
            ("wkv", [P, KB, 2 * H * DH], F32), ("wkvh", [P, KB, 2 * H * DH], F32R), ("wkvl", [P, KB, 2 * H * DH], F32R)])
        assert end <= VW_AT
        (wqx, wqTh, wqTl, wo, bqb, bkb, wqbk, prod, kTh, kTl), end = lay(VW_AT, [
            ("wqx", [P, KB, H * DH], F32), ("wqTh", [P, 4, D], F32R), ("wqTl", [P, 4, D], F32R), ("wo", [P, 4, D], F32),
            ("bqb", [P, D], F32), ("bkb", [P, D], F32), ("wqbk", [P, KB], F32), ("prod", [P, 5, D], F32),
            ("kTh", [P, 4, B * M], F32R), ("kTl", [P, 4, B * M], F32R)])
        assert end <= XR_AT
        (wv,), end = lay(V_AT + 14 * ROW, [("wv", [P, KB, D], F32)])
        assert end <= V_AT + T * ROW
        (wqr, wkr, aqh, akh, aql, akl), end = lay(V_AT + (T + 4) * ROW, [
            ("wqr", [P, KB, D], F32), ("wkr", [P, KB, D], F32), ("aqTh", [P, KB, D], F32R), ("akTh", [P, KB, D], F32R),
            ("aqTl", [P, KB, D], F32R), ("akTl", [P, KB, D], F32R)])
        assert end <= V_END
        (vTh, vTl, vremh, vreml, woh, wol, wvh, wvl, xh, bvb, init, g2c, cst, cmv, crs, xst, xmv, xnm, xrs, qk), _ = lay(TEMP, [
            ("vTh", [P, 4, B * M], F32R), ("vTl", [P, 4, B * M], F32R),
            ("vremh", [P, B, 4, RK], F32R), ("vreml", [P, B, 4, RK], F32R),
            ("woh", [P, 4, D], F32R), ("wol", [P, 4, D], F32R),
            ("wvh", [P, KB, D + 2], F32R), ("wvl", [P, KB, D + 2], F32R),
            ("xh", [P, 2, D], F32), ("bvb", [P, D], F32), ("init", [P, REC], F32), ("g2c", [P, 2 * KB], F32),
            ("cst", [CT, 4, 6], F32), ("cmv", [CT, 4, 2], F32), ("crs", [CT, 4], F32),
            ("xst", [P, T, 6], F32), ("xmv", [P, T, 2], F32), ("xnm", [P, T], F32), ("xrs", [P, T], F32), ("qk", [P, 1], F32)])

        with ExitStack() as ph:
            names = ("wq_ld wk_ld bias_ld wv_ld ctx_ld g2_ld wqx_ld wk2_ld wv2_ld wo_ld bv_ld "
                     "zero_done iota_done ident_set ident_done init_done rem_zero cstat cvar crstd cz split_hi split_done "
                     "dots_done wcol_hi wcol_lo unit_mm unit_hi unit_lo cn_aff xstat xvar xrstd xh_done xt_mm xt_hi xt_lo "
                     "v_mm v_hi v_lo rem_done bv_done").split()
            Q = {n: sem(ph, "a_" + n) for n in names}
            x_in = [sem(ph, f"x_in{c}") for c in range(4)]

            units = [("at", 0), ("at", 1), ("am", 0), ("am", 1), ("cn", 0), ("cn", 1), ("wq", 0), ("wq", 1)]
            first_units = units[:]
            units += [("kv", j) for j in range(8)]
            units += [("kw", k, h) for h in range(H) for k in range(KB)]
            units += [("vw", b, j) for b in range(B) for j in range(4)] + [("vr", b) for b in range(B)]
            units.insert(-3, ("g", 0))
            number = {q: i for i, q in enumerate(units)}
            tiles = []
            for t in range(2, T + 1):
                tiles += [("V", t - 2)] + [("T", t)] * (t < T)
            tiles.append(("V", T - 1))
            items = first_units[:4] + [("T", 0)] + first_units[4:6] + [("T", 1)] + first_units[6:]
            rest = units[len(first_units):]
            items, rest = items + rest[:1], rest[1:]
            while tiles or rest:
                items += rest[:1] + tiles[:1]
                tiles, rest = tiles[1:], rest[1:]
            WARM = {("am", 0): 14, ("kv", 0): 18}
            VWG = [(0, 2), (1, 3), (4, 6), (5, 7)]

            def pieces(q):
                bank = ps[:, 4 + number[q] % 4, :]
                kind, j = q[0], q[1]
                if kind == "at":
                    return bank.rearrange("p (e d) -> p e d", e=KB), (aqh, akh)[j][:], (aql, akl)[j][:]
                if kind == "wq":
                    return bank.rearrange("p (j d) -> p j d", j=2), wqTh[:, 2 * j:2 * j + 2, :], wqTl[:, 2 * j:2 * j + 2, :]
                if kind == "am":
                    return bank[:, 0:D], Ah[:, j, :], Al[:, j, :]
                if kind == "cn":
                    return cnf[:, j, :], cnTh[:, j, :], cnTl[:, j, :]
                if kind == "kv":
                    hi, lo = (kTh, kTl) if j < 4 else (vTh, vTl)
                    return bank[:, 0:B * M], hi[:, j % 4, :], lo[:, j % 4, :]
                if kind == "kw":
                    _, k, h = q
                    hi, lo = (w[:].rearrange("p (b k h m) -> p b k h m", b=B, k=KB, h=H)[:, :, k, h, :] for w in (KWh, KWl))
                    return bank[:, 0:B * M].rearrange("p (b m) -> p b m", b=B), hi, lo
                if kind == "vw":
                    o = q[1] * NBLK + VWG[q[2]][0]
                    hi, lo = (w[:].rearrange("p (n d) -> p n d", d=D)[:, o:o + 3:2, :] for w in (VWh, VWl))
                    return bank.rearrange("p (n d) -> p n d", n=2), hi, lo
                o = (j * NBLK + H) * D
                return bank[0:RK, :], VWh[0:RK, o:o + 2 * D], VWl[0:RK, o:o + 2 * D]

            keys, values = slice(0, H * DH), slice(H * DH, 2 * H * DH)
            splits = [("wv_ld", wvh[:, :, 0:D], wv[:], wvl[:, :, 0:D]), ("wk2_ld", wkvh[:, :, keys], wkv[:, :, keys], wkvl[:, :, keys]),
                      ("wv2_ld", wkvh[:, :, values], wkv[:, :, values], wkvl[:, :, values]), ("wo_ld", woh[:], wo[:], wol[:])]

            block = ph.enter_context(nc.Block())

            @block.sync
            def _(sp):
                wkv_in = Wkv.rearrange("(k p) e -> p k e", p=P)
                sp.dma_start(ctx_n[:], ctx_in.rearrange("b (a p) d -> p (b a) d", p=CT)).then_inc(Q["ctx_ld"], 16)
                sp.dma_start(xr3[:, 0:4, :], X[:, 0:4, :]).then_inc(x_in[0], 16)
                sp.dma_start(wqr[:], Wq.rearrange("(k p) e -> p k e", p=P)).then_inc(Q["wq_ld"], 16)
                sp.dma_start(wkr[:], Wk.rearrange("(k p) e -> p k e", p=P)).then_inc(Q["wk_ld"], 16)
                sp.dma_start(bqb[:], row(bq).broadcast_to([P, D])).then_inc(Q["bias_ld"], 16)
                sp.dma_start(bkb[:], row(bk).broadcast_to([P, D])).then_inc(Q["bias_ld"], 16)
                sp.dma_start(wv[:], Wv.rearrange("(k p) e -> p k e", p=P)).then_inc(Q["wv_ld"], 16)
                sp.dma_start(g2c[:, 0:KB], g2.rearrange("(k p) -> p k", p=P), allow_slow_non_contiguous=True).then_inc(Q["g2_ld"], 16)
                sp.dma_start(g2c[:, KB:2 * KB], b2.rearrange("(k p) -> p k", p=P), allow_slow_non_contiguous=True).then_inc(Q["g2_ld"], 16)
                sp.dma_start(wkv[:, :, keys], wkv_in[:, :, keys]).then_inc(Q["wk2_ld"], 16)
                sp.dma_start(wqx[:], WqX.rearrange("(k p) e -> p k e", p=P)).then_inc(Q["wqx_ld"], 16)
                sp.dma_start(wkv[:, :, values], wkv_in[:, :, values]).then_inc(Q["wv2_ld"], 16)
                sp.dma_start(xr3[:, 4:8, :], X[:, 4:8, :]).then_inc(x_in[1], 16)
                sp.dma_start(wo[:], Wout.rearrange("(j p) d -> p j d", p=P)).then_inc(Q["wo_ld"], 16)
                for c in range(2, 4):
                    sp.dma_start(xr3[:, 4 * c:4 * c + 4, :], X[:, 4 * c:4 * c + 4, :]).then_inc(x_in[c], 16)
                sp.dma_start(bvb[:], row(bv).broadcast_to([P, D])).then_inc(Q["bv_ld"], 16)
                sp.wait_ge(Q["init_done"], 2)
                for k in range(N // P):
                    sp.dma_start(slots[k * P:(k + 1) * P, :], init[:]).then_inc(slots_set, 16)
                sp.wait_ge(slots_set, 16 * (N // P))

            @block.gpsimd
            def _(pool):
                g = nc.gpsimd
                g.memset(mhalf[:], -0.5).then_inc(Q["ident_set"], 1)
                g.memset(ident[:], 0.0).then_inc(Q["ident_set"], 1)
                g.memset(ones[:], 1.0).then_inc(Q["ident_set"], 1)
                pool.wait_ge(Q["ident_set"], 3)
                g.affine_select(out=ident[:], in_=ident[:], compare_op=ALU.not_equal, fill=1.0, base=0,
                                pattern=[[-1, P]], channel_multiplier=1).then_inc(Q["ident_done"], 1)
                g.affine_select(out=tri[:], in_=ones[:], compare_op=ALU.is_ge, fill=0.0, base=0,
                                pattern=[[1, P]], channel_multiplier=-1).then_inc(Q["ident_done"], 1)
                pool.wait_ge(Q["cvar"], 1)
                pool.wait_ge(Q["ident_done"], 2)
                g.tensor_tensor(crs[:], cmv[:, :, 1], mhalf[0:CT, 0:4], ALU.pow).then_inc(Q["crstd"], 1)
                pool.wait_ge(Q["crstd"], 1)

                def rstd(c):
                    pool.wait_ge(Q["xvar"], 2 * c + 2)
                    g.tensor_tensor(xrs[:, 4 * c:4 * c + 4], xmv[:, 4 * c:4 * c + 4, 1], mhalf[:], ALU.pow).then_inc(Q["xrstd"], 1)
                    pool.wait_ge(Q["xrstd"], c + 1)

                def split_lo(n):
                    hi, raw, lo = splits[n][1:]
                    pool.wait_ge(Q["split_hi"], n + 1)
                    g.tensor_tensor(lo, raw, hi.bitcast(F32), ALU.subtract).then_inc(Q["split_done"], 1)

                def values_of_rest():
                    pool.wait_ge(Q["rem_zero"], 2)
                    pool.wait_ge(Q["unit_lo"], number[("kv", 7)] + 1)
                    made = 0
                    for src, dst in ((vTh, vremh), (vTl, vreml)):
                        for h in range(HG):
                            r, c = slice(64 * (h % 2), 64 * (h % 2) + 64), REM * h
                            g.tensor_copy(dst[r, :, h // 2:4:2, c:c + REM],
                                          src[r, h // 2:4:2, :].rearrange("p j (b m) -> p b j m", b=B)[:, :, :, P:M].bitcast(F32)).then_inc(Q["rem_done"], 1)
                            made += 1
                            pool.wait_ge(Q["rem_done"], made)

                def add_bv(c):
                    if c == 0:
                        pool.wait_ge(Q["bv_ld"], 16)
                    pool.wait_ge(Q["xh_done"], 4 * c + 4)
                    xc = xr3[:, 4 * c:4 * c + 4, :]
                    g.tensor_tensor(xc, xc, bvb[:].rearrange("p (a d) -> p a d", a=1).broadcast_to([P, 4, D]), ALU.add).then_inc(Q["bv_done"], 1)

                for t in range(T):
                    if t % 4 == 0:
                        rstd(t // 4)
                    if t == 2:
                        split_lo(0)
                        split_lo(1)
                    if t == 3:
                        split_lo(2)
                    if t == 4:
                        for z in (vremh, vreml):
                            g.memset(z[:].bitcast(F32), 0.0).then_inc(Q["rem_zero"], 1)
                    if t == 5:
                        split_lo(3)
                        g.memset(init[:], 0.0).then_inc(Q["init_done"], 1)
                        pool.wait_ge(Q["init_done"], 1)
                        g.iota(init[:, REC - 1:REC].bitcast(I32), pattern=[[0, 1]], base=int(FAR), channel_multiplier=0).then_inc(Q["init_done"], 1)
                        g.iota(tokens[:], pattern=[[P, T]], base=0, channel_multiplier=1).then_inc(Q["iota_done"], 1)
                    if t in (7, 10, 13):
                        add_bv((t - 7) // 3)
                    if t >= 2:
                        pool.wait_ge(Q["xt_mm"], t - 1)
                    g.tensor_scalar(xh[:, t % 2, :], xr3[:, t, :], xnm[:, t:t + 1], xrs[:, t:t + 1], ALU.add, ALU.mult).then_inc(Q["xh_done"], 1)
                pool.wait_ge(Q["xh_done"], T)
                values_of_rest()
                add_bv(3)

            @block.scalar
            def _(act):
                a = nc.scalar.activation
                def split_high(n):
                    ld, hi, raw = splits[n][:3]
                    act.wait_ge(Q[ld], 16)
                    a(hi, raw, ACT.Copy).then_inc(Q["split_hi"], 1)

                for q in items:
                    kind, t = q[0], q[1]
                    if q == ("am", 0):
                        split_high(0)
                    if q == ("cn", 0):
                        split_high(1)
                    if q == ("kv", 0):
                        split_high(2)
                        act.wait_ge(Q["dots_done"], 5)
                        for k in range(KB):
                            a(wvh[:, k, D:D + 2], wqbk[:, k:k + 1].broadcast_to([P, 2]), ACT.Copy).then_inc(Q["wcol_hi"], 1)
                    if q == ("T", 3):
                        split_high(3)
                    if kind == "T":
                        act.wait_ge(Q["xt_mm"], t + 1)
                        b, o = t // TB, (t % TB) * P
                        dst = xhTh[:].rearrange("p (b k n) -> p b k n", b=B, k=KB)[:, b, :, o:o + P]
                        a(dst, ps[:, t % 2, 0:D].rearrange("p (k n) -> p k n", k=KB), ACT.Copy).then_inc(Q["xt_hi"], 1)
                    elif kind == "V":
                        act.wait_ge(Q["v_mm"], t + 1)
                        a(Vh[:, t * D:(t + 1) * D], ps[:, 2 + t % 2, 0:D], ACT.Copy).then_inc(Q["v_hi"], 1)
                    else:
                        act.wait_ge(Q["unit_mm"], number[q] + 1)
                        if kind == "cn":
                            act.wait_ge(Q["g2_ld"], 32)
                            a(cnf[:, t, :], ps[:, 4 + number[q] % 4, 0:B * M], ACT.Identity, bias=g2c[:, KB + t:KB + t + 1],
                              scale=g2c[:, t:t + 1]).then_inc(Q["cn_aff"], 1)
                            act.wait_ge(Q["cn_aff"], t + 1)
                        if kind == "g":
                            for k in range(KB):
                                last = high_g(4 + number[q] % 4, k)
                            last.then_inc(Q["unit_hi"], 1)
                            continue
                        src, hi, lo = pieces(q)
                        a(hi, src, ACT.Copy).then_inc(Q["unit_hi"], 1)

            @block.vector
            def _(dve):
                v = nc.vector

                def x_stats(tiles):
                    for t in tiles:
                        c = t // 4
                        if t % 4 == 0:
                            dve.wait_ge(x_in[c], 16)
                        v.bn_stats(xst[:, t, :], xr3[:, t, :]).then_inc(Q["xstat"], 1)
                        if t % 4 == 3:
                            for i in range(4 * c, t + 1):
                                dve.wait_ge(Q["xstat"], 4 * c + i + 1)
                                v.bn_aggr(xmv[:, i, :], xst[:, i, :]).then_inc(Q["xstat"], 1)
                            dve.wait_ge(Q["xstat"], 8 * c + 8)
                            v.tensor_scalar(xmv[:, 4 * c:t + 1, 1], xmv[:, 4 * c:t + 1, 1], EPS, None, ALU.add).then_inc(Q["xvar"], 1)
                            v.tensor_scalar(xnm[:, 4 * c:t + 1], xmv[:, 4 * c:t + 1, 0], -1.0, None, ALU.mult).then_inc(Q["xvar"], 1)

                def unit_low(q):
                    dve.wait_ge(Q["unit_hi"], number[q] + 1)
                    if q[0] == "g":
                        for k in range(KB):
                            last = low_g(4 + number[q] % 4, k)
                        last.then_inc(Q["unit_lo"], 1)
                        return
                    src, hi, lo = pieces(q)
                    v.tensor_tensor(lo, src, hi.bitcast(F32), ALU.subtract).then_inc(Q["unit_lo"], 1)

                dve.wait_ge(Q["ctx_ld"], 16)
                for a in range(4):
                    v.bn_stats(cst[:, a, :], ctx_n[:, a, :]).then_inc(Q["cstat"], 1)
                for a in range(4):
                    dve.wait_ge(Q["cstat"], 4 + a)
                    v.bn_aggr(cmv[:, a, :], cst[:, a, :]).then_inc(Q["cstat"], 1)
                dve.wait_ge(Q["cstat"], 8)
                v.tensor_scalar(cmv[:, :, 1], cmv[:, :, 1], EPS, None, ALU.add).then_inc(Q["cvar"], 1)
                x_stats(range(4))
                unit_low(("at", 0))
                unit_low(("at", 1))
                dve.wait_ge(Q["crstd"], 1)
                for a in range(4):
                    v.tensor_scalar(ctx_n[:, a, :], ctx_n[:, a, :], cmv[:, a, 0:1], crs[:, a:a + 1],
                                    ALU.subtract, ALU.mult).then_inc(Q["cz"], 1)
                dve.wait_ge(Q["bias_ld"], 32)
                for n, (w, bias, to) in enumerate(((wqr[:, 0, :], bkb, wqbk[:, 0:1]), (wqr[:, 1, :], bkb, wqbk[:, 1:2]),
                                                   (wkr[:, 0, :], bqb, cb[:, 0:1]), (wkr[:, 1, :], bqb, cb[:, 1:2]),
                                                   (bqb[:], bkb, qk[:]))):
                    v.tensor_tensor_reduce(prod[:, n, :], w, bias[:], 1.0, 0.0, ALU.mult, ALU.add, to).then_inc(Q["dots_done"], 1)
                dve.wait_ge(Q["dots_done"], 5)
                for q in items:
                    kind, t = q[0], q[1]
                    if kind == "at":
                        continue
                    if q == ("kv", 0):
                        dve.wait_ge(Q["wcol_hi"], 2)
                        for k in range(KB):
                            v.tensor_tensor(wvl[:, k, D:D + 2], wqbk[:, k:k + 1].broadcast_to([P, 2]), wvh[:, k, D:D + 2].bitcast(F32),
                                            ALU.subtract).then_inc(Q["wcol_lo"], 1)
                    if q == ("T", 1):
                        x_stats((4, 5))
                    if q == ("V", 0):
                        x_stats((6, 7))
                    if kind == "T" and 2 <= t < T - 6:
                        x_stats((t + 6,))
                    if kind == "T":
                        dve.wait_ge(Q["xt_hi"], t + 1)
                        b, o = t // TB, (t % TB) * P
                        hi, lo = (w[:].rearrange("p (b k n) -> p b k n", b=B, k=KB)[:, b, :, o:o + P] for w in (xhTh, xhTl))
                        v.tensor_tensor(lo, ps[:, t % 2, 0:D].rearrange("p (k n) -> p k n", k=KB), hi.bitcast(F32), ALU.subtract).then_inc(Q["xt_lo"], 1)
                    elif kind == "V":
                        dve.wait_ge(Q["v_hi"], t + 1)
                        c = slice(t * D, (t + 1) * D)
                        v.tensor_tensor(Vl[:, c], ps[:, 2 + t % 2, 0:D], Vh[:, c].bitcast(F32), ALU.subtract)
                        v.tensor_tensor(u[:, t:t + 1], ps[:, 2 + t % 2, D:D + 1], qk[:], ALU.add).then_inc(Q["v_lo"], 1)
                    else:
                        unit_low(q)

            @block.tensor
            def _(pe):
                def product(o, a, b, first=True, last=True):
                    nc.tensor.matmul(o, a[0], b[0], start=first, stop=False)
                    nc.tensor.matmul(o, a[0], b[1], start=False, stop=False)
                    return nc.tensor.matmul(o, a[1], b[0], start=False, stop=last)

                def unit(q):
                    i, kind = number[q], q[0]
                    if i >= 4:
                        pe.wait_ge(Q["unit_lo"], i - 3)
                    bank = ps[:, 4 + i % 4, :]
                    if kind == "at":
                        n = q[1]
                        pe.wait_ge(Q[("wq_ld", "wk_ld")[n]], 16)
                        for e in range(KB):
                            for k in range(KB):
                                last = nc.tensor.transpose(bank[:, e * D + k * P:e * D + (k + 1) * P],
                                                           (wqr, wkr)[n][:, k, e * P:(e + 1) * P], ident[:])
                    elif kind == "wq":
                        pe.wait_ge(Q["wqx_ld"], 16)
                        for j in range(2):
                            for k in range(KB):
                                e = 2 * q[1] + j
                                last = nc.tensor.transpose(bank[:, j * D + k * P:j * D + (k + 1) * P], wqx[:, k, e * P:(e + 1) * P], ident[:])
                    elif kind == "am":
                        k = q[1]
                        pe.wait_ge(Q["unit_lo"], 2)
                        for e in range(KB):
                            d = slice(k * P, (k + 1) * P)
                            last = product(bank[:, 0:D], (aqh[:, e, d], aql[:, e, d]), (akh[:, e, :], akl[:, e, :]), e == 0, e == KB - 1)
                    elif kind == "cn":
                        k = q[1]
                        pe.wait_ge(Q["cz"], 4)
                        for a in range(4):
                            last = nc.tensor.transpose(bank[:, a * CT:(a + 1) * CT], ctx_n[:, a, k * P:(k + 1) * P], ident[0:CT, 0:CT])
                    elif kind == "kv":
                        if q[1] == 0:
                            pe.wait_ge(Q["unit_lo"], number[("cn", KB - 1)] + 1)
                            pe.wait_ge(Q["split_done"], 2)
                        if q[1] == 4:
                            pe.wait_ge(Q["split_done"], 3)
                        w = slice(q[1] * P, (q[1] + 1) * P)
                        for k in range(KB):
                            last = product(bank[:, 0:B * M], (wkvh[:, k, w], wkvl[:, k, w]), (cnTh[:, k, :], cnTl[:, k, :]), k == 0, k == KB - 1)
                    elif kind == "kw":
                        _, k, h = q
                        pe.wait_ge(Q["unit_lo"], number[("kv", 3)] + 1)
                        r, d = slice(64 * (h % 2), 64 * (h % 2) + 64), slice(k * P, (k + 1) * P)
                        last = product(bank[:, 0:B * M], (wqTh[r, h // 2, d], wqTl[r, h // 2, d]), (kTh[r, h // 2, :], kTl[r, h // 2, :]))
                    elif kind == "vw":
                        _, b, j = q
                        pe.wait_ge(Q["unit_lo"], number[("kv", 7)] + 1)
                        pe.wait_ge(Q["split_done"], 4)
                        for n, h in enumerate(VWG[j]):
                            r = slice(64 * (h % 2), 64 * (h % 2) + 64)
                            m = slice(b * M, b * M + P)
                            last = product(bank[:, n * D:(n + 1) * D], (vTh[r, h // 2, m], vTl[r, h // 2, m]), (woh[r, h // 2, :], wol[r, h // 2, :]))
                    elif kind == "g":
                        last = project_xh(4 + i % 4, lambda d: slice(d * S, d * S + 2 * P))
                    else:
                        b = q[1]
                        pe.wait_ge(Q["rem_done"], 2 * HG)
                        for g in range(H // HG):
                            for j in (2 * g, 2 * g + 1):
                                last = product(bank[0:RK, g * D:(g + 1) * D], (vremh[:, b, j, :], vreml[:, b, j, :]), (woh[:, j, :], wol[:, j, :]),
                                               j % 2 == 0, j % 2 == 1)
                    last.then_inc(Q["unit_mm"], 1)

                pe.wait_ge(Q["ident_done"], 2)
                keep_warm(32, 3)
                for q in items:
                    t = q[1]
                    if q in WARM:
                        keep_warm(WARM[q], 3)
                    if q[0] == "T":
                        pe.wait_ge(Q["xh_done"], t + 1)
                        if t >= 2:
                            pe.wait_ge(Q["xt_lo"], t - 1)
                        for k in range(KB):
                            last = nc.tensor.transpose(ps[:, t % 2, k * P:(k + 1) * P], xh[:, t % 2, k * P:(k + 1) * P], ident[:])
                        last.then_inc(Q["xt_mm"], 1)
                    elif q[0] == "V":
                        pe.wait_ge(Q["xt_lo"], t + 1)
                        if t == 0:
                            pe.wait_ge(Q["split_done"], 1)
                            pe.wait_ge(Q["wcol_lo"], 2)
                        if t >= 2:
                            pe.wait_ge(Q["v_lo"], t - 1)
                        for k in range(KB):
                            o = ((t // TB) * KB + k) * S + (t % TB) * P
                            last = product(ps[:, 2 + t % 2, 0:D + 2], (xhTh[:, o:o + P], xhTl[:, o:o + P]), (wvh[:, k, :], wvl[:, k, :]), k == 0, k == KB - 1)
                        last.then_inc(Q["v_mm"], 1)
                    else:
                        unit(q)

        PSC = D ** -0.5
        P2SC = DH ** -0.5
        with ExitStack() as ph:
            (Pr, PTh, PTl, P2, P2r, P2Th, P2Tl, x1s, x2s, rec, zn, xnTh, xnTl, z3, z3T, g1b, b1b, boutb, wr, brb, desc, base, sm, racc, oh, idx), _ = lay(TEMP, [
                ("Pr", [P, S], F32),
                ("PTh", [P, S], F32R),
                ("PTl", [P, S], F32R),
                ("P2", [P, HM], F32),
                ("P2r", [P, H, REM], F32),
                ("P2Th", [P, NBLK * P], F32R),
                ("P2Tl", [P, NBLK * P], F32R),
                ("x1s", [P, D], F32),
                ("x2s", [P, D + 2], F32),
                ("rec", [P, REC], F32),
                ("zn", [P, D], F32),
                ("xnTh", [P, D], F32R),
                ("xnTl", [P, D], F32R),
                ("z3", [P, D], F32),
                ("z3T", [P, D], F32),
                ("g1b", [P, D], F32),
                ("b1b", [P, D], F32),
                ("boutb", [P, D], F32),
                ("wr", [P, KB, E], F32),
                ("brb", [P, E], F32),
                ("desc", [P, E], F32),
                ("base", [P, E], F32),
                ("sm", [P, 160], F32),
                ("racc", [P, E], BF16),
                ("oh", [P, E], BF16),
                ("idx", [P, 1], I32)])
            st1, mv1, r1, v1 = sm[:, 0:6], sm[:, 6:8], sm[:, 8:9], sm[:, 9:10]
            mx, sh, nb, ssum, rs = (sm[:, c:c + 1] for c in range(10, 15))
            mx2, nb2, ss2, rs2 = sm[:, 16:24], sm[:, 24:32], sm[:, 32:40], sm[:, 40:48]
            st3, r3s, v3 = sm[:, 48:54], [sm[:, c:c + 1] for c in (54, 112, 113, 114)], sm[:, 55:56]
            lg, e8, w8 = sm[:, 56:64], sm[:, 64:72], sm[:, 72:80]
            mx3, nmx3, se, wm, slot_at = (sm[:, c:c + 1] for c in range(80, 85))
            far, pb, q8 = sm[:, 88:96], sm[:, 96:104], sm[:, 104:112]

            names = ("par_ld const_c g_mm g_hi g_lo s_mm s_max s_sh s_nb p_done rs_done tp_mm tp_hi tp_lo pv_mm "
                     "x1_done st1_done mv1_done v1_done r1_done z_done zg_done zn_done xb_done zt_mm xn_hi xn_lo "
                     "sim_mm max2 nb2_done exp2 rs2_done p2_done t2_mm t2_hi t2_lo out_mm x2_done st3_done mv3_done "
                     "v3_done r3_done z3_done zt3_mm zt3_sb lg_mm lg_done mx3_done nmx3_done e8_done w8_done wm_done "
                     "oh_done gate_done rg_done cnt_mm far_done pb_done q1_done q2_done slot_done idx_done racc_done "
                     "x2_out scattered idx_read token_set rec_x").split()
            Q = {n: sem(ph, n) for n in names}

            holes = [KW_AT, KW_AT + 4 * B * KB * HM, VW_AT, VW_AT + 4 * B * NBLK * D,
                     XT_AT, XT_AT + 4 * B * KB * S, V_AT, V_AT + 4 * T * D]
            W = {}
            for half in range(2):
                for n in range(2):
                    for part in range(3):
                        hole = holes[4 * half + 2 * n + min(part, 1)]
                        name, dt = f"W{n + 1}{('hi', 'lo', 'raw')[part]}{half}", (F32R, F32R, F32)[part]
                        (W[n, part, half],), _ = lay(hole, [(name, [P, E // 2, KB * D], dt)])
            w_ld = {(n, half): sem(ph, f"w{n + 1}_ld{half}") for half in range(2) for n in range(2)}
            w_hi = sem(ph, "w_hi")
            w_pool = sem(ph, "w_pool")
            SPLIT = {T - 1: (5, 0), T: (2, 0), T + 1: (3, 2), T + 2: (2, 2)}
            order = [(e, n) for e in range(E) for n in range(2)]
            shares, done = {}, 0
            for s_, (n_pool, n_dve) in SPLIT.items():
                shares[s_] = (range(done, done + n_pool), range(done + n_pool, done + n_pool + n_dve))
                done += n_pool + n_dve
            assert done == len(order)

            (P2z, P2rz), _ = lay(XT_AT + 4 * KB * S, [("P2_last", [P, HM], F32), ("P2r_last", [P, H, REM], F32)])

            (P2Thz,), _ = lay(XT_AT + 4 * (B + 1) * KB * S, [("P2Th_last", [P, NBLK * P], F32R)])
            (P2Tlz,), _ = lay(V_AT + TB * ROW, [("P2Tl_last", [P, NBLK * P], F32R)])

            (rec_last, idx_last), _ = lay(holes[1] + 4 * (E // 2) * KB * D, [("rec_last", [P, REC], F32), ("idx_last", [P, 1], I32)])
            (rec_last1, idx_last1, b1rows), end = lay(holes[0] + 4 * (E // 2) * KB * D, [
                ("rec_last1", [P, REC], F32), ("idx_last1", [P, 1], I32), ("b1rows", [E * KB, P], F32)])
            assert end <= holes[1]
            (b2r,), _ = lay(XR_AT, [("b2r", [P, E * D], F32)])

            def rec_of(t):
                return {T - 2: rec_last1, T - 1: rec_last}.get(t, rec) if isinstance(t, int) else rec

            def idx_of(t):
                return {T - 2: idx_last1, T - 1: idx_last}.get(t, idx) if isinstance(t, int) else idx

            def p2_of(t):
                return (P2z, P2rz) if isinstance(t, int) and t == T - 1 else (P2, P2r)

            def p2t_of(t):
                return (P2Thz, P2Tlz) if isinstance(t, int) and t == T - 1 else (P2Th, P2Tl)

            def piece(i, part):
                e, n = order[i]
                return W[n, part, e // (E // 2)][:, e % (E // 2), :]

            block = ph.enter_context(nc.Block())
            BIG = ps[:].rearrange("p b n -> p (b n)")

            def bank(i):
                return ps[:, i, :]

            def out_bank(t):
                return bank(6 if isinstance(t, int) and t == T - 1 else 3)

            def z3_bank(t):
                return bank(5 if isinstance(t, int) and t == T - 1 else 4)

            def score_bank(t):
                return {1: 6, 2: 3}.get(t, 1) if isinstance(t, int) else 1

            def r3_of(t):
                return r3s[t - (T - 4) if isinstance(t, int) and t > T - 4 else 0]

            LOOP = (5, T - 1)

            def slots_of(eng, slot, first):
                for s in range(first, LOOP[0]):
                    slot(s, s % 2)
                with eng.Fori(*LOOP, 2) as s:
                    slot(s, 1)
                    slot(s + 1, 0)
                slot(LOOP[1], 1)

            def pairs(t):
                return t // 2 if isinstance(t, int) else t >> 1

            def live(t):
                return not isinstance(t, int) or 0 <= t < T

            @block.sync
            def _(sp):
                sp.dma_start(g1b[:], row(g1).broadcast_to([P, D])).then_inc(Q["par_ld"], 16)
                sp.dma_start(b1b[:], row(b1).broadcast_to([P, D])).then_inc(Q["par_ld"], 16)
                sp.dma_start(boutb[:], row(bout).broadcast_to([P, D])).then_inc(Q["par_ld"], 16)
                sp.dma_start(wr[:], Wr.rearrange("(k p) e -> p k e", p=P)).then_inc(Q["par_ld"], 16)
                sp.dma_start(brb[:], row(br).broadcast_to([P, E])).then_inc(Q["par_ld"], 16)
                def rows_out(t):
                    sp.wait_ge(Q["rec_x"], t + 1)
                    sp.dma_start(OUT[at(t * P, P), :], rec_of(t)[:, 0:D]).then_inc(Q["x2_out"], 16)

                with sp.Fori(0, TB) as t:
                    rows_out(t)
                for half in range(2):
                    for n, w in enumerate((W1, W2)):
                        sp.dma_start(W[n, 2, half][:].rearrange("p e (k f) -> p e k f", k=KB),
                                     w[half * (E // 2):(half + 1) * (E // 2)].rearrange("e (k p) f -> p e k f", p=P)).then_inc(w_ld[n, half], 16)
                sp.dma_start(b1rows[:], fb1.rearrange("e (k p) -> (e k) p", p=P)).then_inc(b1_ld, 16)
                sp.dma_start(b2r[:], fb2.rearrange("(a e) d -> a (e d)", a=1).broadcast_to([P, E * D])).then_inc(b2_ld, 16)
                with sp.Fori(TB, T - 2) as t:
                    rows_out(t)
                rows_out(T - 2)
                rows_out(T - 1)
                sp.wait_ge(Q["x2_out"], 16 * T)

            @block.tensor
            def _(pe):
                def mm(o, a, b, first=False, last=False):
                    return nc.tensor.matmul(o, a, b, start=first, stop=last)

                def product(o, a, b, first=True, last=True):
                    mm(o, a[0], b[0], first)
                    mm(o, a[0], b[1])
                    return mm(o, a[1], b[0], False, last)

                def project(t):
                    pe.wait_ge(Q["tp_lo"], 2 * (t - 1))
                    t_even = t if isinstance(t, int) else t.with_bounds(min_val=LOOP[0] + 1, max_val=T - 2)
                    project_xh(4, lambda d: at(batch_of(t) * ((KB - 1) * S) + d * S + t_even * P, 2 * P)).then_inc(Q["g_mm"], 1)

                def p_turn(t):
                    pe.wait_ge(Q["p_done"], t + 1)
                    if isinstance(t, int) and t + 1 >= T:
                        pe.wait_ge(Q["g_lo"], T // 2 - 1)
                    else:
                        if not isinstance(t, int) or t > 0:
                            pe.wait_ge(Q["g_lo"], pairs(t + 1))
                    if not isinstance(t, int) or t >= 3:
                        pe.wait_ge(Q["x2_done"], t - 2)
                    for n in range(TB):
                        last = nc.tensor.transpose(BIG[:, (3 * 4 + n) * P:(3 * 4 + n + 1) * P], Pr[:, n * P:(n + 1) * P], ident[:])
                        if n % 4 == 3:
                            last.then_inc(Q["tp_mm"], 1)

                def p2_turn(t):
                    if isinstance(t, int) and t == T - 1:
                        pe.wait_ge(Q["t2_lo"], 3 * (T - 1))
                    pe.wait_ge(Q["x1_done"], T if isinstance(t, int) and t + 2 > T else t + 2)
                    if not known_zero(t):
                        pe.wait_ge(Q["p_done"], T if isinstance(t, int) and t + 3 > T else t + 3)
                    for n in range(NBLK):
                        if n % 4 == 0:
                            pe.wait_ge(Q["p2_done"], 3 * t + n // 4 + 1)
                        if n < H:
                            src, rows = p2_of(t)[0][:, n * M:n * M + P], P
                        else:
                            h = (n - H) * HG
                            src = p2_of(t)[1][:, h:h + HG, :].rearrange("p h m -> p (h m)")
                            rows = RK
                        last = nc.tensor.transpose(BIG[0:rows, n * P:(n + 1) * P], src, ident[:])
                        if n % 4 == 3 or n == NBLK - 1:
                            last.then_inc(Q["t2_mm"], 1)

                def sim(t):
                    pe.wait_ge(Q["xn_lo"], t + 1)
                    b = batch_of(t)
                    for g in range(3):
                        if g == 2 and (not isinstance(t, int) or t >= 3):
                            pe.wait_ge(Q["q2_done"], t - 2)
                        n = (SIMG[g][1] - SIMG[g][0]) * M
                        if not known_zero(t):
                            pe.wait_ge(Q["exp2"], 3 * (t - 1) + g + 1)
                        for k in range(KB):
                            d = slice(k * P, (k + 1) * P)
                            o = at((b * KB + k) * HM + SIMG[g][0] * M, n)
                            last = product(bank(5 + g)[:, 0:n], (xnTh[:, d], xnTl[:, d]), (KWh[:, o], KWl[:, o]), k == 0, k == KB - 1)
                        last.then_inc(Q["sim_mm"], 1)

                def z3_turn(t):
                    pe.wait_ge(Q["z3_done"], t + 1)
                    pe.wait_ge(Q["tp_lo"], 2 * T if isinstance(t, int) and t + 4 > T else 2 * (t + 4))
                    for k in range(KB):
                        d = slice(k * P, (k + 1) * P)
                        last = nc.tensor.transpose(z3_bank(t)[:, d], z3[:, d], ident[:])
                    last.then_inc(Q["zt3_mm"], 1)

                def pv(t):
                    b = batch_of(t)
                    for n in range(TB):
                        if n % 4 == 0:
                            pe.wait_ge(Q["tp_lo"], 2 * t + n // 4 + 1)
                        if n == 0 and (not isinstance(t, int) or t >= 2):
                            pe.wait_ge(Q["t2_lo"], 3 * (t - 1) - 2)
                        c = slice(n * P, (n + 1) * P)
                        o = at((b * TB + n) * D, D)
                        last = product(bank(0)[:, 0:D], (PTh[:, c], PTl[:, c]), (Vh[:, o], Vl[:, o]), n == 0, n == TB - 1)
                    last.then_inc(Q["pv_mm"], 1)

                def logits(t):
                    if known_zero(t):
                        pe.wait_ge(Q["par_ld"], 80)
                    pe.wait_ge(Q["zt3_sb"], t + 1)
                    for k in range(KB):
                        last = mm(z3_bank(t)[:, 0:E], z3T[:, k * P:(k + 1) * P], wr[:, k, :], k == 0, k == KB - 1)
                    last.then_inc(Q["lg_mm"], 1)

                def scores(t, odd):
                    if not isinstance(t, int) or t > 1:
                        pe.wait_ge(Q["g_lo"], pairs(t))
                    if not isinstance(t, int) or t >= 3:
                        pe.wait_ge(Q["t2_lo"], 3 * (t - 2) if not isinstance(t, int) or t - 2 <= T else 3 * T)
                    b = batch_of(t)
                    c = slice(odd * P, (odd + 1) * P)
                    for h in range(2):
                        for k in range(KB):
                            o = at((b * KB + k) * S + h * 512, 512)
                            last = product(bank(score_bank(t) + h), (GTh[:, k, c], GTl[:, k, c]), (xhTh[:, o], xhTl[:, o]), k == 0, k == KB - 1)
                    last.then_inc(Q["s_mm"], 1)

                def count(t, sim_tile):
                    pe.wait_ge(Q["oh_done"], t + 1)
                    pe.wait_ge(Q["exp2"], 3 * T if isinstance(sim_tile, int) and sim_tile >= T else 3 * sim_tile + 3)
                    mm(bank(7)[:, 0:E], tri[:], oh[:], True, False)
                    mm(bank(7)[:, 0:E], ones[:], racc[:], False, True).then_inc(Q["cnt_mm"], 1)

                def outp(t, blocks):
                    b = batch_of(t)
                    o_bank = out_bank(t)
                    p2h, p2l = p2t_of(t)
                    for n in blocks:
                        if n == 0:
                            pe.wait_ge(Q["tp_lo"], 2 * T if isinstance(t, int) and t + 3 > T else 2 * (t + 3))
                        if n % 4 == 0:
                            pe.wait_ge(Q["t2_lo"], 3 * t + n // 4 + 1)
                        rows = P if n < H else RK
                        c = slice(n * P, (n + 1) * P)
                        o = at((b * NBLK + n) * D, D)
                        last = product(o_bank[:, 0:D], (p2h[0:rows, c], p2l[0:rows, c]), (VWh[0:rows, o], VWl[0:rows, o]),
                                       n == 0, n == NBLK - 1)
                    if NBLK - 1 in blocks:
                        last.then_inc(Q["out_mm"], 1)

                def z_turn(t):
                    pe.wait_ge(Q["zn_done"], t + 1)
                    if not known_zero(t):
                        pe.wait_ge(Q["exp2"], 3 * (t - 1) + 1)
                    for k in range(KB):
                        d = slice(k * P, (k + 1) * P)
                        last = nc.tensor.transpose(bank(5)[:, d], zn[:, d], ident[:])
                    last.then_inc(Q["zt_mm"], 1)

                def slot(s, odd):
                    if live(s - 3):
                        p2_turn(s - 3)
                    if live(s - 1):
                        p_turn(s - 1)
                    if live(s - 2):
                        sim(s - 2)
                    if live(s - 4):
                        z3_turn(s - 4)
                    if live(s - 1):
                        pv(s - 1)
                    if live(s - 4):
                        logits(s - 4)
                    scores(s, odd)
                    if live(s - 3):
                        outp(s - 3, range(OUT_SPLIT))
                    if live(s - 4):
                        count(s - 4, s - 2)
                    if live(s - 1):
                        z_turn(s - 1)
                    if odd and live(s + 1):
                        if live(s - 4):
                            pe.wait_ge(Q["lg_done"], s - 3)
                        project(s + 1)
                    if live(s - 3):
                        outp(s - 3, range(OUT_SPLIT, NBLK))

                scores(0, 0)
                scores(1, 1)
                p_turn(0)
                pv(0)
                project(2)
                keep_warm(24, 5)
                p_turn(1)
                keep_warm(12, 5)
                z_turn(0)
                pv(1)
                sim(0)
                scores(2, 0)
                z_turn(1)
                slots_of(pe, slot, 3)
                p2_turn(T - 3)
                p_turn(T - 1)
                sim(T - 2)
                z3_turn(T - 4)
                pv(T - 1)
                logits(T - 4)
                outp(T - 3, range(NBLK))
                z_turn(T - 1)
                count(T - 4, T - 2)
                keep_warm(16, 1)
                sim(T - 1)
                p2_turn(T - 2)
                z3_turn(T - 3)
                logits(T - 3)
                keep_warm(24, 3)
                outp(T - 2, range(4))
                p2_turn(T - 1)
                count(T - 3, T - 1)
                outp(T - 2, range(4, NBLK))
                outp(T - 1, range(NBLK))
                z3_turn(T - 2)
                logits(T - 2)
                z3_turn(T - 1)
                logits(T - 1)
                count(T - 2, T)
                count(T - 1, T)
                keep_warm(40, 0)

            @block.scalar
            def _(act):
                a = nc.scalar.activation

                def p_hi(t):
                    for h in range(2):
                        act.wait_ge(Q["tp_mm"], 2 * t + h + 1)
                        a(PTh[:, h * 512:(h + 1) * 512], bank(3 + h), ACT.Copy).then_inc(Q["tp_hi"], 1)

                def p2_hi(t):
                    for g in range(3):
                        act.wait_ge(Q["t2_mm"], 3 * t + g + 1)
                        rows, n = (P, 512) if g < 2 else (RK, 256)
                        a(p2t_of(t)[0][0:rows, g * 512:g * 512 + n], bank(g)[0:rows, 0:n], ACT.Copy).then_inc(Q["t2_hi"], 1)

                def exp2(t):
                    for g in range(3):
                        act.wait_ge(Q["nb2_done"], 3 * t + g + 1)
                        for n in range(*SIMG[g]):
                            o = (n - SIMG[g][0]) * M
                            last = a(p2_of(t)[0][:, n * M:(n + 1) * M], bank(5 + g)[:, o:o + M], ACT.Exp, bias=nb2[:, n:n + 1], scale=P2SC,
                                     accum_out=ss2[:, n:n + 1])
                        last.then_inc(Q["exp2"], 1)

                def record(t):
                    if not known_zero(t) and rec_of(t) is rec:
                        act.wait_ge(Q["scattered"], 16 * t)
                        act.wait_ge(Q["x2_out"], 16 * t)
                    act.wait_ge(Q["mv3_done"], t + 1)
                    a(rec_of(t)[:, 0:D + 1], x2s[:, 0:D + 1], ACT.Copy).then_inc(Q["rec_x"], 1)

                def gate(t):
                    act.wait_ge(Q["nmx3_done"], t + 1)
                    if not known_zero(t):
                        act.wait_ge(Q["gate_done"], t)
                    a(e8, lg, ACT.Exp, bias=nmx3, scale=1.0, accum_out=se).then_inc(Q["e8_done"], 1)

                def exps(t):
                    act.wait_ge(Q["s_nb"], t + 1)
                    if not known_zero(t):
                        act.wait_ge(Q["tp_mm"], 2 * t)
                        act.wait_ge(Q["rs_done"], t)
                    o = score_bank(t) * 512
                    a(Pr[:], BIG[:, o:o + S], ACT.Exp, bias=nb, scale=PSC, accum_out=ssum).then_inc(Q["p_done"], 1)

                def xn_hi(t):
                    act.wait_ge(Q["zt_mm"], t + 1)
                    a(xnTh[:], bank(5)[:, 0:D], ACT.Copy).then_inc(Q["xn_hi"], 1)

                def g_hi(t):
                    act.wait_ge(Q["g_mm"], pairs(t))
                    for k in range(KB):
                        last = high_g(4, k)
                    last.then_inc(Q["g_hi"], 1)

                def weights_hi(s):
                    for share in shares[s]:
                        for i in share:
                            e, n = order[i]
                            act.wait_ge(w_ld[n, e // (E // 2)], 16)
                            a(piece(i, 0), piece(i, 2), ACT.Copy).then_inc(w_hi, 1)

                def slot(s, odd):
                    if live(s - 3):
                        p2_hi(s - 3)
                    if live(s - 1):
                        p_hi(s - 1)
                    if live(s - 2):
                        exp2(s - 2)
                    if live(s - 4):
                        record(s - 4)
                        gate(s - 4)
                    exps(s)
                    if live(s - 1):
                        xn_hi(s - 1)
                    if odd and live(s + 1):
                        g_hi(s + 1)

                exps(0)
                p_hi(0)
                exps(1)
                g_hi(2)
                p_hi(1)
                xn_hi(0)
                exp2(0)
                exps(2)
                xn_hi(1)
                slots_of(act, slot, 3)
                p2_hi(T - 3)
                p_hi(T - 1)
                weights_hi(T - 1)
                exp2(T - 2)
                record(T - 4)
                gate(T - 4)
                xn_hi(T - 1)
                weights_hi(T)
                exp2(T - 1)
                p2_hi(T - 2)
                record(T - 3)
                gate(T - 3)
                weights_hi(T + 1)
                p2_hi(T - 1)
                weights_hi(T + 2)
                record(T - 2)
                gate(T - 2)
                record(T - 1)
                gate(T - 1)

            @block.gpsimd
            def _(pool):
                g = nc.gpsimd
                g.memset(racc[:], 0.0).then_inc(Q["const_c"], 1)
                g.iota(q8, pattern=[[1, E]], base=0, channel_multiplier=0, allow_small_or_imprecise_dtypes=True).then_inc(Q["const_c"], 1)
                pool.wait_ge(Q["const_c"], 2)
                g.tensor_scalar(desc[:], q8, -1.0, float(E), ALU.mult, ALU.add).then_inc(Q["const_c"], 1)
                g.tensor_scalar(base[:], q8, float(CAP), 0.0, ALU.mult, ALU.add).then_inc(Q["const_c"], 1)
                last_row = pool.to_reg(N - 1)
                pool.wait_ge(Q["par_ld"], 80)

                def affine(t):
                    pool.wait_ge(Q["v1_done"], t + 1)
                    g.tensor_tensor(r1, v1, mhalf[:, 0:1], ALU.pow).then_inc(Q["r1_done"], 1)
                    pool.wait_ge(Q["z_done"], t + 1)
                    g.tensor_tensor(zn[:], zn[:], g1b[:], ALU.mult).then_inc(Q["zg_done"], 1)
                    pool.wait_ge(Q["zg_done"], t + 1)
                    g.tensor_tensor(zn[:], zn[:], b1b[:], ALU.add).then_inc(Q["zn_done"], 1)

                def residual(t):
                    g.tensor_tensor(xr[:, at(t * D, D)], x1s[:], boutb[:], ALU.add).then_inc(Q["xb_done"], 1)

                def norm(t):
                    pool.wait_ge(Q["rs2_done"], t + 1)
                    p2, p2r = p2_of(t)
                    p3 = p2[:].rearrange("p (h m) -> p h m", h=H)
                    r3d = rs2.rearrange("p (h a) -> p h a", a=1)
                    for h in (slice(0, H // 2), slice(H // 2, H)):
                        g.tensor_tensor(p3[:, h, 0:P], p3[:, h, 0:P], r3d[:, h, :].broadcast_to([P, H // 2, P]), ALU.mult).then_inc(Q["p2_done"], 1)
                    g.tensor_tensor(p2r[:], p3[:, :, P:M], r3d.broadcast_to([P, H, REM]), ALU.mult).then_inc(Q["p2_done"], 1)

                def scatter(t):
                    pool.wait_ge(Q["idx_done"], t + 1)
                    pool.wait_ge(Q["token_set"], t + 1)
                    pool.nop(nofuse=True)
                    g.indirect_dma_start(out=slots[:, :], out_offset=bass.IndirectOffsetOnAxis(ap=idx_of(t)[:], axis=0),
                                         in_=rec_of(t)[:], in_offset=None, bounds_check=last_row,
                                         oob_is_err=False, engine_sem=Q["idx_read"]).then_inc(Q["scattered"], 16)

                def rstd3(t):
                    pool.wait_ge(Q["v3_done"], t + 1)
                    g.tensor_tensor(r3_of(t), v3, mhalf[:, 0:1], ALU.pow).then_inc(Q["r3_done"], 1)

                def weights_lo(s):
                    for i in shares[s][0]:
                        pool.wait_ge(w_hi, i + 1)
                        g.tensor_tensor(piece(i, 1), piece(i, 2), piece(i, 0).bitcast(F32), ALU.subtract).then_inc(w_pool, 1)

                def slot(s, odd):
                    if live(s - 1):
                        affine(s - 1)
                    if live(s - 2):
                        norm(s - 2)
                    if live(s - 1):
                        residual(s - 1)
                    if live(s - 4):
                        scatter(s - 4)
                    if live(s - 3):
                        rstd3(s - 3)

                slots_of(pool, slot, 1)
                weights_lo(T - 1)
                affine(T - 1)
                norm(T - 2)
                residual(T - 1)
                rstd3(T - 3)
                scatter(T - 4)
                weights_lo(T)
                norm(T - 1)
                weights_lo(T + 1)
                scatter(T - 3)
                rstd3(T - 2)
                rstd3(T - 1)
                weights_lo(T + 2)
                scatter(T - 2)
                scatter(T - 1)
                pool.wait_ge(Q["scattered"], 16 * T)

            @block.vector
            def _(dve):
                v = nc.vector

                def p_lo(t):
                    for h in range(2):
                        dve.wait_ge(Q["tp_hi"], 2 * t + h + 1)
                        c = slice(h * 512, (h + 1) * 512)
                        v.tensor_tensor(PTl[:, c], bank(3 + h), PTh[:, c].bitcast(F32), ALU.subtract).then_inc(Q["tp_lo"], 1)
                    v.reciprocal(rs, ssum).then_inc(Q["rs_done"], 1)

                def x2_p2lo(t, p):
                    def p2_lo(g):
                        if live(p):
                            dve.wait_ge(Q["t2_hi"], 3 * p + g + 1)
                            rows, n = (P, 512) if g < 2 else (RK, 256)
                            c = slice(g * 512, g * 512 + n)
                            p2h, p2l = p2t_of(p)
                            v.tensor_tensor(p2l[0:rows, c], bank(g)[0:rows, 0:n], p2h[0:rows, c].bitcast(F32), ALU.subtract).then_inc(Q["t2_lo"], 1)

                    if live(t):
                        dve.wait_ge(Q["out_mm"], t + 1)
                        dve.wait_ge(Q["xb_done"], t + 1)
                        if not known_zero(t):
                            dve.wait_ge(Q["rec_x"], t)
                            dve.wait_ge(Q["z3_done"], t)
                        v.tensor_tensor(x2s[:, 0:D], out_bank(t)[:, 0:D], xr[:, at(t * D, D)], ALU.add).then_inc(Q["x2_done"], 1)
                        dve.wait_ge(Q["x2_done"], t + 1)
                        dve.nop(nofuse=True)
                        v.bn_stats(st3, x2s[:, 0:D]).then_inc(Q["st3_done"], 1)
                    p2_lo(0)
                    if live(t):
                        dve.wait_ge(Q["st3_done"], t + 1)
                        dve.nop(nofuse=True)
                        v.bn_aggr(x2s[:, D:D + 2], st3).then_inc(Q["mv3_done"], 1)
                    p2_lo(1)
                    if live(t):
                        dve.wait_ge(Q["mv3_done"], t + 1)
                        v.tensor_scalar(v3, x2s[:, D + 1:D + 2], EPS, None, ALU.add).then_inc(Q["v3_done"], 1)
                    p2_lo(2)

                def max2(t):
                    for g in range(3):
                        dve.wait_ge(Q["sim_mm"], 3 * t + g + 1)
                        h0, h1 = SIMG[g]
                        v.tensor_reduce(mx2[:, h0:h1], bank(5 + g)[:, 0:(h1 - h0) * M].rearrange("p (h m) -> p h m", m=M), AX,
                                        ALU.max).then_inc(Q["max2"], 1)
                        dve.wait_ge(Q["max2"], 3 * t + g + 1)
                        v.tensor_scalar(nb2[:, h0:h1], mx2[:, h0:h1], -P2SC, None, ALU.mult).then_inc(Q["nb2_done"], 1)

                def z3t_copy(t):
                    dve.wait_ge(Q["zt3_mm"], t + 1)
                    v.tensor_copy(z3T[:], z3_bank(t)[:, 0:D]).then_inc(Q["zt3_sb"], 1)

                def x1_route1(t, r):
                    if live(t):
                        dve.wait_ge(Q["pv_mm"], t + 1)
                        dve.wait_ge(Q["rs_done"], t + 1)
                        if not known_zero(t):
                            dve.wait_ge(Q["xb_done"], t)
                        v.scalar_tensor_tensor(out=x1s[:], in0=bank(0)[:, 0:D], scalar=rs, in1=xr[:, at(t * D, D)], op0=ALU.mult,
                                               op1=ALU.add).then_inc(Q["x1_done"], 1)
                    if live(r):
                        if known_zero(r):
                            dve.wait_ge(Q["par_ld"], 80)
                            dve.wait_ge(Q["const_c"], 4)
                        dve.wait_ge(Q["lg_mm"], r + 1)
                        v.tensor_tensor(lg, z3_bank(r)[:, 0:E], brb[:], ALU.add).then_inc(Q["lg_done"], 1)
                    if live(t):
                        dve.wait_ge(Q["x1_done"], t + 1)
                        dve.nop(nofuse=True)
                        v.bn_stats(st1, x1s[:]).then_inc(Q["st1_done"], 1)
                    if live(r):
                        dve.wait_ge(Q["lg_done"], r + 1)
                        v.tensor_reduce(mx3, lg, AX, ALU.max).then_inc(Q["mx3_done"], 1)
                    if live(t):
                        dve.wait_ge(Q["st1_done"], t + 1)
                        dve.nop(nofuse=True)
                        v.bn_aggr(mv1, st1).then_inc(Q["mv1_done"], 1)
                    if live(r):
                        dve.wait_ge(Q["mx3_done"], r + 1)
                        v.tensor_scalar(nmx3, mx3, -1.0, None, ALU.mult).then_inc(Q["nmx3_done"], 1)
                    if live(t):
                        dve.wait_ge(Q["mv1_done"], t + 1)
                        v.tensor_scalar(v1, mv1[:, 1:2], 1.0 + EPS, EPS * EPS, ALU.mult, ALU.add).then_inc(Q["v1_done"], 1)

                def zee(t):
                    dve.wait_ge(Q["r1_done"], t + 1)
                    if not known_zero(t):
                        dve.wait_ge(Q["zt_mm"], t)
                    v.tensor_scalar(zn[:], x1s[:], mv1[:, 0:1], r1, ALU.subtract, ALU.mult).then_inc(Q["z_done"], 1)

                def recip2(t):
                    dve.wait_ge(Q["exp2"], 3 * t + 3)
                    v.reciprocal(rs2, ss2).then_inc(Q["rs2_done"], 1)

                def route2(t):
                    dve.wait_ge(Q["e8_done"], t + 1)
                    v.scalar_tensor_tensor(out=w8, in0=e8, scalar=1.0, in1=desc[:], op0=ALU.is_ge, op1=ALU.mult).then_inc(Q["w8_done"], 1)
                    dve.wait_ge(Q["rec_x"], t + 1)
                    v.tensor_copy(rec_of(t)[:, REC - 1:REC].bitcast(I32), tokens[:, at(t, 1)]).then_inc(Q["token_set"], 1)
                    gt = rec_of(t)[:, D + 2:D + 3]
                    v.reciprocal(gt, se).then_inc(Q["gate_done"], 1)
                    dve.wait_ge(Q["w8_done"], t + 1)
                    v.tensor_reduce(wm, w8, AX, ALU.max).then_inc(Q["wm_done"], 1)
                    dve.wait_ge(Q["wm_done"], t + 1)
                    v.tensor_scalar(oh[:], w8, wm, None, ALU.is_equal).then_inc(Q["oh_done"], 1)
                    dve.wait_ge(Q["gate_done"], t + 1)
                    v.tensor_tensor(rec_of(t)[:, D + 1:D + 2], r3_of(t), gt, ALU.mult).then_inc(Q["rg_done"], 1)

                def smax(t):
                    dve.wait_ge(Q["s_mm"], t + 1)
                    o = score_bank(t) * 512
                    v.tensor_reduce(mx, BIG[:, o:o + S], AX, ALU.max).then_inc(Q["s_max"], 1)
                    dve.wait_ge(Q["s_max"], t + 1)
                    ut = u[:, at(t, 1)]
                    v.tensor_tensor(sh, mx, ut, ALU.add).then_inc(Q["s_sh"], 1)
                    dve.wait_ge(Q["s_sh"], t + 1)
                    v.tensor_scalar(nb, sh, ut, -PSC, ALU.subtract, ALU.mult).then_inc(Q["s_nb"], 1)

                def place(t):
                    dve.wait_ge(Q["cnt_mm"], t + 1)
                    cnt = bank(7)[:, 0:E]
                    v.tensor_scalar(far, cnt, float(CAP), FAR, ALU.is_ge, ALU.mult).then_inc(Q["far_done"], 1)
                    v.tensor_tensor(pb, cnt, base[:], ALU.add).then_inc(Q["pb_done"], 1)
                    v.tensor_tensor(racc[:], racc[:], oh[:], ALU.add).then_inc(Q["racc_done"], 1)
                    dve.wait_ge(Q["far_done"], t + 1)
                    dve.wait_ge(Q["pb_done"], t + 1)
                    v.tensor_tensor(far, far, pb, ALU.add).then_inc(Q["q1_done"], 1)
                    dve.wait_ge(Q["q1_done"], t + 1)
                    v.tensor_tensor(far, far, oh[:], ALU.mult).then_inc(Q["q2_done"], 1)
                    dve.wait_ge(Q["q2_done"], t + 1)
                    v.tensor_reduce(slot_at, far, AX, ALU.add).then_inc(Q["slot_done"], 1)
                    dve.wait_ge(Q["slot_done"], t + 1)
                    dve.wait_ge(Q["rg_done"], t + 1)
                    dve.wait_ge(Q["racc_done"], t + 1)
                    if not known_zero(t):
                        dve.wait_ge(Q["idx_read"], t)
                    v.tensor_copy(idx_of(t)[:], slot_at).then_inc(Q["idx_done"], 1)

                def xn_lo(t):
                    dve.wait_ge(Q["xn_hi"], t + 1)
                    v.tensor_tensor(xnTl[:], bank(5)[:, 0:D], xnTh[:].bitcast(F32), ALU.subtract).then_inc(Q["xn_lo"], 1)

                def g_lo(t):
                    dve.wait_ge(Q["g_hi"], pairs(t))
                    for k in range(KB):
                        last = low_g(4, k)
                    last.then_inc(Q["g_lo"], 1)

                def zee3(t):
                    dve.wait_ge(Q["r3_done"], t + 1)
                    v.tensor_scalar(z3[:], x2s[:, 0:D], x2s[:, D:D + 1], r3_of(t), ALU.subtract, ALU.mult).then_inc(Q["z3_done"], 1)

                def weights_lo(s, part=slice(None)):
                    for i in shares[s][1][part]:
                        dve.wait_ge(w_hi, i + 1)
                        v.tensor_tensor(piece(i, 1), piece(i, 2), piece(i, 0).bitcast(F32), ALU.subtract)

                def head(s):
                    x2_p2lo(s - 4, s - 3)
                    if live(s - 4):
                        zee3(s - 4)
                    p_lo(s - 1)
                    max2(s - 2)
                    if live(s - 4):
                        z3t_copy(s - 4)

                def rest(s, odd):
                    x1_route1(s - 1, s - 4)
                    recip2(s - 2)
                    zee(s - 1)
                    if live(s - 4):
                        route2(s - 4)
                    smax(s)
                    if live(s - 4):
                        place(s - 4)
                    xn_lo(s - 1)
                    if odd and live(s + 1):
                        g_lo(s + 1)

                smax(0)
                p_lo(0)
                smax(1)
                x1_route1(0, T)
                g_lo(2)
                zee(0)
                p_lo(1)
                xn_lo(0)
                x1_route1(1, T)
                max2(0)
                zee(1)
                recip2(0)
                smax(2)
                xn_lo(1)
                head(3)
                rest(3, 1)
                head(4)
                rest(4, 0)
                head(5)
                with dve.Fori(*LOOP, 2) as s:
                    rest(s, 1)
                    head(s + 1)
                    rest(s + 1, 0)
                    head(s + 2)
                rest(T - 1, 1)
                x2_p2lo(T - 4, T - 3)
                zee3(T - 4)
                p_lo(T - 1)
                max2(T - 2)
                z3t_copy(T - 4)
                x1_route1(T - 1, T - 4)
                recip2(T - 2)
                zee(T - 1)
                route2(T - 4)
                x2_p2lo(T - 3, T)
                xn_lo(T - 1)
                place(T - 4)
                zee3(T - 3)
                weights_lo(T)
                max2(T - 1)
                z3t_copy(T - 3)
                recip2(T - 1)
                x1_route1(T, T - 3)
                x2_p2lo(T, T - 2)
                route2(T - 3)
                weights_lo(T + 1)
                x2_p2lo(T, T - 1)
                place(T - 3)
                x2_p2lo(T - 2, T)
                weights_lo(T + 2, slice(0, 1))
                zee3(T - 2)
                x2_p2lo(T - 1, T)
                z3t_copy(T - 2)
                zee3(T - 1)
                x1_route1(T, T - 2)
                z3t_copy(T - 1)
                route2(T - 2)
                weights_lo(T + 2, slice(1, 2))
                x1_route1(T, T - 1)
                place(T - 2)
                route2(T - 1)
                place(T - 1)

        with ExitStack() as ph:
            things = [("nm", [P, E, 2], F32), ("b1c", [P, E * KB], F32)]
            for j in range(2):
                things += [(f"xg{j}", [P, 2, D], F32), (f"dTh{j}", [P, KB, CAP], F32R), (f"dTl{j}", [P, KB, CAP], F32R),
                           (f"hf{j}", [P, KB, CAP], F32), (f"hTh{j}", [P, KB, CAP], F32R), (f"hTl{j}", [P, KB, CAP], F32R),
                           (f"res{j}", [P, 2, D], F32)]
            (nm, b1c, *by_parity), _ = lay(TEMP, things)
            xg, dTh, dTl, hf, hTh, hTl, res = zip(by_parity[:7], by_parity[7:])
            rec = []
            for half in range(2):
                made, _ = lay(VW_AT + 4 * D * NBLK * (2 * half + 1), [(f"rec{e}", [P, 2, REC], F32) for e in range(4 * half, 4 * half + 4)])
                rec += made
            rec_ld = [sem(ph, f"rec_ld{e}") for e in range(E)]
            token_out = [sem(ph, f"token_out{j}") for j in range(2)]
            names = "b1_mm b1_done nm_done xg0_done xg_done xt_mm dt_hi dt_lo h_mm hf_done ht_hi ht_lo o_mm t_done res_done".split()
            R = {n: sem(ph, "e_" + n) for n in names}
            block = ph.enter_context(nc.Block())

            def steps(slot):
                for s in range(E + 1):
                    slot(s)

            def here(e):
                return 0 <= e < E

            def w_of(n, e):
                return [W[n, part, e // (E // 2)][:, e % (E // 2), :] for part in range(2)]

            @block.sync
            def _(sp):
                for e in range(0, E, 2):
                    sp.dma_start(rec[e][:], slots[e * CAP:(e + 1) * CAP, :].rearrange("(i p) c -> p i c", p=P)).then_inc(rec_ld[e], 16)

            @block.tensor
            def _(pe):
                def product(o, a, b, first, last):
                    nc.tensor.matmul(o, a[0], b[0], start=first, stop=False)
                    nc.tensor.matmul(o, a[0], b[1], start=False, stop=False)
                    return nc.tensor.matmul(o, a[1], b[0], start=False, stop=last)

                pe.wait_ge(b1_ld, 16)
                nc.tensor.transpose(ps[:, 6, 0:E * KB], b1rows[:], ident[0:E * KB, 0:E * KB]).then_inc(R["b1_mm"], 1)

                def first(e):
                    j = e % 2
                    wh, wl = w_of(0, e)
                    pe.wait_ge(R["dt_lo"], e + 1)
                    if e >= 2:
                        pe.wait_ge(R["hf_done"], e - 1)
                    for f in range(KB):
                        for k in range(KB):
                            c = slice(k * D + f * P, k * D + (f + 1) * P)
                            last = product(ps[:, 2 + j, f * CAP:(f + 1) * CAP], (wh[:, c], wl[:, c]),
                                           (dTh[j][:, k, :], dTl[j][:, k, :]), k == 0, k == KB - 1)
                    last.then_inc(R["h_mm"], 1)

                def turn(e):
                    j = e % 2
                    if e == 0:
                        pe.wait_ge(R["xg0_done"], 2)
                    else:
                        pe.wait_ge(R["xg_done"], 2 * e)
                    if e >= 2:
                        pe.wait_ge(R["dt_lo"], e - 1)
                    for k in range(KB):
                        for i in range(2):
                            o = k * CAP + i * P
                            last = nc.tensor.transpose(ps[:, j, o:o + P], xg[j][:, i, k * P:(k + 1) * P], ident[:])
                    last.then_inc(R["xt_mm"], 1)

                def second(e):
                    j = e % 2
                    wh, wl = w_of(1, e)
                    pe.wait_ge(R["ht_lo"], e + 1)
                    if e >= 2:
                        pe.wait_ge(R["t_done"], 2 * e - 2)
                    for i in range(2):
                        for f in range(KB):
                            c, w = slice(i * P, (i + 1) * P), slice(f * D, (f + 1) * D)
                            last = product(ps[:, 4 + 2 * i + j, 0:D], (hTh[j][:, f, c], hTl[j][:, f, c]), (wh[:, w], wl[:, w]),
                                           f == 0, f == KB - 1)
                        last.then_inc(R["o_mm"], 1)

                def slot(s):
                    if here(s):
                        first(s)
                    if here(s + 2):
                        turn(s + 2)
                    if here(s - 1):
                        second(s - 1)

                keep_warm(72, 0)
                turn(0)
                turn(1)
                steps(slot)

            @block.scalar
            def _(act):
                a = nc.scalar.activation
                for e in range(1, E, 2):
                    act.dma_start(rec[e][:], slots[e * CAP:(e + 1) * CAP, :].rearrange("(i p) c -> p i c", p=P)).then_inc(rec_ld[e], 16)

                def gated(e):
                    act.wait_ge(R["nm_done"], e + 1)
                    if e >= 2:
                        act.wait_ge(R["xt_mm"], e - 1)
                    for i in range(2):
                        a(xg[e % 2][:, i, :], rec[e][:, i, 0:D], ACT.Identity, bias=nm[:, e, i:i + 1],
                          scale=rec[e][:, i, D + 1:D + 2]).then_inc(R["xg_done"], 1)

                def turned(e):
                    act.wait_ge(R["xt_mm"], e + 1)
                    a(dTh[e % 2][:], ps[:, e % 2, :].rearrange("p (k c) -> p k c", k=KB), ACT.Copy).then_inc(R["dt_hi"], 1)

                def slot(s):
                    j = s % 2
                    if here(s):
                        act.wait_ge(R["h_mm"], s + 1)
                        for f in range(KB):
                            last = a(hf[j][:, f, :], ps[:, 2 + j, f * CAP:(f + 1) * CAP], ACT.Relu,
                                     bias=b1c[:, s * KB + f:s * KB + f + 1], scale=1.0)
                        last.then_inc(R["hf_done"], 1)
                        act.wait_ge(R["hf_done"], s + 1)
                        a(hTh[j][:], hf[j][:], ACT.Copy).then_inc(R["ht_hi"], 1)
                    if here(s + 2):
                        turned(s + 2)
                    if here(s + 4):
                        gated(s + 4)

                gated(1)
                act.wait_ge(R["b1_mm"], 1)
                a(b1c[:], ps[:, 6, 0:E * KB], ACT.Copy).then_inc(R["b1_done"], 1)
                turned(0)
                gated(2)
                turned(1)
                gated(3)
                act.wait_ge(R["b1_done"], 1)
                steps(slot)

            @block.vector
            def _(dve):
                v = nc.vector

                def shift(e):
                    dve.wait_ge(rec_ld[e], 16)
                    v.scalar_tensor_tensor(out=nm[:, e, :], in0=rec[e][:, :, D], scalar=-1.0, in1=rec[e][:, :, D + 1],
                                           op0=ALU.mult, op1=ALU.mult).then_inc(R["nm_done"], 1)

                def turned(e):
                    j = e % 2
                    dve.wait_ge(R["dt_hi"], e + 1)
                    v.tensor_tensor(dTl[j][:], ps[:, j, :].rearrange("p (k c) -> p k c", k=KB), dTh[j][:].bitcast(F32),
                                    ALU.subtract).then_inc(R["dt_lo"], 1)

                def slot(s):
                    if here(s):
                        j = s % 2
                        dve.wait_ge(R["ht_hi"], s + 1)
                        v.tensor_tensor(hTl[j][:], hf[j][:], hTh[j][:].bitcast(F32), ALU.subtract).then_inc(R["ht_lo"], 1)
                    if here(s + 2):
                        turned(s + 2)
                    if here(s - 1):
                        e, j = s - 1, (s - 1) % 2
                        if e == 0:
                            dve.wait_ge(b2_ld, 16)
                        if e >= 2:
                            dve.wait_ge(token_out[j], 32 * (e // 2))
                        for i in range(2):
                            r = rec[e][:, i, :]
                            dve.wait_ge(R["o_mm"], 2 * e + i + 1)
                            v.tensor_tensor(res[j][:, i, :], ps[:, 4 + 2 * i + j, 0:D], b2r[:, e * D:(e + 1) * D], ALU.add).then_inc(R["t_done"], 1)
                            dve.wait_ge(R["t_done"], 2 * e + i + 1)
                            v.scalar_tensor_tensor(out=res[j][:, i, :], in0=res[j][:, i, :], scalar=r[:, D + 2:D + 3], in1=r[:, 0:D],
                                                   op0=ALU.mult, op1=ALU.add).then_inc(R["res_done"], 1)

                for e in range(E):
                    shift(e)
                    if e == 0:
                        dve.wait_ge(R["nm_done"], 1)
                        for i in range(2):
                            v.tensor_scalar(xg[0][:, i, :], rec[0][:, i, 0:D], rec[0][:, i, D + 1:D + 2], nm[:, 0, i:i + 1],
                                            ALU.mult, ALU.add).then_inc(R["xg0_done"], 1)
                    if e in (3, 5):
                        turned((e - 3) // 2)
                steps(slot)

            @block.gpsimd
            def _(pool):
                g = nc.gpsimd
                last_row = pool.to_reg(N - 1)

                for e in range(E):
                    for i in range(2):
                        pool.wait_ge(R["res_done"], 2 * e + i + 1)
                        tok = rec[e][:].bitcast(I32)[:, i, REC - 1:REC]
                        g.indirect_dma_start(out=OUT, out_offset=bass.IndirectOffsetOnAxis(ap=tok, axis=0),
                                             in_=res[e % 2][:, i, :], in_offset=None, bounds_check=last_row,
                                             oob_is_err=False).then_inc(token_out[e % 2], 16)
                for j in range(2):
                    pool.wait_ge(token_out[j], 16 * E)


_INS = ["x", "ctx_1024", "L0_attn_Wq", "L0_attn_bq", "L0_attn_Wk", "L0_attn_bk", "L0_attn_Wv", "L0_attn_bv", "L0_xattn_g1",
        "L0_xattn_b1", "L0_xattn_g2", "L0_xattn_b2", "L0_xattn_Wq", "L0_xattn_Wkv", "L0_xattn_Wout", "L0_xattn_bout",
        "L0_ffn_Wr", "L0_ffn_br", "L0_ffn_W1", "L0_ffn_b1", "L0_ffn_W2", "L0_ffn_b2"]


def kernel(**inputs):
    import numpy as np
    import concourse.bacc as bacc
    from concourse.bass_utils import run_bass_kernel_spmd as run

    nc = bacc.Bacc("TRN2", target_bir_lowering=False, num_devices=1)
    arrays, args = {}, []
    for name in _INS:
        a = np.ascontiguousarray(inputs[name])
        arrays[f"in_{name}"] = a
        args.append(nc.dram_tensor(f"in_{name}", a.shape, mybir.dt.from_np(a.dtype), kind="ExternalInput").ap())
    args.append(nc.dram_tensor("out_rows", (B, S, D), F32, kind="ExternalOutput").ap())
    build(nc, *args)
    r = run(nc, [arrays], core_ids=[0])
    return r.results[0]["out_rows"]
```
